# Optimizing a Trainium2 kernel written in Bass

```python
import numpy as np
import jax
import jax.numpy as jnp

def _softmax(x, axis=-1):
    return jax.nn.softmax(x, axis=axis)

def _gelu(x):
    return jax.nn.gelu(x, approximate=True)

def _silu(x):
    return jax.nn.silu(x)

def _sigmoid(x):
    return jax.nn.sigmoid(x)

def _layernorm(x, axis=-1, eps=1e-05):
    m = jnp.mean(x, axis=axis, keepdims=True)
    v = jnp.var(x, axis=axis, keepdims=True)
    return (x - m) / jnp.sqrt(v + eps)

def _scatter_add(tgt, idx, src, axis=0):
    return tgt.at[idx].add(src)

def _segment_sum(src, seg, n):
    return jax.ops.segment_sum(src, seg, n)
kernel_name = 'mk_flamingo_gated_d1_seqx_r8_56dcc6'

def setup_inputs(seed: int=0):
    np.random.seed(seed)
    _w = jnp.asarray

    def _rec_inputs():
        import jax
        import jax.numpy as jnp
        _rk = jax.random.key(seed)
        x = 0.0002417 + 0.9998 * jax.random.normal(jax.random.fold_in(_rk, 1), (4, 512, 128), jnp.float32)
        _lenS = 512 - jax.random.randint(jax.random.fold_in(_rk, 7), (4,), 0, max(1, 512 // 4) + 1, jnp.int32)
        _lenS2 = 154 - jax.random.randint(jax.random.fold_in(_rk, 8), (4,), 0, max(1, 154 // 4) + 1, jnp.int32)
        _ctx_1024P = jax.random.normal(jax.random.fold_in(_rk, 11), (4, 16, 128), jnp.float32)
        _ctx_1024c = jax.random.dirichlet(jax.random.fold_in(_rk, 511), 0.3 * jnp.ones((16,), jnp.float32), (4, 154))
        _ctx_1024t = jnp.einsum('bsk,bkd->bsd', _ctx_1024c, _ctx_1024P)
        _ctx_1024t = _ctx_1024t * jax.lax.rsqrt(jnp.mean(jnp.square(_ctx_1024t)) + 1e-12) * 0.953939
        ctx_1024 = 7.22013e-05 + 1.00017 * (_ctx_1024t + 0.3 * jax.random.normal(jax.random.fold_in(_rk, 611), (4, 154, 128), jnp.float32))
        _g = jax.random.normal(jax.random.fold_in(_rk, 9001), (2, 1), jnp.float32)
        _g = jnp.sign(_g) * jnp.maximum(jnp.abs(_g), 1.0) + (_g == 0) * 1.0
        g_xattn = _g[0]
        g_ffn = _g[1]
        return (x, ctx_1024, g_xattn, g_ffn)
    x, ctx_1024, g_xattn, g_ffn = _rec_inputs()

    def _L0_xattn_setup():
        import jax, jax.numpy as jnp
        import numpy as np
        EMBED = 128
        HEADS = 16
        HEAD_DIM = EMBED // HEADS
        EXP_DIM = 2 * HEAD_DIM

        def _feature_map(x, fm_w, fm_b):
            z = jnp.einsum('nshd,ed->nshe', x, fm_w) + fm_b
            return jnp.concatenate([jnp.exp(z), jnp.exp(-z)], axis=-1)
        key = jax.random.key(seed)
        ks = jax.random.split(key, 7)
        N, S = (4, 256)
        values = jax.random.normal(ks[0], (N, S, EMBED), dtype=jnp.float32)
        keys_ = jax.random.normal(ks[1], (N, S, EMBED), dtype=jnp.float32)
        query = jax.random.normal(ks[2], (N, S, EMBED), dtype=jnp.float32)
        fm_w = jnp.eye(HEAD_DIM, dtype=jnp.float32) + 0.02 * jax.random.normal(ks[3], (HEAD_DIM, HEAD_DIM), dtype=jnp.float32)
        fm_b = 0.02 * jax.random.normal(ks[4], (HEAD_DIM,), dtype=jnp.float32)
        fc_w = jax.random.normal(ks[5], (EMBED, HEADS * EXP_DIM), dtype=jnp.float32) * (1.0 / np.sqrt(HEADS * EXP_DIM))
        fc_b = jnp.zeros((EMBED,), dtype=jnp.float32)
        return {'values': values, 'keys': keys_, 'query': query, 'fm_w': fm_w, 'fm_b': fm_b, 'fc_w': fc_w, 'fc_b': fc_b}
    _L0_xattn_all = _L0_xattn_setup()
    _L0_xattn_in = {k: v for k, v in _L0_xattn_all.items() if k in ('fm_w', 'fm_b', 'fc_w', 'fc_b')}
    del _L0_xattn_all

    def _L0_ffn_setup():
        import jax, jax.numpy as jnp
        import numpy as np
        B, T, D = (2, 128, 128)
        E = 16
        H = 256
        K = 2
        HS = H * 2
        key = jax.random.key(seed)
        ks = jax.random.split(key, 16)
        s = 0.02
        f32 = jnp.float32
        return {'x': jax.random.normal(ks[0], (B, T, D), f32), 'Wg': jax.random.normal(ks[1], (D, E), f32) * s, 'W1': jax.random.normal(ks[2], (E, D, H), f32) * s, 'b1': jax.random.normal(ks[3], (E, H), f32) * s, 'W11': jax.random.normal(ks[4], (E, D, H), f32) * s, 'b11': jax.random.normal(ks[5], (E, H), f32) * s, 'W2': jax.random.normal(ks[6], (E, H, D), f32) * s, 'b2': jax.random.normal(ks[7], (E, D), f32) * s, 'Ws1': jax.random.normal(ks[8], (D, HS), f32) * s, 'bs1': jax.random.normal(ks[9], (HS,), f32) * s, 'Ws11': jax.random.normal(ks[10], (D, HS), f32) * s, 'bs11': jax.random.normal(ks[11], (HS,), f32) * s, 'Ws2': jax.random.normal(ks[12], (HS, D), f32) * s, 'bs2': jax.random.normal(ks[13], (D,), f32) * s}
    _L0_ffn_all = _L0_ffn_setup()
    _L0_ffn_in = {k: v for k, v in _L0_ffn_all.items() if k in ('Wg', 'W1', 'b1', 'W11', 'b11', 'W2', 'b2', 'Ws1', 'bs1', 'Ws11', 'bs11', 'Ws2', 'bs2')}
    del _L0_ffn_all
    return {'x': x, 'ctx_1024': ctx_1024, 'g_xattn': g_xattn, 'g_ffn': g_ffn, 'L0_xattn_fm_w': _L0_xattn_in['fm_w'], 'L0_xattn_fm_b': _L0_xattn_in['fm_b'], 'L0_xattn_fc_w': _L0_xattn_in['fc_w'], 'L0_xattn_fc_b': _L0_xattn_in['fc_b'], 'L0_ffn_Wg': _L0_ffn_in['Wg'], 'L0_ffn_W1': _L0_ffn_in['W1'], 'L0_ffn_b1': _L0_ffn_in['b1'], 'L0_ffn_W11': _L0_ffn_in['W11'], 'L0_ffn_b11': _L0_ffn_in['b11'], 'L0_ffn_W2': _L0_ffn_in['W2'], 'L0_ffn_b2': _L0_ffn_in['b2'], 'L0_ffn_Ws1': _L0_ffn_in['Ws1'], 'L0_ffn_bs1': _L0_ffn_in['bs1'], 'L0_ffn_Ws11': _L0_ffn_in['Ws11'], 'L0_ffn_bs11': _L0_ffn_in['bs11'], 'L0_ffn_Ws2': _L0_ffn_in['Ws2'], 'L0_ffn_bs2': _L0_ffn_in['bs2']}

def reference(x, ctx_1024, g_xattn, g_ffn, L0_xattn_fm_w, L0_xattn_fm_b, L0_xattn_fc_w, L0_xattn_fc_b, L0_ffn_Wg, L0_ffn_W1, L0_ffn_b1, L0_ffn_W11, L0_ffn_b11, L0_ffn_W2, L0_ffn_b2, L0_ffn_Ws1, L0_ffn_bs1, L0_ffn_Ws11, L0_ffn_bs11, L0_ffn_Ws2, L0_ffn_bs2):
    import jax
    import jax.numpy as jnp

    def _L0_xattn_ref(values, keys, query, fm_w, fm_b, fc_w, fc_b):
        import jax, jax.numpy as jnp
        import numpy as np
        EMBED = 128
        HEADS = 16
        HEAD_DIM = EMBED // HEADS
        EXP_DIM = 2 * HEAD_DIM

        def _feature_map(x, fm_w, fm_b):
            z = jnp.einsum('nshd,ed->nshe', x, fm_w) + fm_b
            return jnp.concatenate([jnp.exp(z), jnp.exp(-z)], axis=-1)
        N, S, _ = query.shape
        v = values.reshape(N, -1, HEADS, HEAD_DIM)
        k = keys.reshape(N, -1, HEADS, HEAD_DIM)
        q = query.reshape(N, -1, HEADS, HEAD_DIM)
        v, k, q = (_feature_map(x, fm_w, fm_b) for x in (v, k, q))
        scores = jnp.einsum('nqhd,nkhd->nhqk', q, k) / jnp.sqrt(jnp.float32(EMBED))
        attn = jax.nn.softmax(scores, axis=-1)
        out = jnp.einsum('nhql,nlhd->nqhd', attn, v)
        out = out.reshape(N, S, HEADS * EXP_DIM)
        return out @ fc_w.T + fc_b

    def _L0_ffn_ref(x, Wg, W1, b1, W11, b11, W2, b2, Ws1, bs1, Ws11, bs11, Ws2, bs2):
        import jax, jax.numpy as jnp
        import numpy as np
        B, T, D = (2, 128, 128)
        E = 16
        H = 256
        K = 2
        HS = H * 2
        b, t, d = x.shape
        xf = x.reshape(b * t, d)
        n = xf.shape[0]
        logits = xf @ Wg
        _, topi = jax.lax.top_k(logits, K)
        mask = jnp.zeros((n, E), bool).at[jnp.arange(n)[:, None], topi].set(True)
        gates = jax.nn.softmax(jnp.where(mask, logits, -jnp.inf), axis=-1)
        y = jnp.zeros_like(xf)
        for e in range(E):
            h = jax.nn.silu(xf @ W1[e] + b1[e]) * (xf @ W11[e] + b11[e])
            y = y + (h @ W2[e] + b2[e]) * gates[:, e, None]
        z = jax.nn.silu(xf @ Ws1 + bs1) * (xf @ Ws11 + bs11) @ Ws2 + bs2
        return (y + z).reshape(b, t, d)
    x = x + jnp.tanh(g_xattn[0]) * _L0_xattn_ref(ctx_1024, ctx_1024, _layernorm(x, axis=-1), L0_xattn_fm_w, L0_xattn_fm_b, L0_xattn_fc_w, L0_xattn_fc_b)
    x = x + jnp.tanh(g_ffn[0]) * _L0_ffn_ref(_layernorm(x, axis=-1), L0_ffn_Wg, L0_ffn_W1, L0_ffn_b1, L0_ffn_W11, L0_ffn_b11, L0_ffn_W2, L0_ffn_b2, L0_ffn_Ws1, L0_ffn_bs1, L0_ffn_Ws11, L0_ffn_bs11, L0_ffn_Ws2, L0_ffn_bs2)
    return x

_drawn_inputs = setup_inputs


def setup_inputs(seed=0):
    import zlib

    import numpy as np

    out = dict(_drawn_inputs(seed))
    spreads = {'L0_xattn_fc_b': (0.0, 0.8)}
    factors = {'L0_ffn_Wg': 8.0,
     'L0_ffn_W1': 8.0,
     'L0_ffn_b1': 8.0,
     'L0_ffn_W11': 8.0,
     'L0_ffn_b11': 8.0,
     'L0_ffn_W2': 8.0,
     'L0_ffn_b2': 53.548,
     'L0_ffn_Ws1': 8.0,
     'L0_ffn_bs1': 8.0,
     'L0_ffn_Ws11': 8.0,
     'L0_ffn_bs11': 8.0,
     'L0_ffn_Ws2': 8.0,
     'L0_ffn_bs2': 41.484}
    for name, (base, spread) in spreads.items():
        noise = np.random.default_rng([zlib.crc32(name.encode()), seed]).standard_normal(out[name].shape)
        drawn = base * np.exp(spread * noise) if base else spread * noise
        out[name] = jnp.asarray(drawn.astype(out[name].dtype))
    for name, factor in factors.items():
        out[name] = (out[name] * factor).astype(out[name].dtype)
    return out
```

```python
from contextlib import ExitStack

import concourse.bass as bass
from concourse import mybir

F32, BF16, F16, U32 = mybir.dt.float32, mybir.dt.bfloat16, mybir.dt.float16, mybir.dt.uint32
ALU = mybir.AluOpType
ACT = mybir.ActivationFunctionType
AX_X = mybir.AxisListType.X

P = 128
NB, T, D = 4, 512, 128
NT = T // P
S = 154
SR = S - P
RP = 32
SP_ = P + RP
H, HD, FD = 16, 8, 16
NG, GH = 4, 4
PARTS = 3
Q_TERMS = (0, 0, 0, 1, 1, 2)
K_TERMS = (0, 1, 2, 0, 1, 0)
KROWS = len(Q_TERMS) * FD
SROWS = KROWS + PARTS
E_ROUTED, HID = 16, 256
E = E_ROUTED + 2
HC = HID // P
WCOLS = 3 * HID
TOK = NB * T
EPS = 1e-5
SCALE = float(D) ** -0.5

C_FM, C_MASK, C_SGN, C_FMB, C_FMBV, C_WG, C_GX, C_GF, C_IOTA = 0, 8, 24, 25, 26, 34, 50, 51, 52
C_B1 = 68
C_B11 = C_B1 + E * HC
C_B2 = C_B11 + E * HC
C_END = C_B2 + E

UNITS = 5
MAXU = NT * H // 2
SLOTS = NB * NG
S_RING, P_RING = 3, 8
MAX_AT = [(3, 2, 2, 2, 1, 1), (3, 2, 2, 2, 1, 1), (2, 2, 2, 2, 1, 1), (0, 0, 0, 0, 0, 0)]
W_RING = 2
WH = WCOLS // 2
X_RING = 2
V_OPS = 2 * NB + 2 * GH


def misc_order():
    out = [("qT", 0), ("cT", 0), ("cT", 1), ("qA", 0), ("qB", 0)]
    out += [("zk", i) for i in range(4)] + [("v", 0), ("v", 1)]
    out += [("qT", 1), ("qA", 1), ("qB", 1), ("nm", 0)]
    for n in range(NB):
        old = n >= 2
        out += [("fc", n - 2)] * old
        out += [("qT", n + 2)] * (n + 2 < NB)
        out += [("xT", n - 2)] * old
        out += [("qA", n + 2), ("qB", n + 2)] * (n + 2 < NB)
        out += [("lg", n - 2)] * old
        out += [("nm", n + 1)] * (n + 1 < NB)
        out += [("gT", n - 2)] * old
    out += [(k, n) for n in (NB - 2, NB - 1) for k in ("fc", "xT", "lg", "gT")]
    out += [("yT", b) for b in range(NB)]
    return {key: (i % 2, i // 2) for i, key in enumerate(out)}


MISC = misc_order()
LN = [(1, 0), (1, 1), (1, 2), (1, 3), (2, 0), (2, 1), (2, 2), (2, 3)]


def build(nc, x, ctx, const, fcw, wall, out):
    with ExitStack() as stack:
        def sb(name, shape, dt=F32):
            return stack.enter_context(nc.sbuf_tensor(name, shape, dt))

        def sem(name):
            return stack.enter_context(nc.semaphore(name))

        bank = [stack.enter_context(nc.psum_tensor(f"bank{i}", [P, 512], F32)) for i in range(8)]
        s_bank, ot_bank, mx_bank, misc_bank = bank[0:3], bank[3], bank[4:6], bank[6:8]
        h1_bank, h2_bank, y_bank = bank[0:2], bank[2:4], bank[4:6]

        k_scr = nc.dram_tensor("k_scr", [PARTS, 2, P, NB * SP_], BF16, kind="Internal").ap()
        q_scr = nc.dram_tensor("q_scr", [NB, PARTS, 2, P, T], BF16, kind="Internal").ap()
        dn_scr = nc.dram_tensor("dn_scr", [NB, 2, GH, NG, T], F32, kind="Internal").ap()
        g_scr = nc.dram_tensor("g_scr", [E, TOK], F32, kind="Internal").ap()

        cst = sb("cst", [P, C_END])
        ident = sb("ident", [P, P])
        ident16 = sb("ident16", [P, P], BF16)
        fc_sb = sb("fc_sb", [P, NG + 1, D])
        bd = sb("bd", [P, H, 2, HD])
        sgnb = sb("sgnb", [P, 1])
        b1 = sb("b1", [P, HC])
        tanhg = sb("tanhg", [P, 2])
        mhalf = sb("mhalf", [P, NT])
        xs = sb("xs", [P, NB * NT, D])
        xhat = sb("xhat", [P, X_RING, NT, D])
        stats = sb("stats", [P, len(LN), NT, 6])
        mv = sb("mv", [P, len(LN), NT, 2])
        veps = sb("veps", [P, len(LN), NT])
        rstd = sb("rstd", [P, len(LN), NT])
        arena = sb("arena", [P, 2 * H * T // 2])
        qs = arena[:, :].bitcast(BF16).rearrange("p (b h t) -> p b h t", b=2, h=H)
        KC = 2 * NB * SP_
        f_k = arena[:, 0:KC].rearrange("p (a n k) -> p a n k", a=2, n=NB)
        r_k = arena[:, KC:2 * KC]
        kp = arena[:, 2 * KC:2 * KC + PARTS * KC // 2].bitcast(BF16).rearrange("p (c k) -> p c k", c=PARTS)
        ctx_sb = arena[:, 4608:5120].rearrange("p (n d) -> p n d", n=NB)
        ctx_rm = arena[:, 5120:5248]
        ctxT = arena[:, 5248:5248 + NB * SP_].rearrange("p (n k) -> p n k", n=NB)
        v_tmp = arena[:, 6016:6528]
        v_tmr = arena[:, 6528:7040]
        gate_rows = [arena[:, b * T:(b + 1) * T] for b in range(NB)]
        acc = [arena[:, (4 + b) * T:(5 + b) * T] for b in range(NB)]
        sil = [arena[:, (8 + c) * T:(9 + c) * T] for c in range(HC)]
        hf = [arena[:, (10 + c) * T:(11 + c) * T] for c in range(HC)]
        hsp = arena[:, 12 * T:16 * T].bitcast(F16).rearrange("p (l b c t) -> p l b c t", l=2, b=2, c=HC)
        ks = sb("ks", [P, H, NB, SP_], BF16)
        v_sb = sb("v_sb", [P, NB, H, 2 * FD])
        one_row = v_sb[0:1, 0, 0, FD:FD + 1].to_broadcast([1, P])
        v_rm = sb("v_rm", [P, NB, NG, P])
        qT = sb("qT", [P, T])
        f_q = sb("f_q", [P, 2, T])
        r_q = sb("r_q", [P, T])
        qp = sb("qp", [P, PARTS, 2 * T], BF16)
        mx = sb("mx", [P, NT, H])
        nm_r = sb("nm_r", [P, NT, H])
        nm = sb("nm", [P, NT, PARTS, H], BF16)
        nmT = sb("nmT", [PARTS * H, T], BF16)
        prob = sb("prob", [P, P_RING, T])
        osum = sb("osum", [P, 2, NG, T])
        dn = sb("dn", [P, 2, NG * GH * T // P])
        den = sb("den", [P, 2, T])
        x2T = sb("x2T", [P, T])
        xh = sb("xh", [P, TOK], F16)
        xl = sb("xl", [P, TOK], F16)
        lg = sb("lg", [P, NT, E_ROUTED])
        top = sb("top", [P, NT, 8])
        idx = sb("idx", [P, NT, 8], U32)
        idf = sb("idf", [P, NT, 8])
        oh = sb("oh", [P, 3, NT, E_ROUTED])
        gex = sb("gex", [P, NT, E_ROUTED])
        gsum = sb("gsum", [P, 2, NT])
        gts = sb("gts", [P, NT, E])
        gT = x2T[0:E, :]
        w_st = sb("w_st", [P, W_RING, WH])
        w_hi = sb("w_hi", [P, E, WCOLS], F16)
        w_lo = sb("w_lo", [P, E, WCOLS], F16)
        yt = f_q
        fin = prob[:, 0:2, :]

        bdz = bd[:, :, :, :].rearrange("p h s e -> p (h s e)")

        d_const, d_fc, d_ctx = sem("d_const"), sem("d_fc"), sem("d_ctx")
        d_x = [sem(f"d_x{n}") for n in range(NB)]
        d_w = [sem(f"d_w{i}") for i in range(W_RING)]
        d_kout, d_kin, d_qout, d_nm, d_gout = (sem(f"d_{k}") for k in ("kout", "kin", "qout", "nm", "gout"))
        d_qin = [sem(f"d_qin{i}") for i in range(2)]
        d_gate = [sem(f"d_gate{b}") for b in range(NB)]
        d_out = [sem(f"d_out{i}") for i in range(2)]
        z_rem, ident_made, ones_made, half_made = sem("z_rem"), sem("ident_made"), sem("ones_made"), sem("half_made")
        bd_made, sgnb_made, tanh_made, ident16_made = (sem(k) for k in ("bd_made", "sgnb_made", "tanh_made", "ident16_made"))
        kp_made, vz_made, v_made = (sem(k) for k in ("kp_made", "vz_made", "v_made"))
        misc_full = [sem(f"misc_full{i}") for i in range(2)]
        misc_free = [sem(f"misc_free{i}") for i in range(2)]
        var_made, rstd_made, xhat_made = (sem(k) for k in ("var_made", "rstd_made", "xhat_made"))
        qp_made, max_done, max_read, nm_made = (sem(k) for k in ("qp_made", "max_done", "max_read", "nm_made"))
        s_done, p_made, pv_done, o_made, den_made, on_made, rec_made = (
            sem(k) for k in ("s_done", "p_made", "pv_done", "o_made", "den_made", "on_made", "rec_made"))
        d_dn = [sem(f"d_dn{i}") for i in range(4)]
        xh_made, lgm_made, gex_made, gts_made = (sem(k) for k in ("xh_made", "lgm_made", "gex_made", "gts_made"))
        whi_made, wlo_made = sem("whi_made"), sem("wlo_made")
        h1_done, h2_done, sil_made, hf_made, hi_made, lo_made = (
            sem(k) for k in ("h1_done", "h2_done", "sil_made", "hf_made", "hi_made", "lo_made"))
        bias_made = sem("bias_made")
        y_done, yt_made, acc_made, fin_made = (sem(k) for k in ("y_done", "yt_made", "acc_made", "fin_made"))
        v_chain, g_chain = sem("v_chain"), sem("g_chain")

        block = stack.enter_context(nc.Block())

        def ln_index(kind, n):
            return LN.index((kind, n))

        @block.sync
        def _(sp):
            sp.dma_start(xs[:, 0:NT, :], x[0]).then_inc(d_x[0], 16)
            sp.dma_start(cst[:, :], const).then_inc(d_const, 16)
            sp.dma_start(ctx_sb, ctx[:, 0:P, :].rearrange("n k d -> k n d")).then_inc(d_ctx, 16)
            sp.wait_ge(z_rem, 1)
            for n in range(NB):
                sp.dma_start(ctx_rm[RP * n:RP * n + SR, :], ctx[n, P:S, :]).then_inc(d_ctx, 16)
            for n in range(1, NB):
                sp.dma_start(xs[:, NT * n:NT * (n + 1), :], x[n]).then_inc(d_x[n], 16)
            sp.dma_start(fc_sb[:, :, :], fcw).then_inc(d_fc, 16)

            def stack_queries(n):
                sp.wait_ge(qp_made, n + 1)
                for c in range(PARTS):
                    sp.dma_start(q_scr[n, c].rearrange("a p t -> p a t"),
                                 qp[:, c, :].rearrange("p (a t) -> p a t", a=2)).then_inc(d_qout, 16)
                sp.wait_ge(d_qout, 16 * PARTS * (n + 1))
                if n >= 2:
                    sp.wait_ge(s_done, UNITS * NG * (n - 1))
                if n == 0:
                    sp.wait_ge(d_kin, 16 * len(K_TERMS))
                    sp.wait_ge(v_made, V_OPS)
                for i, c in enumerate(Q_TERMS):
                    sp.dma_start(qs[FD * i:FD * (i + 1), n % 2, :, :],
                                 q_scr[n, c].rearrange("a (h f) t -> f (a h) t", f=FD)).then_inc(d_qin[n % 2], 16)

            sp.wait_ge(kp_made, 1)
            for c in range(PARTS):
                sp.dma_start(k_scr[c].rearrange("a p k -> p a k"),
                             kp[:, c, :].rearrange("p (a k) -> p a k", a=2)).then_inc(d_kout, 16)
            sp.wait_ge(d_kout, 16 * PARTS)
            for i, c in enumerate(K_TERMS):
                sp.dma_start(ks[FD * i:FD * (i + 1), :, :, :].rearrange("f h n k -> f h (n k)"),
                             k_scr[c].rearrange("a (h f) k -> f (a h) k", f=FD)).then_inc(d_kin, 16)
            def move_denominators(n):
                rows = osum[FD:P:2 * FD, n % 2, :, :]
                spread = dn_scr[n].rearrange("i j g t -> i (j g t)").rearrange("i (p k) -> i p k", p=P)
                sp.wait_ge(o_made, NG * (n + 1))
                sp.dma_start(dn_scr[n, 0], rows).then_inc(d_dn[0], 16)
                sp.wait_ge(d_dn[0], 16 * (n + 1))
                sp.dma_start(dn[:, 0, :], spread[0]).then_inc(d_dn[1], 16)
                sp.wait_ge(rec_made, n + 1)
                sp.dma_start(spread[1], dn[:, 1, :]).then_inc(d_dn[2], 16)
                sp.wait_ge(d_dn[2], 16 * (n + 1))
                sp.dma_start(rows, dn_scr[n, 1]).then_inc(d_dn[3], 16)

            stack_queries(0)
            stack_queries(1)
            stack_queries(2)
            for n in range(NB):
                move_denominators(n)
                if n + 3 < NB:
                    stack_queries(n + 3)

            sp.wait_ge(s_done, UNITS * SLOTS)
            sp.wait_ge(d_gout, 16 * NB)
            for b in range(NB):
                sp.dma_start(gate_rows[b], g_scr[0:1, b * T:(b + 1) * T].to_broadcast([P, T])).then_inc(d_gate[b], 16)
            with sp.Fori(1, E) as e:
                for b in range(NB):
                    sp.wait_ge(yt_made, e * NB + (b + 1 - NB))
                    sp.dma_start(gate_rows[b],
                                 g_scr[bass.ds(e, 1), b * T:(b + 1) * T].to_broadcast([P, T])).then_inc(d_gate[b], 16)
            for b in range(NB):
                sp.wait_ge(fin_made, b + 1)
                sp.dma_start(out[b], fin[:, b % 2, :].rearrange("p (t d) -> p t d", t=NT)).then_inc(d_out[b % 2], 16)
            for i in range(2):
                sp.wait_ge(d_out[i], 16 * NB // 2)

        @block.gpsimd
        def _(pool):
            nc.gpsimd.memset(ctx_rm, 0.0).then_inc(z_rem, 1)
            nc.gpsimd.memset(mhalf[:, :], -0.5).then_inc(half_made, 1)
            nc.gpsimd.memset(ident[:, :], 0.0).then_inc(g_chain, 1)
            pool.wait_ge(g_chain, 1)
            nc.gpsimd.affine_select(out=ident[:, :], in_=ident[:, :], compare_op=ALU.not_equal, fill=1.0,
                                    base=0, pattern=[[-1, P]], channel_multiplier=1).then_inc(ident_made, 1)
            nc.gpsimd.memset(v_sb[:, :, :, :], 1.0).then_inc(ones_made, 1)
            nc.gpsimd.memset(gts[:, :, :], 1.0).then_inc(ones_made, 1)
            pool.wait_ge(ident_made, 1)
            pool.wait_ge(ones_made, 2)
            nc.gpsimd.memset(ks[KROWS:SROWS, :, :, :], 1.0).then_inc(ones_made, 1)
            pool.wait_ge(ones_made, 3)

            def rsqrt(kind, n):
                l = ln_index(kind, n)
                pool.wait_ge(var_made, l + 1)
                nc.gpsimd.tensor_tensor(rstd[:, l, :], veps[:, l, :], mhalf[:, :], ALU.pow).then_inc(rstd_made, 1)

            def weights_low(e):
                for i in (2 * e, 2 * e + 1):
                    pool.wait_ge(whi_made, i + 1)
                    cols = slice(i % 2 * WH, (i % 2 + 1) * WH)
                    nc.gpsimd.tensor_tensor(w_lo[:, e, cols], w_st[:, i % W_RING, :], w_hi[:, e, cols],
                                            ALU.subtract).then_inc(wlo_made, 1)

            pool.wait_ge(half_made, 1)
            for n in range(3):
                rsqrt(1, n)
            weights_low(0)
            weights_low(1)

            def normalise(n):
                for g in range(NG):
                    k = NG * n + g
                    pool.wait_ge(den_made, k + 1)
                    rows = osum[:, n % 2, g, :]
                    nc.gpsimd.tensor_tensor(rows, rows, den[:, k % 2, :], ALU.mult).then_inc(on_made, 1)

            for s in range(SLOTS):
                n, g = divmod(s, NG)
                if g == 0 and n >= 2:
                    rsqrt(2, n - 2)
                if g == 3 and n + 3 < NB:
                    rsqrt(1, n + 3)
                weights_low(s + 2)
                if g == 3 and n >= 1:
                    normalise(n - 1)
            rsqrt(2, NB - 2)
            normalise(NB - 1)
            rsqrt(2, NB - 1)

            pool.wait_ge(s_done, UNITS * SLOTS)
            for b in range(NB):
                last = nc.gpsimd.memset(acc[b], 0.0)
                last.then_inc(g_chain, 1)
            pool.wait_ge(g_chain, 1 + NB)

            def add(b):
                nc.gpsimd.tensor_tensor(acc[b], acc[b], yt[:, b % 2, :], ALU.add).then_inc(acc_made, 1)

            for b in range(NB):
                pool.wait_ge(yt_made, b + 1)
                add(b)
            with pool.Fori(1, E) as e:
                for b in range(NB):
                    pool.wait_ge(yt_made, e * NB + (b + 1))
                    pool.wait_ge(acc_made, e * NB + (b + 1 - NB))
                    add(b)

        @block.scalar
        def _(act):
            def full(key):
                i, m = MISC[key]
                act.wait_ge(misc_full[i], m + 1)
                return misc_bank[i], misc_free[i]

            def load_weights(i):
                if i >= W_RING:
                    act.wait_ge(wlo_made, i - W_RING + 1)
                act.dma_start(w_st[:, i % W_RING, :], wall[i // 2, :, i % 2 * WH:(i % 2 + 1) * WH])\
                    .then_inc(d_w[i % W_RING], 16)

            def weights_high(i):
                act.wait_ge(d_w[i % W_RING], 16 * (i // W_RING + 1))
                nc.scalar.activation(w_hi[:, i // 2, i % 2 * WH:(i % 2 + 1) * WH], w_st[:, i % W_RING, :],
                                     ACT.Copy).then_inc(whi_made, 1)
                if i >= 1 and i + 1 < 2 * E:
                    load_weights(i + 1)

            load_weights(0)
            load_weights(1)

            act.wait_ge(d_const, 16)
            nc.scalar.activation(tanhg[:, :], cst[:, C_GX:C_GX + 2], ACT.Tanh).then_inc(tanh_made, 1)

            def copy_qT(n):
                src, free = full(("qT", n))
                if n >= 1:
                    i, m = MISC[("qB", n - 1)]
                    act.wait_ge(misc_full[i], m + 1)
                nc.scalar.activation(qT[:, :], src[:, :], ACT.Copy).then_inc(free, 1)

            def exp_q(n, half):
                if half == 0 and n >= 1:
                    act.wait_ge(qp_made, n)
                src, free = full(("qA" if half == 0 else "qB", n))
                act.wait_ge(sgnb_made, 1)
                nc.scalar.activation(f_q[:, half, :], src[:, :], ACT.Exp, bias=sgnb[:, :],
                                     scale=cst[:, C_SGN:C_SGN + 1]).then_inc(free, 1)

            copy_qT(0)
            src, free = full(("cT", 0))
            nc.scalar.activation(ctxT[:, :, 0:P], src[:, :].rearrange("p (n k) -> p n k", n=NB),
                                 ACT.Copy).then_inc(free, 1)
            src, free = full(("cT", 1))
            nc.scalar.activation(ctxT[:, :, P:SP_], src[:, 0:P].rearrange("p (n k) -> p n k", n=NB),
                                 ACT.Copy).then_inc(free, 1)
            exp_q(0, 0)
            exp_q(0, 1)
            fk = arena[:, 0:KC]
            for i in range(4):
                src, free = full(("zk", i))
                nc.scalar.activation(fk[:, i * KC // 4:(i + 1) * KC // 4], src[:, 0:KC // 4], ACT.Exp, bias=sgnb[:, :],
                                     scale=cst[:, C_SGN:C_SGN + 1]).then_inc(free, 1)
            i, m = MISC[("v", 0)]
            act.wait_ge(misc_free[i], m + 1)
            act.wait_ge(ones_made, 1)
            z = v_tmp.rearrange("p (n h e) -> p n h e", n=NB, h=H)
            for k, sg in enumerate((1.0, -1.0)):
                for n in range(NB):
                    ins = nc.scalar.activation(v_sb[:, n, :, k * HD:(k + 1) * HD], z[:, n, :, :], ACT.Exp, scale=sg)
                    ins.then_inc(v_made, 1)
            i, m = MISC[("v", 1)]
            act.wait_ge(misc_free[i], m + 1)
            act.wait_ge(vz_made, 1)
            z = v_tmr[:, 0:NB * NG * HD].rearrange("p (n g e) -> p n g e", n=NB, g=NG)
            for j in range(GH):
                for k, sg in enumerate((1.0, -1.0)):
                    rows = slice(RP * j, RP * j + SR)
                    nc.scalar.activation(v_rm[rows, :, :, RP * j + k * HD:RP * j + (k + 1) * HD],
                                         z[rows, :, :, :], ACT.Exp, scale=sg).then_inc(v_made, 1)
            copy_qT(1)
            exp_q(1, 0)
            exp_q(1, 1)
            for i in range(4):
                weights_high(i)

            def move_max(n):                          
                src, free = full(("nm", n))
                if n >= 1:
                    act.wait_ge(d_nm, 16 * PARTS * n)
                if n >= 2:
                    act.wait_ge(s_done, UNITS * NG * (n - 1))
                nc.scalar.activation(nmT[:, :], src[0:PARTS * H, :].bitcast(BF16)[:, 0:T], ACT.Copy)\
                    .then_inc(free, 1)
                act.wait_ge(free, MISC[("nm", n)][1] + 1)
                for c in range(PARTS):
                    act.dma_start(qs[KROWS + c:KROWS + c + 1, n % 2, :, :], nmT[c * H:(c + 1) * H, :])\
                        .then_inc(d_nm, 16)

            move_max(0)

            def probs(s, u):
                k = UNITS * s + u
                act.wait_ge(s_done, k + 1)
                if k >= P_RING:
                    act.wait_ge(pv_done, (k - P_RING) // UNITS + 1)
                nc.scalar.activation(prob[:, k % P_RING, :], s_bank[k % S_RING][:, :], ACT.Exp,
                                     scale=SCALE).then_inc(p_made, 1)

            def copy_out(s):
                act.wait_ge(pv_done, s + 1)
                n, g = divmod(s, NG)
                if n >= 2:
                    i, m = MISC[("fc", n - 2)]
                    act.wait_ge(misc_full[i], m + 1)
                nc.scalar.activation(osum[:, n % 2, g, :], ot_bank[:, :], ACT.Copy).then_inc(o_made, 1)

            def copy_x2T(n):
                src, free = full(("xT", n))
                if n >= 1:
                    i, m = MISC[("lg", n - 1)]
                    act.wait_ge(misc_full[i], m + 1)
                    act.wait_ge(xh_made, n)
                    act.wait_ge(d_gout, 16 * n)
                nc.scalar.activation(x2T[:, :], src[:, :], ACT.Copy).then_inc(free, 1)

            def exp_gates(n):
                act.wait_ge(lgm_made, n + 1)
                nc.scalar.activation(gex[:, :, :], lg[:, :, :], ACT.Exp).then_inc(gex_made, 1)

            def move_gates(n):
                src, free = full(("gT", n))
                act.wait_ge(xh_made, n + 1)
                nc.scalar.activation(gT[:, :], src[0:E, :], ACT.Copy).then_inc(free, 1)
                act.wait_ge(free, MISC[("gT", n)][1] + 1)
                act.dma_start(g_scr[:, n * T:(n + 1) * T], gT[:, :]).then_inc(d_gout, 16)

            for s in range(SLOTS):
                n, g = divmod(s, NG)
                for u in range(3):
                    probs(s, u)
                if g == 1 and n >= 2:
                    copy_x2T(n - 2)
                if g == 3 and n + 1 < NB:
                    move_max(n + 1)
                if g == 2 and n >= 2:
                    exp_gates(n - 2)
                if s >= 1:
                    copy_out(s - 1)
                weights_high(2 * s + 4)
                for u in range(3, UNITS):
                    probs(s, u)
                if g == 0 and n + 2 < NB:
                    copy_qT(n + 2)
                if g == 1 and n + 2 < NB:
                    exp_q(n + 2, 0)
                    exp_q(n + 2, 1)
                if g == 3 and n >= 2:
                    move_gates(n - 2)
                weights_high(2 * s + 5)
            copy_out(SLOTS - 1)
            for n in (NB - 2, NB - 1):
                copy_x2T(n)
                exp_gates(n)
                move_gates(n)

            act.wait_ge(s_done, UNITS * SLOTS)

            def expert_bias(e):
                nc.scalar.activation(b1[:, :], cst[:, bass.ds(e * HC + C_B1, HC)], ACT.Copy).then_inc(bias_made, 1)

            def silu(c):
                nc.scalar.activation(sil[c], h1_bank[c][:, :], ACT.Silu,
                                     bias=b1[:, c:c + 1]).then_inc(sil_made, 1)

            def high(b, c):
                nc.scalar.activation(hsp[:, 0, b % 2, c, :], hf[c], ACT.Copy).then_inc(hi_made, 1)

            def step(e, b, c, first):
                q = 2 * b + c
                if q == 0:
                    if not first:
                        act.wait_ge(sil_made, e * 8)
                    expert_bias(e)
                    act.wait_ge(bias_made, e + 1)
                act.wait_ge(h1_done, e * 8 + (q + 1))
                if not (first and q < 2):
                    act.wait_ge(hf_made, e * 8 + (q - 1))
                silu(c)
                if first and q == 0:
                    return
                pb, pc = ((b, 0) if c else ((b - 1) % NB, 1))
                act.wait_ge(hf_made, e * 8 + q)
                if not (first and q <= 4):
                    act.wait_ge(y_done, e * 4 + (q - 5) // 2 + 0 if q % 2 else e * 4 + (q - 6) // 2)
                high(pb, pc)

            for b in range(NB):
                for c in range(HC):
                    step(0, b, c, True)
            with act.Fori(1, E) as e:
                for b in range(NB):
                    for c in range(HC):
                        step(e, b, c, False)
            act.wait_ge(hf_made, 8 * E)
            act.wait_ge(y_done, 4 * E - 2)
            high(NB - 1, 1)

        @block.vector
        def _(dve):
            chain = [0]

            def link(ins):
                chain[0] += 1
                ins.then_inc(v_chain, 1)
                dve.wait_ge(v_chain, chain[0])

            def full(key):
                i, m = MISC[key]
                dve.wait_ge(misc_full[i], m + 1)
                return misc_bank[i], misc_free[i]

            def layer_norm(kind, n):
                l = ln_index(kind, n)
                if kind == 1:
                    dve.wait_ge(d_x[n], 16)
                for t in range(NT):
                    ins = nc.vector.bn_stats(stats[:, l, t, :], xs[:, NT * n + t, :])
                link(ins)
                for t in range(NT):
                    ins = nc.vector.bn_aggr(mv[:, l, t, :], stats[:, l, t, :])
                link(ins)
                nc.vector.tensor_scalar(veps[:, l, :], mv[:, l, :, 1], EPS, None, ALU.add).then_inc(var_made, 1)
                dve.wait_ge(rstd_made, l + 1)
                if l >= X_RING:
                    kind_, n_ = LN[l - X_RING]
                    i, m = MISC[("qT" if kind_ == 1 else "xT", n_)]
                    dve.wait_ge(misc_full[i], m + 1)
                for t in range(NT):
                    ins = nc.vector.tensor_scalar(xhat[:, l % X_RING, t, :], xs[:, NT * n + t, :], mv[:, l, t, 0:1],
                                                  rstd[:, l, t:t + 1], ALU.subtract, ALU.mult)
                ins.then_inc(xhat_made, 1)

            def split(src, rest, parts):
                link(nc.vector.tensor_copy(parts[0], src))
                link(nc.vector.tensor_tensor(rest, src, parts[0], ALU.subtract))
                link(nc.vector.tensor_copy(parts[1], rest))
                return nc.vector.tensor_tensor(parts[2], rest, parts[1], ALU.subtract)

            def split_q(n):
                for half in ("qA", "qB"):
                    i, m = MISC[(half, n)]
                    dve.wait_ge(misc_free[i], m + 1)
                if n >= 1:
                    dve.wait_ge(d_qout, 16 * PARTS * n)
                link(split(f_q[:, 0, :], r_q[:, :], [qp[:, c, 0:T] for c in range(PARTS)]))
                split(f_q[:, 1, :], r_q[:, :], [qp[:, c, T:2 * T] for c in range(PARTS)]).then_inc(qp_made, 1)

            layer_norm(1, 0)
            dve.wait_ge(d_const, 16)
            nc.vector.tensor_tensor(bd[:, :, :, :].rearrange("p h s e -> p h s e"),
                                    cst[:, C_MASK:C_MASK + H].rearrange("p (h s e) -> p h s e", s=1, e=1)
                                    .to_broadcast([P, H, 2, HD]),
                                    cst[:, C_FM:C_FM + HD].rearrange("p (h s e) -> p h s e", h=1, s=1)
                                    .to_broadcast([P, H, 2, HD]), ALU.mult).then_inc(bd_made, 1)
            nc.vector.tensor_tensor(sgnb[:, :], cst[:, C_FMB:C_FMB + 1], cst[:, C_SGN:C_SGN + 1],
                                    ALU.mult).then_inc(sgnb_made, 1)
            dve.wait_ge(ident_made, 1)
            nc.vector.tensor_copy(ident16[:, :], ident[:, :]).then_inc(ident16_made, 1)
            link(nc.vector.memset(v_rm[:, :, :, :], 0.0))
            for j in range(GH):
                ins = nc.vector.memset(v_rm[RP * j:RP * j + SR, :, :, RP * j + FD:RP * (j + 1)], 1.0)
            ins.then_inc(vz_made, 1)
            layer_norm(1, 1)
            split_q(0)
            for i in range(4):
                b, m = MISC[("zk", i)]
                dve.wait_ge(misc_free[b], m + 1)
            link(nc.vector.memset(f_k[:, :, :, S:SP_], 0.0))
            split(arena[:, 0:KC], r_k, [kp[:, c, :] for c in range(PARTS)]).then_inc(kp_made, 1)
            src, free = full(("v", 0))
            vb = cst[:, C_FMBV:C_FMBV + HD].rearrange("p (m e) -> p m e", m=1).to_broadcast([P, NB * H, HD])
            nc.vector.tensor_tensor(v_tmp.rearrange("p (m e) -> p m e", e=HD),
                                    src[:, :].rearrange("p (m e) -> p m e", e=HD), vb, ALU.add)\
                .then_inc(free, 1)
            src, free = full(("v", 1))
            vb = cst[:, C_FMBV:C_FMBV + HD].rearrange("p (m e) -> p m e", m=1).to_broadcast([P, NB * NG, HD])
            nc.vector.tensor_tensor(v_tmr[:, 0:NB * NG * HD].rearrange("p (m e) -> p m e", e=HD),
                                    src[:, 0:NB * NG * HD].rearrange("p (m e) -> p m e", e=HD), vb, ALU.add)\
                .then_inc(free, 1)
            split_q(1)
            layer_norm(1, 2)

            def row_max(m):
                t, pair = divmod(m % MAXU, H // 2)
                dve.wait_ge(max_done, m + 1)
                nc.vector.reduce_max(mx[:, t, 2 * pair:2 * pair + 2],
                                     mx_bank[m % 2][:, 0:2 * S].rearrange("p (h k) -> p h k", h=2), AX_X)\
                    .then_inc(max_read, 1)

            def split_max(n):
                dve.wait_ge(max_read, MAXU * (n + 1))
                if n >= 1:
                    i, m = MISC[("nm", n - 1)]
                    dve.wait_ge(misc_full[i], m + 1)
                link(nc.vector.tensor_scalar(nm[:, :, 0, :], mx[:, :, :], -1.0, None, ALU.mult))
                link(nc.vector.scalar_tensor_tensor(out=nm_r[:, :, :], in0=mx[:, :, :], scalar=-1.0,
                                                    in1=nm[:, :, 0, :], op0=ALU.mult, op1=ALU.subtract))
                link(nc.vector.tensor_copy(nm[:, :, 1, :], nm_r[:, :, :]))
                nc.vector.tensor_tensor(nm[:, :, 2, :], nm_r[:, :, :], nm[:, :, 1, :],
                                        ALU.subtract).then_inc(nm_made, 1)

            for m in range(MAXU):
                row_max(m)
            split_max(0)

            def reciprocals(n):
                dve.wait_ge(d_dn[1], 16 * (n + 1))
                if n >= 1:
                    dve.wait_ge(d_dn[2], 16 * n)
                nc.vector.reciprocal(dn[:, 1, :], dn[:, 0, :]).then_inc(rec_made, 1)

            def spread(n):
                dve.wait_ge(d_dn[3], 16 * (n + 1))
                for g in range(NG):
                    k = NG * n + g
                    if k >= 2:
                        dve.wait_ge(on_made, k - 1)
                    nc.vector.stream_shuffle(den[:, k % 2, :], osum[:, n % 2, g, :],
                                             [FD] * (2 * FD)).then_inc(den_made, 1)

            def add_attention(n):
                src, free = full(("fc", n))
                dve.wait_ge(tanh_made, 1)
                rows = xs[:, NT * n:NT * (n + 1), :].rearrange("p t d -> p (t d)")
                ins = nc.vector.scalar_tensor_tensor(out=rows, in0=src[:, :], scalar=tanhg[:, 0:1], in1=rows,
                                                     op0=ALU.mult, op1=ALU.add)
                ins.then_inc(free, 1)
                dve.wait_ge(free, MISC[("fc", n)][1] + 1)

            def split_x2(n):
                i, m = MISC[("xT", n)]
                dve.wait_ge(misc_free[i], m + 1)
                cols = slice(n * T, (n + 1) * T)
                link(nc.vector.tensor_copy(xh[:, cols], x2T[:, :]))
                nc.vector.tensor_tensor(xl[:, cols], x2T[:, :], xh[:, cols], ALU.subtract).then_inc(xh_made, 1)

            def route(n):
                src, free = full(("lg", n))
                if n >= 1:
                    dve.wait_ge(gex_made, n)
                nc.vector.tensor_copy(lg[:, :, :], src[:, 0:NT * E_ROUTED].rearrange("p (t e) -> p t e", t=NT))\
                    .then_inc(free, 1)
                dve.wait_ge(free, MISC[("lg", n)][1] + 1)
                for t in range(NT):
                    ins = nc.vector.max(top[:, t, :], lg[:, t, :])
                link(ins)
                for t in range(NT):
                    ins = nc.vector.max_index(idx[:, t, :], top[:, t, :], lg[:, t, :])
                link(ins)
                nc.vector.tensor_tensor(lg[:, :, :], lg[:, :, :], top[:, :, 0:1].to_broadcast([P, NT, E_ROUTED]),
                                        ALU.subtract).then_inc(lgm_made, 1)
                link(nc.vector.tensor_copy(idf[:, :, :], idx[:, :, :]))
                iota = cst[:, C_IOTA:C_IOTA + E_ROUTED].rearrange("p (t e) -> p t e", t=1)\
                    .to_broadcast([P, NT, E_ROUTED])
                for i in range(2):
                    ins = nc.vector.tensor_tensor(oh[:, i, :, :], iota,
                                                  idf[:, :, i:i + 1].to_broadcast([P, NT, E_ROUTED]), ALU.is_equal)
                link(ins)
                link(nc.vector.tensor_tensor(oh[:, 2, :, :], oh[:, 0, :, :], oh[:, 1, :, :], ALU.add))

            def gates(n):
                dve.wait_ge(gex_made, n + 1)
                dve.wait_ge(ones_made, 2)
                if n >= 1:
                    i, m = MISC[("gT", n - 1)]
                    dve.wait_ge(misc_full[i], m + 1)
                link(nc.vector.tensor_tensor(oh[:, 0, :, :], gex[:, :, :], oh[:, 2, :, :], ALU.mult))
                link(nc.vector.reduce_sum(gsum[:, 0, :], oh[:, 0, :, :], AX_X))
                link(nc.vector.reciprocal(gsum[:, 1, :], gsum[:, 0, :]))
                nc.vector.tensor_tensor(gts[:, :, 2:E], oh[:, 0, :, :],
                                        gsum[:, 1, :].rearrange("p (t e) -> p t e", e=1)
                                        .to_broadcast([P, NT, E_ROUTED]), ALU.mult).then_inc(gts_made, 1)

            m = MAXU
            for s in range(SLOTS):
                n, g = divmod(s, NG)
                last = m + (sum(MAX_AT[g]) if n + 1 < NB else 0)
                for i in range(m, last):
                    row_max(i)
                m = last
                if g == 0 and n >= 2:
                    add_attention(n - 2)
                    layer_norm(2, n - 2)
                if g == 1:
                    if n >= 1:
                        reciprocals(n - 1)
                    if n >= 2:
                        split_x2(n - 2)
                        route(n - 2)
                if g == 2:
                    if n + 1 < NB:
                        split_max(n + 1)
                    if n + 2 < NB:
                        split_q(n + 2)
                if g == 3:
                    if n >= 2:
                        gates(n - 2)
                    if n + 3 < NB:
                        layer_norm(1, n + 3)
                    if n >= 1:
                        spread(n - 1)
            add_attention(NB - 2)
            layer_norm(2, NB - 2)
            reciprocals(NB - 1)
            split_x2(NB - 2)
            route(NB - 2)
            gates(NB - 2)
            spread(NB - 1)
            add_attention(NB - 1)
            layer_norm(2, NB - 1)
            split_x2(NB - 1)
            route(NB - 1)
            gates(NB - 1)

            def hidden(e, b, c):
                nc.vector.scalar_tensor_tensor(out=hf[c], in0=h2_bank[c][:, :],
                                               scalar=cst[:, bass.ds(e * HC + (C_B11 + c), 1)], in1=sil[c],
                                               op0=ALU.add, op1=ALU.mult).then_inc(hf_made, 1)

            def low(b, c):
                nc.vector.tensor_tensor(hsp[:, 1, b % 2, c, :], hf[c], hsp[:, 0, b % 2, c, :],
                                        ALU.subtract).then_inc(lo_made, 1)

            def gated(e, b):
                nc.vector.scalar_tensor_tensor(out=yt[:, b % 2, :], in0=y_bank[b % 2][:, :],
                                               scalar=cst[:, bass.ds(e + C_B2, 1)], in1=gate_rows[b],
                                               op0=ALU.add, op1=ALU.mult).then_inc(yt_made, 1)

            def step(e, b, c, first):
                q = 2 * b + c
                dve.wait_ge(sil_made, e * 8 + (q + 1))
                dve.wait_ge(h2_done, e * 8 + (q + 1))
                if not (first and q < 2):
                    dve.wait_ge(lo_made, e * 8 + (q - 1))
                hidden(e, b, c)
                if not (first and q == 0):
                    pb, pc = ((b, 0) if c else ((b - 1) % NB, 1))
                    dve.wait_ge(hi_made, e * 8 + q)
                    low(pb, pc)
                if c == 1 and not (first and b == 0):
                    dve.wait_ge(y_done, e * 4 + b)
                    if b == 0:
                        dve.wait_ge(d_gate[NB - 1], e * 16)
                    else:
                        dve.wait_ge(d_gate[b - 1], e * 16 + 16)
                    if not (first and b < 3):
                        dve.wait_ge(acc_made, e * 4 + (b - 2))
                    gated(e - 1 if b == 0 else e, (b - 1) % NB)

            for b in range(NB):
                for c in range(HC):
                    step(0, b, c, True)
            with dve.Fori(1, E) as e:
                for b in range(NB):
                    for c in range(HC):
                        step(e, b, c, False)
            dve.wait_ge(hi_made, 8 * E)
            low(NB - 1, 1)
            dve.wait_ge(y_done, 4 * E)
            dve.wait_ge(d_gate[NB - 1], 16 * E)
            dve.wait_ge(acc_made, 4 * E - 2)
            gated(E - 1, NB - 1)

            for b in range(NB):
                src, free = full(("yT", b))
                if b >= 2:
                    dve.wait_ge(d_out[b % 2], 16 * (b // 2))
                nc.vector.scalar_tensor_tensor(out=fin[:, b % 2, :], in0=src[:, :], scalar=tanhg[:, 1:2],
                                               in1=xs[:, NT * b:NT * (b + 1), :].rearrange("p t d -> p (t d)"),
                                               op0=ALU.mult, op1=ALU.add).then_inc(fin_made, 1)

        @block.tensor
        def _(pe):
            def claim(key):
                i, m = MISC[key]
                if m >= 1:
                    pe.wait_ge(misc_free[i], m)
                return misc_bank[i], misc_full[i]

            def xhat_T(kind, n):
                l = ln_index(kind, n)
                dst, full = claim(("qT" if kind == 1 else "xT", n))
                pe.wait_ge(xhat_made, l + 1)
                for t in range(NT):
                    mm = nc.tensor.transpose(dst[:, t * P:(t + 1) * P], xhat[:, l % X_RING, t, :], ident[:, :])
                mm.then_inc(full, 1)
                return full

            def q_T(n):
                xhat_T(1, n)

            def q_features(n, half):
                dst, full = claim(("qA" if half == 0 else "qB", n))
                i, m = MISC[("qT", n)]
                pe.wait_ge(misc_free[i], m + 1)
                pe.wait_ge(bd_made, 1)
                nc.tensor.matmul(dst[:, :], bdz[:, half * P:(half + 1) * P], qT[:, :],
                                 start=True, stop=True).then_inc(full, 1)

            pe.wait_ge(ident_made, 1)
            q_T(0)
            dst, full = claim(("cT", 0))
            pe.wait_ge(d_ctx, 16 * (1 + NB))
            for n in range(NB):
                mm = nc.tensor.transpose(dst[:, n * P:(n + 1) * P], ctx_sb[:, n, :], ident[:, :])
            mm.then_inc(full, 1)
            dst, full = claim(("cT", 1))
            nc.tensor.transpose(dst[:, 0:P], ctx_rm, ident[:, :]).then_inc(full, 1)
            q_features(0, 0)
            q_features(0, 1)
            for k in range(2):
                i, m = MISC[("cT", k)]
                pe.wait_ge(misc_free[i], m + 1)
            ct = ctxT.rearrange("p n k -> p (n k)")
            W4 = NB * SP_ // 2
            for i in range(4):
                dst, full = claim(("zk", i))
                nc.tensor.matmul(dst[:, 0:W4], bdz[:, i // 2 * P:(i // 2 + 1) * P], ct[:, i % 2 * W4:(i % 2 + 1) * W4],
                                 start=True, stop=True).then_inc(full, 1)
            dst, full = claim(("v", 0))
            for n in range(NB):
                mm = nc.tensor.matmul(dst[:, n * P:(n + 1) * P], ctxT[:, n, 0:P], bd[:, :, 0, :],
                                      start=True, stop=True)
            mm.then_inc(full, 1)
            dst, full = claim(("v", 1))
            for n in range(NB):
                for j in range(GH):
                    mm = nc.tensor.matmul(dst[RP * j:RP * (j + 1), n * NG * HD:(n + 1) * NG * HD], ctxT[:, n, P:SP_],
                                          bd[:, j:H:GH, 0, :], start=True, stop=True)
            mm.then_inc(full, 1)
            q_T(1)
            q_features(1, 0)
            q_features(1, 1)

            def max_unit(m):
                n, i = divmod(m, MAXU)
                t, pair = divmod(i, H // 2)
                if m >= 2:
                    pe.wait_ge(max_read, m - 1)
                for j in range(2):
                    h = 2 * pair + j
                    mm = nc.tensor.matmul(mx_bank[m % 2][:, j * S:(j + 1) * S],
                                          qs[0:KROWS, n % 2, h, t * P:(t + 1) * P],
                                          ks[0:KROWS, h, n, 0:S], start=True, stop=True)
                mm.then_inc(max_done, 1)

            def max_T(n):
                dst, full = claim(("nm", n))
                pe.wait_ge(nm_made, n + 1)
                pe.wait_ge(ident16_made, 1)
                for t in range(NT):
                    mm = nc.tensor.transpose(dst[0:PARTS * H, :].bitcast(BF16)[:, t * P:(t + 1) * P],
                                             nm[:, t, :, :].rearrange("p c h -> p (c h)"), ident16[:, :])
                mm.then_inc(full, 1)

            pe.wait_ge(d_kin, 16 * len(K_TERMS))
            pe.wait_ge(d_qin[0], 16 * len(Q_TERMS))
            for m in range(MAXU):
                max_unit(m)
            max_T(0)
            pe.wait_ge(ones_made, 3)

            def scores(s, u):
                n, g = divmod(s, NG)
                k = UNITS * s + u
                if k >= S_RING:
                    pe.wait_ge(p_made, k - S_RING + 1)
                dst = s_bank[k % S_RING]
                if u < GH:
                    h = GH * g + u
                    mm = nc.tensor.matmul(dst[:, :], ks[0:SROWS, h, n, 0:P], qs[0:SROWS, n % 2, h, :],
                                          start=True, stop=True)
                else:
                    for j in range(GH):
                        h = GH * g + j
                        mm = nc.tensor.matmul(dst[RP * j:RP * (j + 1), :], ks[0:SROWS, h, n, P:SP_],
                                              qs[0:SROWS, n % 2, h, :], start=True, stop=True)
                mm.then_inc(s_done, 1)

            def weighted(s):
                n, g = divmod(s, NG)
                k = UNITS * s
                pe.wait_ge(p_made, k + UNITS)
                if s == 0:
                    pe.wait_ge(v_made, V_OPS)
                    pe.wait_ge(ones_made, 1)
                if s >= 1:
                    pe.wait_ge(o_made, s)
                nc.tensor.matmul(ot_bank[:, :], v_rm[:, n, g, :], prob[:, (k + GH) % P_RING, :],
                                 start=True, stop=False, skip_group_check=True)
                for j in range(GH):
                    mm = nc.tensor.matmul(ot_bank[RP * j:RP * (j + 1), :], v_sb[:, n, GH * g + j, :],
                                          prob[:, (k + j) % P_RING, :], start=False, stop=True,
                                          skip_group_check=True)
                mm.then_inc(pv_done, 1)

            def project(n):
                dst, full = claim(("fc", n))
                pe.wait_ge(on_made, NG * (n + 1))
                pe.wait_ge(d_fc, 16)
                for t in range(NT):
                    for g in range(NG):
                        nc.tensor.matmul(dst[:, t * P:(t + 1) * P], osum[:, n % 2, g, t * P:(t + 1) * P],
                                         fc_sb[:, g, :], start=(g == 0), stop=False)
                    mm = nc.tensor.matmul(dst[:, t * P:(t + 1) * P], one_row, fc_sb[0:1, NG, :],
                                          start=False, stop=True)
                mm.then_inc(full, 1)

            def logits(n):
                dst, full = claim(("lg", n))
                i, m = MISC[("xT", n)]
                pe.wait_ge(misc_free[i], m + 1)
                for t in range(NT):
                    mm = nc.tensor.matmul(dst[:, t * E_ROUTED:(t + 1) * E_ROUTED], x2T[:, t * P:(t + 1) * P],
                                          cst[:, C_WG:C_WG + E_ROUTED], start=True, stop=True)
                mm.then_inc(full, 1)

            def gates_T(n):
                dst, full = claim(("gT", n))
                pe.wait_ge(gts_made, n + 1)
                for t in range(NT):
                    mm = nc.tensor.transpose(dst[0:E, t * P:(t + 1) * P], gts[:, t, :], ident[:, :])
                mm.then_inc(full, 1)

            m = MAXU
            pe.wait_ge(d_nm, 16 * PARTS)
            for s in range(SLOTS):
                n, g = divmod(s, NG)
                if g == 0 and n >= 1:
                    pe.wait_ge(d_nm, 16 * PARTS * (n + 1))
                if g == 0 and n + 1 < NB:
                    pe.wait_ge(d_qin[(n + 1) % 2], 16 * len(Q_TERMS) * ((n + 1) // 2 + 1))

                def maxima(i):
                    nonlocal m
                    if n + 1 < NB:
                        for _ in range(MAX_AT[g][i]):
                            max_unit(m)
                            m += 1

                for u in range(3):
                    scores(s, u)
                    maxima(u)
                if g == 0 and n >= 2:
                    project(n - 2)
                if g == 1 and n >= 2:
                    xhat_T(2, n - 2)
                if g == 3 and n + 1 < NB:
                    max_T(n + 1)
                if s >= 1:
                    weighted(s - 1)
                maxima(3)
                scores(s, 3)
                maxima(4)
                scores(s, 4)
                maxima(5)
                if g == 0 and n + 2 < NB:
                    q_T(n + 2)
                if g == 1 and n + 2 < NB:
                    q_features(n + 2, 0)
                    q_features(n + 2, 1)
                if g == 1 and n >= 2:
                    logits(n - 2)
                if g == 3 and n >= 2:
                    gates_T(n - 2)
            weighted(SLOTS - 1)
            for n in (NB - 2, NB - 1):
                project(n)
                xhat_T(2, n)
                logits(n)
                gates_T(n)

            pe.wait_ge(wlo_made, 2 * E)
            pe.wait_ge(xh_made, NB)
            pe.wait_ge(p_made, UNITS * SLOTS)
            pe.wait_ge(o_made, SLOTS)

            def three(dst, w_col, e, x_hi, x_lo, start, stop):
                hi = w_hi[:, e, w_col:w_col + P]
                lo = w_lo[:, e, w_col:w_col + P]
                nc.tensor.matmul(dst, hi, x_hi, start=start, stop=False)
                nc.tensor.matmul(dst, hi, x_lo, start=False, stop=False)
                return nc.tensor.matmul(dst, lo, x_hi, start=False, stop=stop)

            def up(e, b, first):
                x_hi, x_lo = xh[:, b * T:(b + 1) * T], xl[:, b * T:(b + 1) * T]
                for c in range(HC):
                    q = 2 * b + c
                    if not (first and q < 2):
                        pe.wait_ge(hf_made, e * 8 + (q - 1))
                    three(h1_bank[c][:, :], c * P, e, x_hi, x_lo, True, True).then_inc(h1_done, 1)
                    three(h2_bank[c][:, :], HID + c * P, e, x_hi, x_lo, True, True).then_inc(h2_done, 1)

            def down(e, b, first):
                pe.wait_ge(lo_made, e * 8 + (2 * b + 1))
                if not (first and b < 2):
                    pe.wait_ge(yt_made, e * 4 + (b - 1))
                for c in range(HC):
                    if c:
                        pe.wait_ge(lo_made, e * 8 + (2 * b + 2))
                    mm = three(y_bank[b % 2][:, :], 2 * HID + c * P, e, hsp[:, 0, b % 2, c, :],
                               hsp[:, 1, b % 2, c, :], c == 0, c == HC - 1)
                mm.then_inc(y_done, 1)

            for b in range(NB):
                up(0, b, True)
                if b >= 1:
                    down(0, b - 1, True)
            with pe.Fori(1, E) as e:
                for b in range(NB):
                    up(e, b, False)
                    if b == 0:
                        down(e - 1, NB - 1, False)
                    else:
                        down(e, b - 1, False)
            down(E - 1, NB - 1, False)
            for b in range(NB):
                i, m = MISC[("yT", b)]
                dst, full = misc_bank[i], misc_full[i]
                if b < 2:
                    pe.wait_ge(misc_free[i], m)
                else:
                    pe.wait_ge(fin_made, b - 1)
                pe.wait_ge(acc_made, 4 * (E - 1) + b + 1)
                for t in range(NT):
                    mm = nc.tensor.transpose(dst[:, t * P:(t + 1) * P], acc[b][:, t * P:(t + 1) * P], ident[:, :])
                mm.then_inc(full, 1)


def kernel(x, ctx_1024, g_xattn, g_ffn, L0_xattn_fm_w, L0_xattn_fm_b, L0_xattn_fc_w, L0_xattn_fc_b,
           L0_ffn_Wg, L0_ffn_W1, L0_ffn_b1, L0_ffn_W11, L0_ffn_b11, L0_ffn_W2, L0_ffn_b2,
           L0_ffn_Ws1, L0_ffn_bs1, L0_ffn_Ws11, L0_ffn_bs11, L0_ffn_Ws2, L0_ffn_bs2):
    import numpy as np
    import concourse.bacc as bacc
    from concourse.bass_utils import run_bass_kernel_spmd

    f = lambda a: np.asarray(a)
    xin = np.ascontiguousarray(f(x).reshape(NB, NT, P, D).transpose(0, 2, 1, 3))

    const = np.zeros((P, C_END), np.float32)
    const[:, C_FM:C_FM + HD] = np.tile(f(L0_xattn_fm_w).T, (H, 1))
    rows = np.arange(P)
    const[:, C_MASK:C_MASK + H] = rows[:, None] // HD == np.arange(H)[None, :]
    const[:, C_SGN] = np.where(rows % FD < HD, 1.0, -1.0)
    const[:, C_FMB] = np.tile(f(L0_xattn_fm_b), P // HD)
    const[:, C_FMBV:C_FMBV + HD] = f(L0_xattn_fm_b)[None, :]
    const[:, C_WG:C_WG + E_ROUTED] = f(L0_ffn_Wg)
    const[:, C_GX] = f(g_xattn)
    const[:, C_GF] = f(g_ffn)
    const[:, C_IOTA:C_IOTA + E_ROUTED] = np.arange(E_ROUTED)[None, :]

    def chunks(shared, routed):
        a = np.concatenate([f(shared).reshape(2, HID), f(routed)])
        return a.reshape(E, HC, P).transpose(2, 0, 1).reshape(P, E * HC)

    const[:, C_B1:C_B11] = chunks(L0_ffn_bs1, L0_ffn_b1)
    const[:, C_B11:C_B2] = chunks(L0_ffn_bs11, L0_ffn_b11)
    const[:, C_B2] = f(L0_ffn_bs2)
    const[:, C_B2 + 2:C_END] = f(L0_ffn_b2).T

    fcw = np.zeros((P, NG + 1, D), np.float32)
    w = f(L0_xattn_fc_w).T.reshape(NG, GH, FD, D)
    for j in range(GH):
        fcw[2 * FD * j:2 * FD * j + FD, 0:NG] = w[:, j].transpose(1, 0, 2)
    fcw[0, NG] = f(L0_xattn_fc_b)

    def ups(shared, routed):
        return np.concatenate([f(shared).reshape(D, 2, HID).transpose(1, 0, 2), f(routed)])

    downs = np.concatenate([f(L0_ffn_Ws2).reshape(2, HID, D), f(L0_ffn_W2)])
    downs = downs.reshape(E, HC, P, D).transpose(0, 2, 1, 3).reshape(E, P, HC * D)
    wall = np.concatenate([ups(L0_ffn_Ws1, L0_ffn_W1), ups(L0_ffn_Ws11, L0_ffn_W11), downs], axis=2)

    arrays = {"x": xin, "ctx": f(ctx_1024), "const": const, "fcw": fcw, "wall": wall}
    nc = bacc.Bacc("TRN2", target_bir_lowering=False, num_devices=1)
    args = [nc.dram_tensor(f"in_{k}", a.shape, F32, kind="ExternalInput").ap() for k, a in arrays.items()]
    out = nc.dram_tensor("out", (NB, P, NT, D), F32, kind="ExternalOutput").ap()
    build(nc, *args, out)
    r = run_bass_kernel_spmd(nc, [{f"in_{k}": np.ascontiguousarray(a) for k, a in arrays.items()}], core_ids=[0])
    y = r.results[0]["out"]
    return y.transpose(0, 2, 1, 3).reshape(NB, T, D)
```

```python
from contextlib import ExitStack

import concourse.bass as bass
from concourse import mybir

F32, BF16, F16, U32 = mybir.dt.float32, mybir.dt.bfloat16, mybir.dt.float16, mybir.dt.uint32
ALU = mybir.AluOpType
ACT = mybir.ActivationFunctionType
AX_X = mybir.AxisListType.X

P = 128
NB, T, D = 4, 512, 128
NT = T // P
S = 154
SR = S - P
RP = 32
SP_ = P + RP
H, HD, FD = 16, 8, 16
NG, GH = 4, 4
PARTS = 3
Q_TERMS = (0, 0, 0, 1, 1, 2)
K_TERMS = (0, 1, 2, 0, 1, 0)
KROWS = len(Q_TERMS) * FD
SROWS = KROWS + PARTS
E_ROUTED, HID = 16, 256
E = E_ROUTED + 2
HC = HID // P
WCOLS = 3 * HID
TOK = NB * T
EPS = 1e-5
SCALE = float(D) ** -0.5

C_FM, C_MASK, C_SGN, C_FMB, C_FMBV, C_WG, C_GX, C_GF, C_IOTA = 0, 8, 24, 25, 26, 34, 50, 51, 52
C_B1 = 68
C_B11 = C_B1 + E * HC
C_B2 = C_B11 + E * HC
C_ID = C_B2 + E
C_END = C_ID + P

UNITS = 5
MAXU = NT * GH // 2
SLOTS = NB * NG
AHEAD = 2
S_RING, P_RING = 3, 8
K_ROUNDS = ((0, 1), (1, NB))
UNIT = [(e, b) for b in range(NB) for e in range(2)] + [(2, b) for b in range(NB)]
ZK_COLS = (2 * SP_, 3 * SP_, 3 * SP_)
W_RING = 2
WH = WCOLS // 2
X_RING = 2
V_OPS = 2 * NB + 2 * GH


def misc_order():
    out = [("cT", 0), ("cT", 1), ("zk", 0), ("qT", 0), ("qA", 0), ("qB", 0), ("zk", 1), ("zk", 2)]
    out += [("v", 0), ("v", 1), ("qT", 1), ("qA", 1), ("qB", 1), ("nm", 0)]
    out += [("nm", s) for s in range(1, AHEAD - 1)]
    for s in range(SLOTS):
        n, g = divmod(s, NG)
        old = n >= 2
        out += [("nm", s + AHEAD - 1)] * (s + AHEAD <= SLOTS)
        out += [(("fc", "xT", "lg", "gT")[g], n - 2)] * old
        if n + 2 < NB:
            out += {0: [("qT", n + 2)], 1: [("qA", n + 2), ("qB", n + 2)]}.get(g, [])
    out += [("fc", 2), ("xT", 2), ("lg", 2), ("fc", 3), ("gT", 2), ("xT", 3), ("lg", 3), ("gT", 3)]
    out += [("yT", b) for b in range(NB)]
    return {key: (i % 2, i // 2) for i, key in enumerate(out)}


MISC = misc_order()
LN = [(1, 0), (1, 1), (1, 2), (1, 3), (2, 0), (2, 1), (2, 2), (2, 3)]


def build(nc, x, ctx, const, fcw, wall, out):
    with ExitStack() as stack:
        def sb(name, shape, dt=F32):
            return stack.enter_context(nc.sbuf_tensor(name, shape, dt))

        def sem(name):
            return stack.enter_context(nc.semaphore(name))

        bank = [stack.enter_context(nc.psum_tensor(f"bank{i}", [P, 512], F32)) for i in range(8)]
        s_bank, ot_bank, mx_bank, misc_bank = bank[0:3], bank[3], bank[4:6], bank[6:8]
        h1_bank, h2_bank, y_bank = bank[0:2], bank[2:4], bank[4:6]

        k_scr = nc.dram_tensor("k_scr", [PARTS, 2, P, NB * SP_], BF16, kind="Internal").ap()
        q_scr = nc.dram_tensor("q_scr", [NB, PARTS, 2, P, T], BF16, kind="Internal").ap()
        dn_scr = nc.dram_tensor("dn_scr", [NB, 2, GH, NG, T], F32, kind="Internal").ap()
        g_scr = nc.dram_tensor("g_scr", [E_ROUTED, TOK], F32, kind="Internal").ap()

        cst = sb("cst", [P, C_END])
        ident = cst[:, C_ID:C_ID + P]
        ident16 = sb("ident16", [P, P], BF16)
        fc_sb = sb("fc_sb", [P, NG + 1, D])
        bd = sb("bd", [P, H, 2, HD])
        sgnb = sb("sgnb", [P, 1])
        b1 = sb("b1", [P, HC])
        tanhg = sb("tanhg", [P, 2])
        mhalf = sb("mhalf", [P, NT])
        xs = sb("xs", [P, NB * NT, D])
        xhat = sb("xhat", [P, X_RING, NT, D])
        stats = sb("stats", [P, len(LN), NT, 6])
        mv = sb("mv", [P, len(LN), NT, 2])
        veps = sb("veps", [P, len(LN), NT])
        rstd = sb("rstd", [P, len(LN), NT])
        arena = sb("arena", [P, 2 * H * T // 2])
        qs = arena[:, :].bitcast(BF16).rearrange("p (b h t) -> p b h t", b=2, h=H)
        ctx_sb = arena[:, 4608:5120].rearrange("p (n d) -> p n d", n=NB)
        ctx_rm = arena[:, 5120:5248]
        ctxT = arena[:, 5248:5248 + NB * SP_].rearrange("p (n k) -> p n k", n=NB)
        v_tmp = arena[:, 6016:6528]
        v_tmr = arena[:, 6528:7040]
        gate_rows = [arena[:, b * T:(b + 1) * T] for b in range(NB)]
        acc = [arena[:, (4 + b) * T:(5 + b) * T] for b in range(NB)]
        sil = [arena[:, (8 + c) * T:(9 + c) * T] for c in range(HC)]
        hf = [arena[:, (10 + c) * T:(11 + c) * T] for c in range(HC)]
        hsp = arena[:, 12 * T:16 * T].bitcast(F16).rearrange("p (l b c t) -> p l b c t", l=2, b=2, c=HC)
        ks = sb("ks", [P, H, NB, SP_], BF16)
        v_sb = sb("v_sb", [P, NB, H, 2 * FD])
        one_row = v_sb[0:1, 0, 0, FD:FD + 1].to_broadcast([1, P])
        v_rm = sb("v_rm", [P, NB, NG, P])
        qT = sb("qT", [P, T])
        f_q = sb("f_q", [P, 2, T])
        qp = sb("qp", [P, PARTS, 2 * T], BF16)
        mx = sb("mx", [P, NT, GH])
        nm_r = sb("nm_r", [P, NT, GH])
        nm = sb("nm", [P, NT, PARTS, GH], BF16)
        nmT = sb("nmT", [PARTS * GH, T], BF16)
        prob = sb("prob", [P, P_RING, T])
        osum = sb("osum", [P, 2, NG, T])
        flat = osum[:, :, :, :].rearrange("p b g t -> p (b g t)")
        f_k, kp = [], []
        at = 0
        for n0, n1 in K_ROUNDS:
            w = 2 * (n1 - n0) * SP_
            f_k.append(flat[:, at:at + w])
            kp.append(flat[:, at + w:at + w + PARTS * w // 2].bitcast(BF16).rearrange("p (c k) -> p c k", c=PARTS))
            at += w + PARTS * w // 2
        dn = sb("dn", [P, 2, NG * GH * T // P])
        den = sb("den", [P, 2, T])
        x2T = sb("x2T", [P, T])
        xh = sb("xh", [P, TOK], F16)
        xl = sb("xl", [P, TOK], F16)
        lg = sb("lg", [P, NT, E_ROUTED])
        top = sb("top", [P, NT, 8])
        idx = sb("idx", [P, NT, 8], U32)
        idf = sb("idf", [P, NT, 8])
        oh = sb("oh", [P, 3, NT, E_ROUTED])
        gex = sb("gex", [P, NT, E_ROUTED])
        gsum = sb("gsum", [P, 2, NT])
        gts = sb("gts", [P, NT, E_ROUTED])
        gT = x2T[0:E_ROUTED, :]
        w_st = sb("w_st", [P, W_RING, WH])
        w_hi = sb("w_hi", [P, E, WCOLS], F16)
        w_lo = sb("w_lo", [P, E, WCOLS], F16)
        yt = f_q
        fin = prob[:, 0:2, :]

        bdz = bd[:, :, :, :].rearrange("p h s e -> p (h s e)")

        d_const, d_fc, d_ctx = sem("d_const"), sem("d_fc"), sem("d_ctx")
        d_x = [sem(f"d_x{n}") for n in range(NB)]
        d_w = [sem(f"d_w{i}") for i in range(W_RING)]
        d_ones, d_nm = sem("d_ones"), sem("d_nm")
        d_kout, d_kin = ([sem(f"d_{k}{i}") for i in range(2)] for k in ("kout", "kin"))
        d_qout = [sem(f"d_qout{i}") for i in range(2)]
        d_qin = [[sem(f"d_qin{i}{a}") for a in range(2)] for i in range(2)]
        d_gout = [sem(f"d_gout{b}") for b in range(NB)]
        d_gate = [sem(f"d_gate{b}") for b in range(NB)]
        d_out = [sem(f"d_out{i}") for i in range(2)]
        z_rem, ones_made, ones_row, half_made = (sem(k) for k in ("z_rem", "ones_made", "ones_row", "half_made"))
        bd_made, sgnb_made, tanh_made, ident16_made = (sem(k) for k in ("bd_made", "sgnb_made", "tanh_made", "ident16_made"))
        fk_made, kp_made, vz_made, v_made = (sem(k) for k in ("fk_made", "kp_made", "vz_made", "v_made"))
        misc_full = [sem(f"misc_full{i}") for i in range(2)]
        misc_free = [sem(f"misc_free{i}") for i in range(2)]
        var_made, rstd_made, xhat_made = (sem(k) for k in ("var_made", "rstd_made", "xhat_made"))
        qr_made, qp1_made = sem("qr_made"), sem("qp1_made")
        qp_made, max_done, max_read, nm_made = (sem(k) for k in ("qp_made", "max_done", "max_read", "nm_made"))
        s_done, p_made, pv_done, o_made, den_made, on_made, rec_made = (
            sem(k) for k in ("s_done", "p_made", "pv_done", "o_made", "den_made", "on_made", "rec_made"))
        d_dn = [sem(f"d_dn{i}") for i in range(4)]
        xh_made, lgm_made, gex_made, gts_made = (sem(k) for k in ("xh_made", "lgm_made", "gex_made", "gts_made"))
        whi_made, wlo_made = sem("whi_made"), sem("wlo_made")
        h1_done, h2_done, sil_made, hf_made, hi_made, lo_made = (
            sem(k) for k in ("h1_done", "h2_done", "sil_made", "hf_made", "hi_made", "lo_made"))
        bias_made = sem("bias_made")
        y_done, yt_made, acc_made, fin_made = (sem(k) for k in ("y_done", "yt_made", "acc_made", "fin_made"))
        v_chain, g_chain = sem("v_chain"), sem("g_chain")

        block = stack.enter_context(nc.Block())

        def den_tile(n, g):
            return den[:, g % 2, :] if n + 1 < NB else prob[:, 4 + g, :]

        def ln_index(kind, n):
            return LN.index((kind, n))

        @block.sync
        def _(sp):
            sp.dma_start(cst[:, :], const).then_inc(d_const, 16)
            sp.dma_start(xs[:, 0:NT, :], x[0]).then_inc(d_x[0], 16)
            sp.wait_ge(z_rem, 1)
            for n in range(NB):
                sp.dma_start(ctx_rm[RP * n:RP * n + SR, :], ctx[n, P:S, :]).then_inc(d_ctx, 16)
            sp.wait_ge(ones_row, 1)
            w = H * NB * SP_ // RP
            for c in range(PARTS):
                sp.dma_start(ks[KROWS + c:KROWS + c + 1, :, :, :].rearrange("c h n k -> c (h n k)")
                             .rearrange("c (a b) -> c a b", b=w), qp[RP * c:RP * (c + 1), 2, 0:w]).then_inc(d_ones, 16)
            for n in range(1, NB):
                sp.dma_start(xs[:, NT * n:NT * (n + 1), :], x[n]).then_inc(d_x[n], 16)

            def keys_out(r):
                sp.wait_ge(kp_made, r + 1)
                n0, n1 = K_ROUNDS[r]
                for c in range(PARTS):
                    sp.dma_start(k_scr[c, :, :, n0 * SP_:n1 * SP_].rearrange("a p k -> p a k"),
                                 kp[r][:, c, :].rearrange("p (a k) -> p a k", a=2)).then_inc(d_kout[r], 16)

            def keys_in(r):
                sp.wait_ge(d_kout[r], 16 * PARTS)
                n0, n1 = K_ROUNDS[r]
                for i, c in enumerate(K_TERMS):
                    sp.dma_start(ks[FD * i:FD * (i + 1), :, n0:n1, :].rearrange("f h n k -> f h (n k)"),
                                 k_scr[c, :, :, n0 * SP_:n1 * SP_].rearrange("a (h f) k -> f (a h) k", f=FD))\
                        .then_inc(d_kin[r], 16)

            def queries_out(n, a):
                sp.wait_ge(qp_made, 2 * n + a + 1)
                sp.dma_start(q_scr[n, :, a].rearrange("c p t -> p c t"), qp[:, :, a * T:(a + 1) * T])\
                    .then_inc(d_qout[a], 16)

            def queries_in(n, a):
                sp.wait_ge(d_qout[a], 16 * (n + 1))
                if n >= 2:
                    sp.wait_ge(s_done, UNITS * (NG * (n - 2) + (a + 1) * NG // 2))
                if n == 1:
                    sp.wait_ge(v_made, V_OPS)
                for i, c in enumerate(Q_TERMS):
                    sp.dma_start(qs[FD * i:FD * (i + 1), n % 2, a * H // 2:(a + 1) * H // 2, :],
                                 q_scr[n, c, a].rearrange("(h f) t -> f h t", f=FD)).then_inc(d_qin[n % 2][a], 16)

            def move_denominators(n):
                rows = osum[FD:P:2 * FD, n % 2, :, :]
                spread = dn_scr[n].rearrange("i j g t -> i (j g t)").rearrange("i (p k) -> i p k", p=P)
                sp.wait_ge(o_made, NG * (n + 1))
                sp.dma_start(dn_scr[n, 0], rows).then_inc(d_dn[0], 16)
                sp.wait_ge(d_dn[0], 16 * (n + 1))
                sp.dma_start(dn[:, 0, :], spread[0]).then_inc(d_dn[1], 16)
                sp.wait_ge(rec_made, n + 1)
                sp.dma_start(spread[1], dn[:, 1, :]).then_inc(d_dn[2], 16)
                sp.wait_ge(d_dn[2], 16 * (n + 1))
                sp.dma_start(rows, dn_scr[n, 1]).then_inc(d_dn[3], 16)

            keys_out(0)
            keys_in(0)
            queries_out(0, 0)
            queries_in(0, 0)
            queries_out(0, 1)
            queries_in(0, 1)
            keys_out(1)
            keys_in(1)
            sp.dma_start(fc_sb[:, :, :], fcw).then_inc(d_fc, 16)
            for n in range(1, NB):
                for a in range(2):
                    queries_out(n, a)
                for a in range(2):
                    queries_in(n, a)
                if n >= 2:
                    move_denominators(n - 2)
            for n in range(NB - 2, NB):
                move_denominators(n)

            sp.wait_ge(s_done, UNITS * SLOTS)
            for b in range(NB):
                sp.wait_ge(d_gout[b], 16)
                sp.dma_start(gate_rows[b], g_scr[0:1, b * T:(b + 1) * T].to_broadcast([P, T])).then_inc(d_gate[b], 16)
            with sp.Fori(3, E) as e:
                for b in range(NB):
                    sp.wait_ge(yt_made, e * NB + (b + 1 - NB))
                    sp.dma_start(gate_rows[b],
                                 g_scr[bass.ds(e - 2, 1), b * T:(b + 1) * T].to_broadcast([P, T])).then_inc(d_gate[b], 16)
            for b in range(NB):
                sp.wait_ge(fin_made, b + 1)
                sp.dma_start(out[b], fin[:, b % 2, :].rearrange("p (t d) -> p t d", t=NT)).then_inc(d_out[b % 2], 16)
            for i in range(2):
                sp.wait_ge(d_out[i], 16 * NB // 2)

        @block.gpsimd
        def _(pool):
            nc.gpsimd.memset(mhalf[:, :], -0.5).then_inc(half_made, 1)
            nc.gpsimd.memset(qp[:, 2, 0:H * NB * SP_ // RP], 1.0).then_inc(ones_row, 1)
            nc.gpsimd.memset(v_sb[:, :, :, FD:2 * FD], 1.0).then_inc(ones_made, 1)

            def rsqrt(kind, n):
                l = ln_index(kind, n)
                pool.wait_ge(var_made, l + 1)
                nc.gpsimd.tensor_tensor(rstd[:, l, :], veps[:, l, :], mhalf[:, :], ALU.pow).then_inc(rstd_made, 1)

            def weights_low(e):
                for i in (2 * e, 2 * e + 1):
                    pool.wait_ge(whi_made, i + 1)
                    cols = slice(i % 2 * WH, (i % 2 + 1) * WH)
                    nc.gpsimd.tensor_tensor(w_lo[:, e, cols], w_st[:, i % W_RING, :], w_hi[:, e, cols],
                                            ALU.subtract).then_inc(wlo_made, 1)

            pool.wait_ge(half_made, 1)
            rsqrt(1, 0)

            def rest_q(n, a):
                i, m = MISC[("qB" if a else "qA", n)]
                pool.wait_ge(misc_free[i], m + 1)
                nc.gpsimd.tensor_tensor(f_q[:, a, :], f_q[:, a, :], qp[:, 0, a * T:(a + 1) * T],
                                        ALU.subtract).then_inc(qr_made, 1)

            def third_q(n, a):
                pool.wait_ge(qp1_made, 2 * n + a - 1)
                nc.gpsimd.tensor_tensor(qp[:, 2, a * T:(a + 1) * T], f_q[:, a, :], qp[:, 1, a * T:(a + 1) * T],
                                        ALU.subtract).then_inc(qp_made, 1)

            weights_low(0)
            weights_low(1)
            rsqrt(1, 1)
            rest_q(1, 0)
            rest_q(1, 1)
            third_q(1, 0)
            third_q(1, 1)
            rsqrt(1, 2)

            def normalise(n):
                for g in range(NG):
                    k = NG * n + g
                    pool.wait_ge(den_made, k + 1)
                    rows = osum[:, n % 2, g, :]
                    nc.gpsimd.tensor_tensor(rows, rows, den_tile(n, g), ALU.mult).then_inc(on_made, 1)

            for s in range(SLOTS):
                n, g = divmod(s, NG)
                if g == 2 and n + 2 < NB:
                    rest_q(n + 2, 0)
                    rest_q(n + 2, 1)
                if g == 3 and n + 2 < NB:
                    third_q(n + 2, 0)
                    third_q(n + 2, 1)
                if g == 3 and n + 3 < NB:
                    rsqrt(1, n + 3)
                weights_low(s + 2)
                if g == 0 and n >= 2:
                    rsqrt(2, n - 2)
                if g == 3 and n >= 1:
                    normalise(n - 1)

            pool.wait_ge(s_done, UNITS * SLOTS)
            rsqrt(2, 2)
            for b in range(NB):
                nc.gpsimd.memset(acc[b], 0.0).then_inc(g_chain, 1)
            pool.wait_ge(g_chain, NB)

            def add(b, ring, made, before):
                pool.wait_ge(yt_made, made)
                if before is not None:
                    pool.wait_ge(acc_made, before)
                nc.gpsimd.tensor_tensor(acc[b], acc[b], yt[:, ring, :], ALU.add).then_inc(acc_made, 1)

            for u, (e, b) in enumerate(UNIT):
                if u == 2:
                    normalise(3)
                if u == 3:
                    rsqrt(2, 3)
                earlier = [i + 1 for i in range(u) if UNIT[i][1] == b]
                add(b, u % 2, u + 1, earlier[-1] if earlier else None)
            with pool.Fori(3, E) as e:
                for b in range(NB):
                    add(b, b % 2, e * NB + (b + 1), e * NB + (b + 1 - NB))

        @block.scalar
        def _(act):
            def full(key):
                i, m = MISC[key]
                act.wait_ge(misc_full[i], m + 1)
                return misc_bank[i], misc_free[i]

            def load_weights(i):
                if i >= W_RING:
                    act.wait_ge(wlo_made, i - W_RING + 1)
                act.dma_start(w_st[:, i % W_RING, :], wall[i // 2, :, i % 2 * WH:(i % 2 + 1) * WH])\
                    .then_inc(d_w[i % W_RING], 16)

            def weights_high(i):
                act.wait_ge(d_w[i % W_RING], 16 * (i // W_RING + 1))
                nc.scalar.activation(w_hi[:, i // 2, i % 2 * WH:(i % 2 + 1) * WH], w_st[:, i % W_RING, :],
                                     ACT.Copy).then_inc(whi_made, 1)
                if i >= 1 and i + 1 < 2 * E:
                    load_weights(i + 1)

            act.dma_start(ctx_sb, ctx[:, 0:P, :].rearrange("n k d -> k n d")).then_inc(d_ctx, 16)
            load_weights(0)
            load_weights(1)

            act.wait_ge(d_const, 16)
            nc.scalar.activation(tanhg[:, :], cst[:, C_GX:C_GX + 2], ACT.Tanh).then_inc(tanh_made, 1)

            def copy_qT(n):
                src, free = full(("qT", n))
                if n >= 1:
                    i, m = MISC[("qB", n - 1)]
                    act.wait_ge(misc_full[i], m + 1)
                nc.scalar.activation(qT[:, :], src[:, :], ACT.Copy).then_inc(free, 1)

            def features(dst, src):
                return nc.scalar.activation(dst, src, ACT.Exp, bias=sgnb[:, :], scale=cst[:, C_SGN:C_SGN + 1])

            def exp_q(n, half):
                if n >= 1:
                    act.wait_ge(qp_made, 2 * n + half - 1)
                    act.wait_ge(d_qout[half], 16 * n)
                src, free = full(("qA" if half == 0 else "qB", n))
                features(f_q[:, half, :], src[:, :])
                features(qp[:, 0, half * T:(half + 1) * T], src[:, :]).then_inc(free, 1)

            def exp_k(r, lo, i):
                w = ZK_COLS[i]
                src, free = full(("zk", i))
                features(f_k[r][:, lo:lo + w], src[:, 0:w])
                features(kp[r][:, 0, lo:lo + w], src[:, 0:w]).then_inc(free, 1)

            weights_high(0)
            weights_high(1)
            src, free = full(("cT", 0))
            nc.scalar.activation(ctxT[:, :, 0:P], src[:, :].rearrange("p (n k) -> p n k", n=NB),
                                 ACT.Copy).then_inc(free, 1)
            src, free = full(("cT", 1))
            nc.scalar.activation(ctxT[:, :, P:SP_], src[:, 0:P].rearrange("p (n k) -> p n k", n=NB),
                                 ACT.Copy).then_inc(free, 1)
            act.wait_ge(sgnb_made, 1)
            exp_k(0, 0, 0)
            copy_qT(0)
            exp_q(0, 0)
            exp_q(0, 1)
            weights_high(2)
            exp_k(1, 0, 1)
            exp_k(1, ZK_COLS[1], 2)
            weights_high(3)
            copy_qT(1)
            i, m = MISC[("v", 0)]
            act.wait_ge(misc_free[i], m + 1)
            act.wait_ge(ones_made, 1)
            z = v_tmp.rearrange("p (n h e) -> p n h e", n=NB, h=H)
            for k, sg in enumerate((1.0, -1.0)):
                for n in range(NB):
                    ins = nc.scalar.activation(v_sb[:, n, :, k * HD:(k + 1) * HD], z[:, n, :, :], ACT.Exp, scale=sg)
                    ins.then_inc(v_made, 1)
            i, m = MISC[("v", 1)]
            act.wait_ge(misc_free[i], m + 1)
            act.wait_ge(vz_made, 1)
            z = v_tmr[:, 0:NB * NG * HD].rearrange("p (n g e) -> p n g e", n=NB, g=NG)
            for j in range(GH):
                for k, sg in enumerate((1.0, -1.0)):
                    rows = slice(RP * j, RP * j + SR)
                    nc.scalar.activation(v_rm[rows, :, :, RP * j + k * HD:RP * j + (k + 1) * HD],
                                         z[rows, :, :, :], ACT.Exp, scale=sg).then_inc(v_made, 1)
            exp_q(1, 0)
            exp_q(1, 1)

            def move_max(s):
                n, g = divmod(s, NG)
                src, free = full(("nm", s))
                if s >= 1:
                    act.wait_ge(d_nm, 16 * s)
                nc.scalar.activation(nmT[:, :], src[0:PARTS * GH, :].bitcast(BF16)[:, 0:T], ACT.Copy)\
                    .then_inc(free, 1)
                act.wait_ge(free, MISC[("nm", s)][1] + 1)
                act.dma_start(qs[KROWS:SROWS, n % 2, GH * g:GH * (g + 1), :], nmT[:, :]).then_inc(d_nm, 16)

            move_max(0)
            for s in range(1, AHEAD - 1):
                move_max(s)

            def probs(s, u):
                k = UNITS * s + u
                act.wait_ge(s_done, k + 1)
                if k >= P_RING:
                    act.wait_ge(pv_done, (k - P_RING) // UNITS + 1)
                nc.scalar.activation(prob[:, k % P_RING, :], s_bank[k % S_RING][:, :], ACT.Exp,
                                     scale=SCALE).then_inc(p_made, 1)

            def copy_out(s):
                act.wait_ge(pv_done, s + 1)
                n, g = divmod(s, NG)
                if s == 0:
                    for i in range(2):
                        act.wait_ge(d_kout[i], 16 * PARTS)
                if n >= 2:
                    i, m = MISC[("fc", n - 2)]
                    act.wait_ge(misc_full[i], m + 1)
                nc.scalar.activation(osum[:, n % 2, g, :], ot_bank[:, :], ACT.Copy).then_inc(o_made, 1)

            def copy_x2T(n):
                src, free = full(("xT", n))
                if n >= 1:
                    i, m = MISC[("lg", n - 1)]
                    act.wait_ge(misc_full[i], m + 1)
                    act.wait_ge(xh_made, n)
                    act.wait_ge(d_gout[n - 1], 16)
                nc.scalar.activation(x2T[:, :], src[:, :], ACT.Copy).then_inc(free, 1)

            def exp_gates(n):
                act.wait_ge(lgm_made, n + 1)
                nc.scalar.activation(gex[:, :, :], lg[:, :, :], ACT.Exp).then_inc(gex_made, 1)

            def move_gates(n):
                src, free = full(("gT", n))
                act.wait_ge(xh_made, n + 1)
                nc.scalar.activation(gT[:, :], src[0:E_ROUTED, :], ACT.Copy).then_inc(free, 1)
                act.wait_ge(free, MISC[("gT", n)][1] + 1)
                act.dma_start(g_scr[:, n * T:(n + 1) * T], gT[:, :]).then_inc(d_gout[n], 16)

            for s in range(SLOTS):
                n, g = divmod(s, NG)
                probs(s, 0)
                probs(s, 1)
                if s + AHEAD <= SLOTS:
                    move_max(s + AHEAD - 1)
                probs(s, 2)
                weights_high(2 * s + 4)
                probs(s, 3)
                if s >= 1:
                    copy_out(s - 1)
                probs(s, 4)
                if g == 0 and n + 2 < NB:
                    copy_qT(n + 2)
                if g == 1 and n + 2 < NB:
                    exp_q(n + 2, 0)
                    exp_q(n + 2, 1)
                if g == 1 and n >= 2:
                    copy_x2T(n - 2)
                if g == 3 and n >= 2:
                    exp_gates(n - 2)
                weights_high(2 * s + 5)
                if g == 3 and n >= 2:
                    move_gates(n - 2)
            copy_out(SLOTS - 1)

            act.wait_ge(s_done, UNITS * SLOTS)

            def silu(c, bias):
                nc.scalar.activation(sil[c], h1_bank[c][:, :], ACT.Silu, bias=bias).then_inc(sil_made, 1)

            def high(ring, c):
                nc.scalar.activation(hsp[:, 0, ring, c, :], hf[c], ACT.Copy).then_inc(hi_made, 1)

            for u, (e, b) in enumerate(UNIT):
                for c in range(HC):
                    k = HC * u + c
                    act.wait_ge(h1_done, k + 1)
                    if k >= 2:
                        act.wait_ge(hf_made, k - 1)
                    at = C_B1 + HC * e + c
                    silu(c, cst[:, at:at + 1])
                    if k >= 1:
                        act.wait_ge(hf_made, k)
                        high((k - 1) // HC % 2, (k - 1) % HC)
                if u == 1:
                    copy_x2T(2)
                if u == 3:
                    exp_gates(2)
                if u == 4:
                    move_gates(2)
                if u == 5:
                    copy_x2T(3)
                if u == 7:
                    exp_gates(3)
                if u == 8:
                    move_gates(3)
            with act.Fori(3, E) as e:
                act.wait_ge(sil_made, e * 8)
                nc.scalar.activation(b1[:, :], cst[:, bass.ds(e * HC + C_B1, HC)], ACT.Copy).then_inc(bias_made, 1)
                act.wait_ge(bias_made, e - 2)
                for k in range(HC * NB):
                    b, c = divmod(k, HC)
                    act.wait_ge(h1_done, e * 8 + (k + 1))
                    act.wait_ge(hf_made, e * 8 + (k - 1))
                    silu(c, b1[:, c:c + 1])
                    act.wait_ge(hf_made, e * 8 + k)
                    high((b + 1) % 2 if c == 0 else b % 2, 1 - c)
            act.wait_ge(hf_made, 8 * E)
            high(1, 1)

        @block.vector
        def _(dve):
            chain = [0]

            def link(ins):
                chain[0] += 1
                ins.then_inc(v_chain, 1)
                dve.wait_ge(v_chain, chain[0])

            def full(key):
                i, m = MISC[key]
                dve.wait_ge(misc_full[i], m + 1)
                return misc_bank[i], misc_free[i]

            def layer_norm(kind, n):
                moments(kind, n)
                scale_rows(kind, n)

            def moments(kind, n):
                l = ln_index(kind, n)
                if kind == 1:
                    dve.wait_ge(d_x[n], 16)
                for t in range(NT):
                    ins = nc.vector.bn_stats(stats[:, l, t, :], xs[:, NT * n + t, :])
                link(ins)
                for t in range(NT):
                    ins = nc.vector.bn_aggr(mv[:, l, t, :], stats[:, l, t, :])
                link(ins)
                nc.vector.tensor_scalar(veps[:, l, :], mv[:, l, :, 1], EPS, None, ALU.add).then_inc(var_made, 1)

            def scale_rows(kind, n):
                l = ln_index(kind, n)
                dve.wait_ge(rstd_made, l + 1)
                if l >= X_RING:
                    kind_, n_ = LN[l - X_RING]
                    i, m = MISC[("qT" if kind_ == 1 else "xT", n_)]
                    dve.wait_ge(misc_full[i], m + 1)
                for t in range(NT):
                    ins = nc.vector.tensor_scalar(xhat[:, l % X_RING, t, :], xs[:, NT * n + t, :], mv[:, l, t, 0:1],
                                                  rstd[:, l, t:t + 1], ALU.subtract, ALU.mult)
                ins.then_inc(xhat_made, 1)

            def split_rest(src, parts):
                link(nc.vector.tensor_tensor(src, src, parts[0], ALU.subtract))
                link(nc.vector.tensor_copy(parts[1], src))
                return nc.vector.tensor_tensor(parts[2], src, parts[1], ALU.subtract)

            def first_queries(half):
                i, m = MISC[("qB" if half else "qA", 0)]
                dve.wait_ge(misc_free[i], m + 1)
                dve.wait_ge(d_ones, 16 * PARTS)
                split_rest(f_q[:, half, :], [qp[:, c, half * T:(half + 1) * T] for c in range(PARTS)])\
                    .then_inc(qp_made, 1)

            def second_part(n):
                for half in range(2):
                    dve.wait_ge(qr_made, 2 * n + half - 1)
                    nc.vector.tensor_copy(qp[:, 1, half * T:(half + 1) * T], f_q[:, half, :]).then_inc(qp1_made, 1)

            def split_keys(r):
                for i in ((0,), (1, 2))[r]:
                    b, m = MISC[("zk", i)]
                    dve.wait_ge(misc_free[b], m + 1)
                link(split_rest(f_k[r], [kp[r][:, c, :] for c in range(PARTS)]))
                n0, n1 = K_ROUNDS[r]
                pad = kp[r].rearrange("p c (m k) -> p c m k", k=SP_)[:, :, :, S:SP_]
                nc.vector.memset(pad, 0.0).then_inc(kp_made, 1)

            nc.vector.memset(ctx_rm, 0.0).then_inc(z_rem, 1)
            link(nc.vector.memset(v_rm[:, :, :, :], 0.0))
            for j in range(GH):
                ins = nc.vector.memset(v_rm[RP * j:RP * j + SR, :, :, RP * j + FD:RP * (j + 1)], 1.0)
            ins.then_inc(vz_made, 1)
            dve.wait_ge(d_const, 16)
            nc.vector.tensor_tensor(bd[:, :, :, :].rearrange("p h s e -> p h s e"),
                                    cst[:, C_MASK:C_MASK + H].rearrange("p (h s e) -> p h s e", s=1, e=1)
                                    .to_broadcast([P, H, 2, HD]),
                                    cst[:, C_FM:C_FM + HD].rearrange("p (h s e) -> p h s e", h=1, s=1)
                                    .to_broadcast([P, H, 2, HD]), ALU.mult).then_inc(bd_made, 1)
            nc.vector.tensor_tensor(sgnb[:, :], cst[:, C_FMB:C_FMB + 1], cst[:, C_SGN:C_SGN + 1],
                                    ALU.mult).then_inc(sgnb_made, 1)
            nc.vector.tensor_copy(ident16[:, :], ident).then_inc(ident16_made, 1)
            layer_norm(1, 0)
            split_keys(0)
            first_queries(0)
            first_queries(1)
            src, free = full(("v", 0))
            vb = cst[:, C_FMBV:C_FMBV + HD].rearrange("p (m e) -> p m e", m=1).to_broadcast([P, NB * H, HD])
            nc.vector.tensor_tensor(v_tmp.rearrange("p (m e) -> p m e", e=HD),
                                    src[:, :].rearrange("p (m e) -> p m e", e=HD), vb, ALU.add)\
                .then_inc(free, 1)
            src, free = full(("v", 1))
            vb = cst[:, C_FMBV:C_FMBV + HD].rearrange("p (m e) -> p m e", m=1).to_broadcast([P, NB * NG, HD])
            nc.vector.tensor_tensor(v_tmr[:, 0:NB * NG * HD].rearrange("p (m e) -> p m e", e=HD),
                                    src[:, 0:NB * NG * HD].rearrange("p (m e) -> p m e", e=HD), vb, ALU.add)\
                .then_inc(free, 1)

            layer_norm(1, 1)
            split_keys(1)

            def row_max(m):
                t, pair = divmod(m % MAXU, GH // 2)
                dve.wait_ge(max_done, m + 1)
                nc.vector.reduce_max(mx[:, t, 2 * pair:2 * pair + 2],
                                     mx_bank[m % 2][:, 0:2 * S].rearrange("p (h k) -> p h k", h=2), AX_X)\
                    .then_inc(max_read, 1)

            def split_max(s):
                dve.wait_ge(max_read, MAXU * (s + 1))
                if s >= 1:
                    i, m = MISC[("nm", s - 1)]
                    dve.wait_ge(misc_full[i], m + 1)
                link(nc.vector.tensor_scalar(nm[:, :, 0, :], mx[:, :, :], -1.0, None, ALU.mult))
                link(nc.vector.scalar_tensor_tensor(out=nm_r[:, :, :], in0=mx[:, :, :], scalar=-1.0,
                                                    in1=nm[:, :, 0, :], op0=ALU.mult, op1=ALU.subtract))
                link(nc.vector.tensor_copy(nm[:, :, 1, :], nm_r[:, :, :]))
                nc.vector.tensor_tensor(nm[:, :, 2, :], nm_r[:, :, :], nm[:, :, 1, :],
                                        ALU.subtract).then_inc(nm_made, 1)

            def maxima(s, half):
                for m in range(MAXU * s + MAXU * half // 2, MAXU * s + MAXU * (half + 1) // 2):
                    row_max(m)
                if half == 1:
                    split_max(s)

            for s in range(AHEAD):
                maxima(s, 0)
                maxima(s, 1)
            second_part(1)
            moments(1, 2)

            def reciprocals(n):
                dve.wait_ge(d_dn[1], 16 * (n + 1))
                if n >= 1:
                    dve.wait_ge(d_dn[2], 16 * n)
                nc.vector.reciprocal(dn[:, 1, :], dn[:, 0, :]).then_inc(rec_made, 1)

            def spread(n, groups):
                dve.wait_ge(d_dn[3], 16 * (n + 1))
                for g in groups:
                    k = NG * n + g
                    if n + 1 == NB:
                        dve.wait_ge(pv_done, SLOTS)
                    elif k >= 2:
                        dve.wait_ge(on_made, k - 1)
                    nc.vector.stream_shuffle(den_tile(n, g), osum[:, n % 2, g, :],
                                             [FD] * (2 * FD)).then_inc(den_made, 1)

            def add_attention(n):
                src, free = full(("fc", n))
                dve.wait_ge(tanh_made, 1)
                rows = xs[:, NT * n:NT * (n + 1), :].rearrange("p t d -> p (t d)")
                ins = nc.vector.scalar_tensor_tensor(out=rows, in0=src[:, :], scalar=tanhg[:, 0:1], in1=rows,
                                                     op0=ALU.mult, op1=ALU.add)
                ins.then_inc(free, 1)
                dve.wait_ge(free, MISC[("fc", n)][1] + 1)

            def split_x2(n):
                i, m = MISC[("xT", n)]
                dve.wait_ge(misc_free[i], m + 1)
                cols = slice(n * T, (n + 1) * T)
                link(nc.vector.tensor_copy(xh[:, cols], x2T[:, :]))
                nc.vector.tensor_tensor(xl[:, cols], x2T[:, :], xh[:, cols], ALU.subtract).then_inc(xh_made, 1)

            def route(n):
                src, free = full(("lg", n))
                if n >= 1:
                    dve.wait_ge(gex_made, n)
                nc.vector.tensor_copy(lg[:, :, :], src[:, 0:NT * E_ROUTED].rearrange("p (t e) -> p t e", t=NT))\
                    .then_inc(free, 1)
                dve.wait_ge(free, MISC[("lg", n)][1] + 1)
                for t in range(NT):
                    ins = nc.vector.max(top[:, t, :], lg[:, t, :])
                link(ins)
                for t in range(NT):
                    ins = nc.vector.max_index(idx[:, t, :], top[:, t, :], lg[:, t, :])
                link(ins)
                nc.vector.tensor_tensor(lg[:, :, :], lg[:, :, :], top[:, :, 0:1].to_broadcast([P, NT, E_ROUTED]),
                                        ALU.subtract).then_inc(lgm_made, 1)
                link(nc.vector.tensor_copy(idf[:, :, :], idx[:, :, :]))
                iota = cst[:, C_IOTA:C_IOTA + E_ROUTED].rearrange("p (t e) -> p t e", t=1)\
                    .to_broadcast([P, NT, E_ROUTED])
                for i in range(2):
                    ins = nc.vector.tensor_tensor(oh[:, i, :, :], iota,
                                                  idf[:, :, i:i + 1].to_broadcast([P, NT, E_ROUTED]), ALU.is_equal)
                link(ins)
                link(nc.vector.tensor_tensor(oh[:, 2, :, :], oh[:, 0, :, :], oh[:, 1, :, :], ALU.add))

            def gates(n):
                dve.wait_ge(gex_made, n + 1)
                if n >= 1:
                    i, m = MISC[("gT", n - 1)]
                    dve.wait_ge(misc_full[i], m + 1)
                link(nc.vector.tensor_tensor(oh[:, 0, :, :], gex[:, :, :], oh[:, 2, :, :], ALU.mult))
                link(nc.vector.reduce_sum(gsum[:, 0, :], oh[:, 0, :, :], AX_X))
                link(nc.vector.reciprocal(gsum[:, 1, :], gsum[:, 0, :]))
                nc.vector.tensor_tensor(gts[:, :, :], oh[:, 0, :, :],
                                        gsum[:, 1, :].rearrange("p (t e) -> p t e", e=1)
                                        .to_broadcast([P, NT, E_ROUTED]), ALU.mult).then_inc(gts_made, 1)

            for s in range(SLOTS):
                n, g = divmod(s, NG)
                if s + AHEAD < SLOTS:
                    maxima(s + AHEAD, 0)
                if s == 0:
                    scale_rows(1, 2)
                if g == 1 and n >= 2:
                    scale_rows(2, n - 2)
                if g == 2 and n >= 2:
                    split_x2(n - 2)
                if g == 3 and n >= 1:
                    spread(n - 1, (0, 1))
                if s + AHEAD < SLOTS:
                    maxima(s + AHEAD, 1)
                if g == 0 and n >= 2:
                    add_attention(n - 2)
                    moments(2, n - 2)
                if g == 1 and n >= 1:
                    reciprocals(n - 1)
                if g == 2:
                    if n + 2 < NB:
                        second_part(n + 2)
                    if n >= 2:
                        route(n - 2)
                    if n + 3 < NB:
                        moments(1, n + 3)
                if g == 3:
                    if n + 3 < NB:
                        scale_rows(1, n + 3)
                    if n >= 2:
                        gates(n - 2)
                    if n >= 1:
                        spread(n - 1, (2, 3))
            add_attention(2)
            layer_norm(2, 2)

            def hidden(e, c):
                nc.vector.scalar_tensor_tensor(out=hf[c], in0=h2_bank[c][:, :],
                                               scalar=cst[:, bass.ds(e * HC + (C_B11 + c), 1)], in1=sil[c],
                                               op0=ALU.add, op1=ALU.mult).then_inc(hf_made, 1)

            def low(ring, c):
                nc.vector.tensor_tensor(hsp[:, 1, ring, c, :], hf[c], hsp[:, 0, ring, c, :],
                                        ALU.subtract).then_inc(lo_made, 1)

            def ungated(e, ring):
                nc.vector.tensor_scalar(yt[:, ring, :], y_bank[ring][:, :], cst[:, C_B2 + e:C_B2 + e + 1], None,
                                        ALU.add).then_inc(yt_made, 1)

            def gated(e, b):
                nc.vector.scalar_tensor_tensor(out=yt[:, b % 2, :], in0=y_bank[b % 2][:, :],
                                               scalar=cst[:, bass.ds(e + C_B2, 1)], in1=gate_rows[b],
                                               op0=ALU.add, op1=ALU.mult).then_inc(yt_made, 1)

            for u, (e, b) in enumerate(UNIT):
                for c in range(HC):
                    k = HC * u + c
                    dve.wait_ge(sil_made, k + 1)
                    dve.wait_ge(h2_done, k + 1)
                    if k >= 2:
                        dve.wait_ge(lo_made, k - 1)
                    hidden(e, c)
                    if k >= 1:
                        dve.wait_ge(hi_made, k)
                        low((k - 1) // HC % 2, (k - 1) % HC)
                if u >= 1:
                    dve.wait_ge(y_done, u)
                    if u >= 3:
                        dve.wait_ge(acc_made, u - 2)
                    old_e, old_b = UNIT[u - 1]
                    if old_e < 2:
                        ungated(old_e, (u - 1) % 2)
                    else:
                        dve.wait_ge(d_gate[old_b], 16)
                        gated(old_e, old_b)
                if u == 1:
                    reciprocals(3)
                if u == 2:
                    split_x2(2)
                    route(2)
                    spread(3, range(NG))
                if u == 3:
                    gates(2)
                    add_attention(3)
                    layer_norm(2, 3)
                if u == 5:
                    split_x2(3)
                if u == 6:
                    route(3)
                if u == 7:
                    gates(3)
            with dve.Fori(3, E) as e:
                for k in range(HC * NB):
                    b, c = divmod(k, HC)
                    dve.wait_ge(sil_made, e * 8 + (k + 1))
                    dve.wait_ge(h2_done, e * 8 + (k + 1))
                    dve.wait_ge(lo_made, e * 8 + (k - 1))
                    hidden(e, c)
                    dve.wait_ge(hi_made, e * 8 + k)
                    low((b + 1) % 2 if c == 0 else b % 2, 1 - c)
                    if c == 1:
                        dve.wait_ge(y_done, e * 4 + b)
                        if b == 0:
                            dve.wait_ge(d_gate[NB - 1], (e - 2) * 16)
                        else:
                            dve.wait_ge(d_gate[b - 1], (e - 2) * 16 + 16)
                        dve.wait_ge(acc_made, e * 4 + (b - 2))
                        gated(e - 1 if b == 0 else e, (b - 1) % NB)
            dve.wait_ge(hi_made, 8 * E)
            low(1, 1)
            dve.wait_ge(y_done, 4 * E)
            dve.wait_ge(d_gate[NB - 1], 16 * E_ROUTED)
            dve.wait_ge(acc_made, 4 * E - 2)
            gated(E - 1, NB - 1)

            for b in range(NB):
                src, free = full(("yT", b))
                if b >= 2:
                    dve.wait_ge(d_out[b % 2], 16 * (b // 2))
                nc.vector.scalar_tensor_tensor(out=fin[:, b % 2, :], in0=src[:, :], scalar=tanhg[:, 1:2],
                                               in1=xs[:, NT * b:NT * (b + 1), :].rearrange("p t d -> p (t d)"),
                                               op0=ALU.mult, op1=ALU.add).then_inc(fin_made, 1)

        @block.tensor
        def _(pe):
            def claim(key):
                i, m = MISC[key]
                if m >= 1:
                    pe.wait_ge(misc_free[i], m)
                return misc_bank[i], misc_full[i]

            def xhat_T(kind, n):
                l = ln_index(kind, n)
                dst, full = claim(("qT" if kind == 1 else "xT", n))
                pe.wait_ge(xhat_made, l + 1)
                for t in range(NT):
                    mm = nc.tensor.transpose(dst[:, t * P:(t + 1) * P], xhat[:, l % X_RING, t, :], ident)
                mm.then_inc(full, 1)
                return full

            def q_T(n):
                xhat_T(1, n)

            def q_features(n, half):
                dst, full = claim(("qA" if half == 0 else "qB", n))
                i, m = MISC[("qT", n)]
                pe.wait_ge(misc_free[i], m + 1)
                pe.wait_ge(bd_made, 1)
                nc.tensor.matmul(dst[:, :], bdz[:, half * P:(half + 1) * P], qT[:, :],
                                 start=True, stop=True).then_inc(full, 1)

            pe.wait_ge(d_const, 16)
            dst, full = claim(("cT", 0))
            pe.wait_ge(d_ctx, 16 * (1 + NB))
            for n in range(NB):
                mm = nc.tensor.transpose(dst[:, n * P:(n + 1) * P], ctx_sb[:, n, :], ident)
            mm.then_inc(full, 1)
            dst, full = claim(("cT", 1))
            nc.tensor.transpose(dst[:, 0:P], ctx_rm, ident).then_inc(full, 1)
            for k in range(2):
                i, m = MISC[("cT", k)]
                pe.wait_ge(misc_free[i], m + 1)
            pe.wait_ge(bd_made, 1)

            def keys_z(dst, at, half, n0, n1):
                return nc.tensor.matmul(dst[:, at:at + (n1 - n0) * SP_], bdz[:, half * P:(half + 1) * P],
                                        ctxT.rearrange("p n k -> p (n k)")[:, n0 * SP_:n1 * SP_],
                                        start=True, stop=True)

            dst, full = claim(("zk", 0))
            keys_z(dst, 0, 0, *K_ROUNDS[0])
            keys_z(dst, SP_, 1, *K_ROUNDS[0]).then_inc(full, 1)
            q_T(0)
            q_features(0, 0)
            q_features(0, 1)
            for half in range(2):
                dst, full = claim(("zk", 1 + half))
                keys_z(dst, 0, half, *K_ROUNDS[1]).then_inc(full, 1)
            dst, full = claim(("v", 0))
            for n in range(NB):
                mm = nc.tensor.matmul(dst[:, n * P:(n + 1) * P], ctxT[:, n, 0:P], bd[:, :, 0, :],
                                      start=True, stop=True)
            mm.then_inc(full, 1)
            dst, full = claim(("v", 1))
            for n in range(NB):
                for j in range(GH):
                    mm = nc.tensor.matmul(dst[RP * j:RP * (j + 1), n * NG * HD:(n + 1) * NG * HD], ctxT[:, n, P:SP_],
                                          bd[:, j:H:GH, 0, :], start=True, stop=True)
            mm.then_inc(full, 1)
            q_T(1)

            def max_unit(m):
                s, i = divmod(m, MAXU)
                n, g = divmod(s, NG)
                t, pair = divmod(i, GH // 2)
                if i == 0 and g % 2 == 0:
                    pe.wait_ge(d_qin[n % 2][g // 2], 16 * len(Q_TERMS) * (n // 2 + 1))
                if i == 0 and s in (0, NG):
                    pe.wait_ge(d_kin[s // NG], 16 * len(K_TERMS))
                if m >= 2:
                    pe.wait_ge(max_read, m - 1)
                for j in range(2):
                    h = GH * g + 2 * pair + j
                    mm = nc.tensor.matmul(mx_bank[m % 2][:, j * S:(j + 1) * S],
                                          qs[0:KROWS, n % 2, h, t * P:(t + 1) * P],
                                          ks[0:KROWS, h, n, 0:S], start=True, stop=True)
                mm.then_inc(max_done, 1)

            def max_T(s):
                dst, full = claim(("nm", s))
                pe.wait_ge(nm_made, s + 1)
                pe.wait_ge(ident16_made, 1)
                for t in range(NT):
                    mm = nc.tensor.transpose(dst[0:PARTS * GH, :].bitcast(BF16)[:, t * P:(t + 1) * P],
                                             nm[:, t, :, :].rearrange("p c h -> p (c h)"), ident16[:, :])
                mm.then_inc(full, 1)

            q_features(1, 0)
            q_features(1, 1)
            for m in range(MAXU):
                max_unit(m)
            max_T(0)
            for s in range(1, AHEAD):
                for m in range(MAXU * s, MAXU * (s + 1)):
                    max_unit(m)
                if s + 1 < AHEAD:
                    max_T(s)
            pe.wait_ge(d_ones, 16 * PARTS)

            def scores(s, u):
                n, g = divmod(s, NG)
                k = UNITS * s + u
                if k >= S_RING:
                    pe.wait_ge(p_made, k - S_RING + 1)
                dst = s_bank[k % S_RING]
                if u < GH:
                    h = GH * g + u
                    mm = nc.tensor.matmul(dst[:, :], ks[0:SROWS, h, n, 0:P], qs[0:SROWS, n % 2, h, :],
                                          start=True, stop=True)
                else:
                    for j in range(GH):
                        h = GH * g + j
                        mm = nc.tensor.matmul(dst[RP * j:RP * (j + 1), :], ks[0:SROWS, h, n, P:SP_],
                                              qs[0:SROWS, n % 2, h, :], start=True, stop=True)
                mm.then_inc(s_done, 1)

            def weighted(s):
                n, g = divmod(s, NG)
                k = UNITS * s
                pe.wait_ge(p_made, k + UNITS)
                if s == 0:
                    pe.wait_ge(v_made, V_OPS)
                    pe.wait_ge(ones_made, 1)
                if s >= 1:
                    pe.wait_ge(o_made, s)
                nc.tensor.matmul(ot_bank[:, :], v_rm[:, n, g, :], prob[:, (k + GH) % P_RING, :],
                                 start=True, stop=False, skip_group_check=True)

            def weighted_rest(s):
                n, g = divmod(s, NG)
                k = UNITS * s
                for j in range(GH):
                    mm = nc.tensor.matmul(ot_bank[RP * j:RP * (j + 1), :], v_sb[:, n, GH * g + j, :],
                                          prob[:, (k + j) % P_RING, :], start=False, stop=True,
                                          skip_group_check=True)
                mm.then_inc(pv_done, 1)

            def project(n):
                dst, full = claim(("fc", n))
                pe.wait_ge(on_made, NG * (n + 1))
                pe.wait_ge(d_fc, 16)
                for t in range(NT):
                    for g in range(NG):
                        nc.tensor.matmul(dst[:, t * P:(t + 1) * P], osum[:, n % 2, g, t * P:(t + 1) * P],
                                         fc_sb[:, g, :], start=(g == 0), stop=False)
                    mm = nc.tensor.matmul(dst[:, t * P:(t + 1) * P], one_row, fc_sb[0:1, NG, :],
                                          start=False, stop=True)
                mm.then_inc(full, 1)

            def logits(n):
                dst, full = claim(("lg", n))
                i, m = MISC[("xT", n)]
                pe.wait_ge(misc_free[i], m + 1)
                for t in range(NT):
                    mm = nc.tensor.matmul(dst[:, t * E_ROUTED:(t + 1) * E_ROUTED], x2T[:, t * P:(t + 1) * P],
                                          cst[:, C_WG:C_WG + E_ROUTED], start=True, stop=True)
                mm.then_inc(full, 1)

            def gates_T(n):
                dst, full = claim(("gT", n))
                pe.wait_ge(gts_made, n + 1)
                for t in range(NT):
                    mm = nc.tensor.transpose(dst[0:E_ROUTED, t * P:(t + 1) * P], gts[:, t, :], ident)
                mm.then_inc(full, 1)

            m = AHEAD * MAXU
            for s in range(SLOTS):
                n, g = divmod(s, NG)
                pe.wait_ge(d_nm, 16 * (s + 1))

                def maximum():
                    nonlocal m
                    if s + AHEAD < SLOTS:
                        max_unit(m)
                        m += 1

                scores(s, 0)
                maximum()
                scores(s, 1)
                maximum()
                if s + AHEAD <= SLOTS:
                    max_T(s + AHEAD - 1)
                scores(s, 2)
                maximum()
                if s >= 1:
                    weighted(s - 1)
                maximum()
                scores(s, 3)
                maximum()
                if s >= 1:
                    weighted_rest(s - 1)
                maximum()
                if g == 0 and n >= 2:
                    project(n - 2)
                if g == 1 and n >= 2:
                    xhat_T(2, n - 2)
                if g == 2 and n >= 2:
                    logits(n - 2)
                if g == 0 and n + 2 < NB:
                    q_T(n + 2)
                if g == 1 and n + 2 < NB:
                    q_features(n + 2, 0)
                    q_features(n + 2, 1)
                scores(s, 4)
                maximum()
                maximum()
                if g == 3 and n >= 2:
                    gates_T(n - 2)
            weighted(SLOTS - 1)
            weighted_rest(SLOTS - 1)
            project(2)

            pe.wait_ge(wlo_made, 2 * E)
            pe.wait_ge(p_made, UNITS * SLOTS)
            pe.wait_ge(o_made, SLOTS)

            def three(dst, w_col, e, x_hi, x_lo, start, stop):
                hi = w_hi[:, e, w_col:w_col + P]
                lo = w_lo[:, e, w_col:w_col + P]
                nc.tensor.matmul(dst, hi, x_hi, start=start, stop=False)
                nc.tensor.matmul(dst, hi, x_lo, start=False, stop=False)
                return nc.tensor.matmul(dst, lo, x_hi, start=False, stop=stop)

            def up_step(e, b, c):
                x_hi, x_lo = xh[:, b * T:(b + 1) * T], xl[:, b * T:(b + 1) * T]
                three(h1_bank[c][:, :], c * P, e, x_hi, x_lo, True, True).then_inc(h1_done, 1)
                three(h2_bank[c][:, :], HID + c * P, e, x_hi, x_lo, True, True).then_inc(h2_done, 1)

            def down_step(e, ring, c):
                return three(y_bank[ring][:, :], 2 * HID + c * P, e, hsp[:, 0, ring, c, :], hsp[:, 1, ring, c, :],
                             c == 0, c == HC - 1)

            for u, (e, b) in enumerate(UNIT):
                pe.wait_ge(xh_made, b + 1)
                for c in range(HC):
                    if u >= 1:
                        pe.wait_ge(hf_made, HC * u + c - 1)
                    up_step(e, b, c)
                if u >= 1:
                    if u >= 3:
                        pe.wait_ge(yt_made, u - 2)
                    for c in range(HC):
                        pe.wait_ge(lo_made, HC * (u - 1) + c + 1)
                        mm = down_step(UNIT[u - 1][0], (u - 1) % 2, c)
                    mm.then_inc(y_done, 1)
                if u == 1:
                    xhat_T(2, 2)
                if u == 2:
                    logits(2)
                if u == 3:
                    project(3)
                if u == 4:
                    gates_T(2)
                if u == 5:
                    xhat_T(2, 3)
                if u == 6:
                    logits(3)
                if u == 7:
                    gates_T(3)
            with pe.Fori(3, E) as e:
                for b in range(NB):
                    for c in range(HC):
                        pe.wait_ge(hf_made, e * 8 + (HC * b + c - 1))
                        up_step(e, b, c)
                    pe.wait_ge(yt_made, e * 4 + (b - 2))
                    for c in range(HC):
                        pe.wait_ge(lo_made, e * 8 + (HC * (b - 1) + c + 1))
                        mm = down_step(e - 1 if b == 0 else e, (b - 1) % 2, c)
                    mm.then_inc(y_done, 1)
            pe.wait_ge(yt_made, 4 * E - 2)
            for c in range(HC):
                pe.wait_ge(lo_made, 8 * E - 1 + c)
                mm = down_step(E - 1, 1, c)
            mm.then_inc(y_done, 1)
            for b in range(NB):
                i, m = MISC[("yT", b)]
                dst, full = misc_bank[i], misc_full[i]
                if b < 2:
                    pe.wait_ge(misc_free[i], m)
                else:
                    pe.wait_ge(fin_made, b - 1)
                pe.wait_ge(acc_made, 4 * (E - 1) + b + 1)
                for t in range(NT):
                    mm = nc.tensor.transpose(dst[:, t * P:(t + 1) * P], acc[b][:, t * P:(t + 1) * P], ident)
                mm.then_inc(full, 1)


def kernel(x, ctx_1024, g_xattn, g_ffn, L0_xattn_fm_w, L0_xattn_fm_b, L0_xattn_fc_w, L0_xattn_fc_b,
           L0_ffn_Wg, L0_ffn_W1, L0_ffn_b1, L0_ffn_W11, L0_ffn_b11, L0_ffn_W2, L0_ffn_b2,
           L0_ffn_Ws1, L0_ffn_bs1, L0_ffn_Ws11, L0_ffn_bs11, L0_ffn_Ws2, L0_ffn_bs2):
    import numpy as np
    import concourse.bacc as bacc
    from concourse.bass_utils import run_bass_kernel_spmd

    f = lambda a: np.asarray(a)
    xin = np.ascontiguousarray(f(x).reshape(NB, NT, P, D).transpose(0, 2, 1, 3))

    const = np.zeros((P, C_END), np.float32)
    const[:, C_FM:C_FM + HD] = np.tile(f(L0_xattn_fm_w).T, (H, 1))
    rows = np.arange(P)
    const[:, C_MASK:C_MASK + H] = rows[:, None] // HD == np.arange(H)[None, :]
    const[:, C_SGN] = np.where(rows % FD < HD, 1.0, -1.0)
    const[:, C_FMB] = np.tile(f(L0_xattn_fm_b), P // HD)
    const[:, C_FMBV:C_FMBV + HD] = f(L0_xattn_fm_b)[None, :]
    const[:, C_WG:C_WG + E_ROUTED] = f(L0_ffn_Wg)
    const[:, C_GX] = f(g_xattn)
    const[:, C_GF] = f(g_ffn)
    const[:, C_IOTA:C_IOTA + E_ROUTED] = np.arange(E_ROUTED)[None, :]

    def chunks(shared, routed):
        a = np.concatenate([f(shared).reshape(2, HID), f(routed)])
        return a.reshape(E, HC, P).transpose(2, 0, 1).reshape(P, E * HC)

    const[:, C_B1:C_B11] = chunks(L0_ffn_bs1, L0_ffn_b1)
    const[:, C_B11:C_B2] = chunks(L0_ffn_bs11, L0_ffn_b11)
    const[:, C_B2] = f(L0_ffn_bs2)
    const[:, C_B2 + 2:C_ID] = f(L0_ffn_b2).T
    const[:, C_ID:C_END] = np.eye(P)

    fcw = np.zeros((P, NG + 1, D), np.float32)
    w = f(L0_xattn_fc_w).T.reshape(NG, GH, FD, D)
    for j in range(GH):
        fcw[2 * FD * j:2 * FD * j + FD, 0:NG] = w[:, j].transpose(1, 0, 2)
    fcw[0, NG] = f(L0_xattn_fc_b)

    def ups(shared, routed):
        return np.concatenate([f(shared).reshape(D, 2, HID).transpose(1, 0, 2), f(routed)])

    downs = np.concatenate([f(L0_ffn_Ws2).reshape(2, HID, D), f(L0_ffn_W2)])
    downs = downs.reshape(E, HC, P, D).transpose(0, 2, 1, 3).reshape(E, P, HC * D)
    wall = np.concatenate([ups(L0_ffn_Ws1, L0_ffn_W1), ups(L0_ffn_Ws11, L0_ffn_W11), downs], axis=2)

    arrays = {"x": xin, "ctx": f(ctx_1024), "const": const, "fcw": fcw, "wall": wall}
    nc = bacc.Bacc("TRN2", target_bir_lowering=False, num_devices=1)
    args = [nc.dram_tensor(f"in_{k}", a.shape, F32, kind="ExternalInput").ap() for k, a in arrays.items()]
    out = nc.dram_tensor("out", (NB, P, NT, D), F32, kind="ExternalOutput").ap()
    build(nc, *args, out)
    r = run_bass_kernel_spmd(nc, [{f"in_{k}": np.ascontiguousarray(a) for k, a in arrays.items()}], core_ids=[0])
    y = r.results[0]["out"]
    return y.transpose(0, 2, 1, 3).reshape(NB, T, D)
```

```python
from contextlib import ExitStack

import concourse.bass as bass
from concourse import mybir

F32, BF16, F16, U32 = mybir.dt.float32, mybir.dt.bfloat16, mybir.dt.float16, mybir.dt.uint32
ALU = mybir.AluOpType
ACT = mybir.ActivationFunctionType
AX_X = mybir.AxisListType.X

P = 128
NB, T, D = 4, 512, 128
NT = T // P
S = 154
SR = S - P
RP = 32
SP_ = P + RP
H, HD, FD = 16, 8, 16
NG, GH = 4, 4
PARTS = 3
Q_TERMS = (0, 0, 0, 1, 1, 2)
K_TERMS = (0, 1, 2, 0, 1, 0)
KROWS = len(Q_TERMS) * FD
SROWS = KROWS + PARTS
E_ROUTED, HID = 16, 256
E = E_ROUTED + 2
HC = HID // P
WCOLS = 3 * HID
TOK = NB * T
EPS = 1e-5
SCALE = float(D) ** -0.5

C_FM, C_MASK, C_SGN, C_FMB, C_FMBV, C_WG, C_GX, C_GF, C_IOTA = 0, 8, 24, 25, 26, 34, 50, 51, 52
C_B1 = C_IOTA + 32
C_B11 = C_B1 + 2 * HC
C_PART = C_B11 + 2 * HC
C_ID = C_PART + 1
C_END = C_ID + P

GROUPS = 2
GB = NB // GROUPS
GJ = GB * NT
TILES = -(-(2 * GJ + E_ROUTED - 1) // 4) * 4
QUAD = 4
QUADS = TILES // QUAD
ALLQ = GROUPS * QUADS
CMAX = GJ

UNITS = 5
MAX_BLOCKS = (2, 3, 3, 3, 3, 2)
MAXU = len(MAX_BLOCKS)
SLOTS = NB * NG
AHEAD = 2
S_RING, P_RING = 3, 8
K_ROUNDS = ((0, 1), (1, NB))
SHARED_A = [(e, b) for b in range(NB // 2) for e in range(2)]
SHARED_B = [(e, b) for b in range(NB // 2, NB) for e in range(2)]
UA = len(SHARED_A)
ZK_COLS = (2 * SP_, 3 * SP_, 3 * SP_)
W_RING = 2
WH = WCOLS // 2
X_RING = 2
V_OPS = 2 * NB + 2 * GH


def misc_order():
    out = [("cT", 0), ("cT", 1), ("zk", 0), ("qT", 0), ("qA", 0), ("qB", 0), ("zk", 1), ("zk", 2)]
    out += [("v", 0), ("v", 1), ("qT", 1), ("qA", 1), ("qB", 1), ("nm", 0)]
    out += [("nm", s) for s in range(1, AHEAD - 1)]
    for s in range(SLOTS):
        n, g = divmod(s, NG)
        old = n >= 2
        out += [("nm", s + AHEAD - 1)] * (s + AHEAD <= SLOTS)
        out += [(("fc", "xT", "lg", "")[g], n - 2)] * (old and g < 3)
        out += [("pf", 0)] * (s + 1 == SLOTS)
        if n + 2 < NB:
            out += {0: [("qT", n + 2)], 1: [("qA", n + 2), ("qB", n + 2)]}.get(g, [])
    where = {key: (i % 2, i // 2) for i, key in enumerate(out)}
    first = (len(out) + 1) // 2
    late = [("fc", 2), ("gT", 0), ("gT", 1), ("bs", 0), ("xT", 2), ("fc", 3), ("lg", 2), ("xT", 3), ("lg", 3),
            ("pf", 1), ("bs", 1), ("gT", 2), ("gT", 3)]
    where.update({key: (0, first + i) for i, key in enumerate(late)})
    return where, len(out) // 2


MISC, SECOND_USES = misc_order()
LN = [(1, 0), (1, 1), (1, 2), (1, 3), (2, 0), (2, 1), (2, 2), (2, 3)]


def build(nc, x, ctx, const, tri, brows, fcw, wall, out):
    with ExitStack() as stack:
        def sb(name, shape, dt=F32):
            return stack.enter_context(nc.sbuf_tensor(name, shape, dt))

        def sem(name):
            return stack.enter_context(nc.semaphore(name))

        bank = [stack.enter_context(nc.psum_tensor(f"bank{i}", [P, 512], F32)) for i in range(8)]
        s_bank, ot_bank, mx_bank, misc_bank = bank[0:3], bank[3], bank[4:6], bank[6:8]
        h1_bank, h2_bank, y_bank = bank[0:2], bank[2:4], bank[4:6]

        k_scr = nc.dram_tensor("k_scr", [PARTS, 2, P, NB * SP_], BF16, kind="Internal").ap()
        q_scr = nc.dram_tensor("q_scr", [NB, PARTS, 2, P, T], BF16, kind="Internal").ap()
        dn_scr = nc.dram_tensor("dn_scr", [NB, 2, GH, NG, T], F32, kind="Internal").ap()
        x_scr = [nc.dram_tensor(f"x_scr{i}", [TILES * P, D], F32, kind="Internal").ap() for i in range(GROUPS)]
        y_scr = [nc.dram_tensor(f"y_scr{i}", [TILES * P, D], F32, kind="Internal").ap() for i in range(GROUPS)]

        cst = sb("cst", [P, C_END])
        ident = cst[:, C_ID:C_ID + P]
        ident16 = sb("ident16", [P, P], BF16)
        fc_sb = sb("fc_sb", [P, NG + 1, D])
        bd = sb("bd", [P, H, 2, HD])
        sgnb = sb("sgnb", [P, 1])
        b1q = sb("b1q", [P, 2, HC, QUAD])
        tri16 = sb("tri16", [P, P], BF16)
        ones16 = sb("ones16", [P, P], BF16)
        b2r = sb("b2r", [E_ROUTED + 1, D])
        tanhg = sb("tanhg", [P, 2])
        mhalf = sb("mhalf", [P, NT])
        xs = sb("xs", [P, NB * NT, D])
        xhat = sb("xhat", [P, X_RING, NT, D])
        stats = sb("stats", [P, len(LN), NT, 6])
        mv = sb("mv", [P, len(LN), NT, 2])
        veps = sb("veps", [P, len(LN), NT])
        rstd = sb("rstd", [P, len(LN), NT])
        arena = sb("arena", [P, 2 * H * T // 2])
        qs = arena[:, :].bitcast(BF16).rearrange("p (b h t) -> p b h t", b=2, h=H)
        ctx_sb = arena[:, 4608:5120].rearrange("p (n d) -> p n d", n=NB)
        ctx_rm = arena[:, 5120:5248]
        ctxT = arena[:, 5248:5248 + NB * SP_].rearrange("p (n k) -> p n k", n=NB)
        v_tmp = arena[:, 6016:6528]
        v_tmr = arena[:, 6528:7040]
        xq = [arena[:, i * T:(i + 1) * T] for i in range(2)]
        yq = [arena[:, (2 + i) * T:(3 + i) * T] for i in range(2)]
        xqs = arena[:, 4 * T:6 * T].bitcast(F16).rearrange("p (l b t) -> p l b t", l=2, b=2)
        gT = [arena[0:E_ROUTED + 1, (6 + i) * T:(7 + i) * T] for i in range(2)]
        sil = [arena[:, (8 + c) * T:(9 + c) * T] for c in range(HC)]
        hf = [arena[:, (10 + c) * T:(11 + c) * T] for c in range(HC)]
        hsp = arena[:, 12 * T:16 * T].bitcast(F16).rearrange("p (l b c t) -> p l b c t", l=2, b=2, c=HC)
        ks = sb("ks", [P, H, NB, SP_], BF16)
        v_sb = sb("v_sb", [P, NB, H, 2 * FD])
        one_row = v_sb[0:1, 0, 0, FD:FD + 1].to_broadcast([1, P])
        v_rm = sb("v_rm", [P, NB, NG, P])
        qT = sb("qT", [P, T])
        f_q = sb("f_q", [P, 2, T])
        qp = sb("qp", [P, PARTS, 2 * T], BF16)
        mx = sb("mx", [P, NT, GH])
        mxf = mx[:, :, :].rearrange("p t h -> p (t h)")
        nm_r = sb("nm_r", [P, NT, GH])
        nm = sb("nm", [P, NT, PARTS, GH], BF16)
        nmT = sb("nmT", [PARTS * GH, T], BF16)
        prob = sb("prob", [P, P_RING, T])
        osum = sb("osum", [P, 2, NG, T])
        flat = osum[:, :, :, :].rearrange("p b g t -> p (b g t)")
        f_k, kp = [], []
        at = 0
        for n0, n1 in K_ROUNDS:
            w = 2 * (n1 - n0) * SP_
            f_k.append(flat[:, at:at + w])
            kp.append(flat[:, at + w:at + w + PARTS * w // 2].bitcast(BF16).rearrange("p (c k) -> p c k", c=PARTS))
            at += w + PARTS * w // 2
        dn = sb("dn", [P, 2, NG * GH * T // P])
        den = sb("den", [P, 2, T])
        x2T = sb("x2T", [P, T])
        xh = sb("xh", [P, TOK], F16)
        xl = sb("xl", [P, TOK], F16)
        lg = sb("lg", [P, NT, E_ROUTED])
        top = sb("top", [P, NT, 8])
        idx = sb("idx", [P, NT, 8], U32)
        idf = sb("idf", [P, NT, 8])
        dl = sb("dl", [P, NT])
        gex = sb("gex", [P, NT])
        gsum = sb("gsum", [P, 2, NT])
        gk = sb("gk", [P, NB * NT, 2])
        gkt = sb("gkt", [P, NB * NT, 2])
        f32s = qp[:, :, :].rearrange("p c t -> p (c t)").bitcast(F32)
        EJ = E_ROUTED * NT * NB
        oh = f32s[:, 0:2 * EJ].rearrange("p (k j e) -> p k j e", k=2, j=NB * NT)
        gts = f32s[:, 2 * EJ:2 * EJ + NB * NT * (E_ROUTED + 1)].rearrange("p (j e) -> p j e", j=NB * NT)
        gtmp = f32s[:, 2 * EJ + 2 * 272:2 * EJ + 2 * 272 + NT * E_ROUTED].rearrange("p (t e) -> p t e", t=NT)
        fq = f_q[:, :, :].rearrange("p a t -> p (a t)")
        cmp_ = fq[:, 0:TILES * E_ROUTED]
        slot0 = fq[:, 512:512 + GJ * E_ROUTED].rearrange("p (j e) -> p j e", j=GJ)
        below = fq[:, 640:640 + E_ROUTED ** 2].rearrange("p (e f) -> p e f", e=E_ROUTED)
        member = fq[:, 896:896 + (GJ + 1) * E_ROUTED // 2].bitcast(BF16).rearrange("p (j e) -> p j e", j=GJ + 1)
        pref = qT[:, 0:(GJ + 1) * E_ROUTED].rearrange("p (j e) -> p j e", j=GJ + 1)
        btile = sb("btile", [P, 4, E_ROUTED])
        exf = sb("exf", [P, TILES])
        exT = sb("exT", [E_ROUTED, TILES])
        exu = sb("exu", [1, GROUPS * TILES], U32)
        posf = sb("posf", [P, 2, GJ])
        posu = sb("posu", [P, GROUPS, 2, GJ], U32)
        bsel = sb("bsel", [P, 2 * HC, GROUPS * TILES])
        bTs = prob[0:E_ROUTED, 2, :]
        w_st = sb("w_st", [P, W_RING, WH])
        w_hi = sb("w_hi", [P, E, WCOLS], F16)
        w_lo = sb("w_lo", [P, E, WCOLS], F16)
        yg = [osum[:, i, :, :].rearrange("p g t -> p (g t)").rearrange("p (k j d) -> p k j d", k=2, d=D)
              for i in range(GROUPS)]

        bdz = bd[:, :, :, :].rearrange("p h s e -> p (h s e)")

        d_const, d_fc, d_ctx = sem("d_const"), sem("d_fc"), sem("d_ctx")
        d_x = [sem(f"d_x{n}") for n in range(NB)]
        d_w = [sem(f"d_w{i}") for i in range(W_RING)]
        d_ones, d_nm = sem("d_ones"), sem("d_nm")
        d_kout, d_kin = ([sem(f"d_{k}{i}") for i in range(2)] for k in ("kout", "kin"))
        d_qout = [sem(f"d_qout{i}") for i in range(2)]
        d_qin = [[sem(f"d_qin{i}{a}") for a in range(2)] for i in range(2)]
        d_tri, d_brow, d_b2, d_fill = (sem(k) for k in ("d_tri", "d_brow", "d_b2", "d_fill"))
        d_xs = [sem(f"d_xs{i}") for i in range(GROUPS)]
        d_xq = [sem(f"d_xq{i}") for i in range(2)]
        d_yq = [sem(f"d_yq{i}") for i in range(2)]
        d_y = [sem(f"d_y{i}") for i in range(GROUPS)]
        d_yg = [sem(f"d_yg{b}") for b in range(NB)]
        d_out = sem("d_out")
        z_rem, ones_made, ones_row, half_made = (sem(k) for k in ("z_rem", "ones_made", "ones_row", "half_made"))
        bd_made, sgnb_made, tanh_made, ident16_made = (sem(k) for k in ("bd_made", "sgnb_made", "tanh_made", "ident16_made"))
        fk_made, kp_made, vz_made, v_made = (sem(k) for k in ("fk_made", "kp_made", "vz_made", "v_made"))
        misc_full = [sem(f"misc_full{i}") for i in range(2)]
        misc_free = [sem(f"misc_free{i}") for i in range(2)]
        var_made, rstd_made, xhat_made = (sem(k) for k in ("var_made", "rstd_made", "xhat_made"))
        qr_made, qp1_made = sem("qr_made"), sem("qp1_made")
        qp_made, max_done, max_read, nm_made = (sem(k) for k in ("qp_made", "max_done", "max_read", "nm_made"))
        s_done, p_made, pv_done, o_made, den_made, on_made, rec_made = (
            sem(k) for k in ("s_done", "p_made", "pv_done", "o_made", "den_made", "on_made", "rec_made"))
        d_dn = [sem(f"d_dn{i}") for i in range(4)]
        xh_made, dl_made, gex_made, gts_made = (sem(k) for k in ("xh_made", "dl_made", "gex_made", "gts_made"))
        member_made, pos_made, ext_made, zero_made, ones16_made, tri_made = (
            sem(k) for k in ("member_made", "pos_made", "ext_made", "zero_made", "ones16_made", "tri_made"))
        whi_made, wlo_made = sem("whi_made"), sem("wlo_made")
        h1_done, h2_done, sil_made, hf_made, hi_made, lo_made = (
            sem(k) for k in ("h1_done", "h2_done", "sil_made", "hf_made", "hi_made", "lo_made"))
        y_done, y_add, y_out, fin_made = (sem(k) for k in ("y_done", "y_add", "y_out", "fin_made"))
        y_stored = sem("y_stored")
        b1_made, bsel_made = sem("b1_made"), sem("bsel_made")
        xt_done, xqh_made, xql_made = (sem(k) for k in ("xt_done", "xqh_made", "xql_made"))
        v_chain = sem("v_chain")

        block = stack.enter_context(nc.Block())

        def den_tile(n, g):
            return den[:, g % 2, :] if n + 1 < NB else prob[:, 4 + g, :]

        def xhat_tile(kind, n):
            l = ln_index(kind, n)
            return prob[:, n - 2, :].rearrange("p (t d) -> p t d", t=NT) if (kind, n) in ((2, 2), (2, 3)) \
                else xhat[:, l % X_RING, :, :]

        def ge(engine, signal, value):
            if not isinstance(value, int) or value > 0:
                engine.wait_ge(signal, value)

        def ln_index(kind, n):
            return LN.index((kind, n))

        @block.sync
        def _(sp):
            sp.dma_start(cst[:, :], const).then_inc(d_const, 16)
            sp.dma_start(xs[:, 0:NT, :], x[0]).then_inc(d_x[0], 16)
            sp.wait_ge(z_rem, 1)
            for n in range(NB):
                sp.dma_start(ctx_rm[RP * n:RP * n + SR, :], ctx[n, P:S, :]).then_inc(d_ctx, 16)
            sp.wait_ge(ones_row, 1)
            w = H * NB * SP_ // RP
            for c in range(PARTS):
                sp.dma_start(ks[KROWS + c:KROWS + c + 1, :, :, :].rearrange("c h n k -> c (h n k)")
                             .rearrange("c (a b) -> c a b", b=w), qp[RP * c:RP * (c + 1), 2, 0:w]).then_inc(d_ones, 16)
            for n in range(1, NB):
                sp.dma_start(xs[:, NT * n:NT * (n + 1), :], x[n]).then_inc(d_x[n], 16)
            sp.dma_start(den[:, 1, 0:P], tri).then_inc(d_tri, 16)
            sp.dma_start(b2r[:, :], brows[:, 2 * HID:2 * HID + D]).then_inc(d_b2, 16)

            def keys_out(r):
                sp.wait_ge(kp_made, r + 1)
                n0, n1 = K_ROUNDS[r]
                for c in range(PARTS):
                    sp.dma_start(k_scr[c, :, :, n0 * SP_:n1 * SP_].rearrange("a p k -> p a k"),
                                 kp[r][:, c, :].rearrange("p (a k) -> p a k", a=2)).then_inc(d_kout[r], 16)

            def keys_in(r):
                sp.wait_ge(d_kout[r], 16 * PARTS)
                n0, n1 = K_ROUNDS[r]
                for i, c in enumerate(K_TERMS):
                    sp.dma_start(ks[FD * i:FD * (i + 1), :, n0:n1, :].rearrange("f h n k -> f h (n k)"),
                                 k_scr[c, :, :, n0 * SP_:n1 * SP_].rearrange("a (h f) k -> f (a h) k", f=FD))\
                        .then_inc(d_kin[r], 16)

            def queries_out(n, a):
                sp.wait_ge(qp_made, 2 * n + a + 1)
                sp.dma_start(q_scr[n, :, a].rearrange("c p t -> p c t"), qp[:, :, a * T:(a + 1) * T])\
                    .then_inc(d_qout[a], 16)

            def queries_in(n, a):
                sp.wait_ge(d_qout[a], 16 * (n + 1))
                if n >= 2:
                    sp.wait_ge(s_done, UNITS * (NG * (n - 2) + (a + 1) * NG // 2))
                if n == 1:
                    sp.wait_ge(v_made, V_OPS)
                for i, c in enumerate(Q_TERMS):
                    sp.dma_start(qs[FD * i:FD * (i + 1), n % 2, a * H // 2:(a + 1) * H // 2, :],
                                 q_scr[n, c, a].rearrange("(h f) t -> f h t", f=FD)).then_inc(d_qin[n % 2][a], 16)

            def move_denominators(n):
                rows = osum[FD:P:2 * FD, n % 2, :, :]
                spread = dn_scr[n].rearrange("i j g t -> i (j g t)").rearrange("i (p k) -> i p k", p=P)
                sp.wait_ge(o_made, NG * (n + 1))
                sp.dma_start(dn_scr[n, 0], rows).then_inc(d_dn[0], 16)
                sp.wait_ge(d_dn[0], 16 * (n + 1))
                sp.dma_start(dn[:, 0, :], spread[0]).then_inc(d_dn[1], 16)
                sp.wait_ge(rec_made, n + 1)
                sp.dma_start(spread[1], dn[:, 1, :]).then_inc(d_dn[2], 16)
                sp.wait_ge(d_dn[2], 16 * (n + 1))
                sp.dma_start(rows, dn_scr[n, 1]).then_inc(d_dn[3], 16)

            keys_out(0)
            keys_in(0)
            queries_out(0, 0)
            queries_in(0, 0)
            queries_out(0, 1)
            queries_in(0, 1)
            keys_out(1)
            keys_in(1)
            sp.dma_start(fc_sb[:, :, :], fcw).then_inc(d_fc, 16)
            sp.wait_ge(zero_made, 1)
            for i in range(GROUPS):
                sp.dma_start(x_scr[i].rearrange("(i p) d -> p i d", p=P),
                             den[:, 0:1, 0:D].to_broadcast([P, TILES, D])).then_inc(d_fill, 16)
            for n in range(1, NB):
                for a in range(2):
                    queries_out(n, a)
                for a in range(2):
                    queries_in(n, a)
                if n >= 2:
                    move_denominators(n - 2)
            for n in range(NB - 2, NB):
                move_denominators(n)

            sp.wait_ge(pv_done, SLOTS)
            sp.dma_start(bTs, brows[0:E_ROUTED, 0:2 * HID]).then_inc(d_brow, 16)
            sp.wait_ge(s_done, UNITS * SLOTS)

            def load_quad(g, q, ring, k):
                if not isinstance(k, int) or k >= 2:
                    sp.wait_ge(xt_done, k - 1)
                rows = x_scr[g].rearrange("(q t p) d -> p q t d", t=QUAD, p=P)[:, bass.ds(q, 1), :, :]
                sp.dma_start(xq[ring], rows.rearrange("p q t d -> p (q t) d")).then_inc(d_xq[ring], 16)

            def store_quad(g, q, ring, k):
                sp.wait_ge(y_out, k + 1)
                rows = y_scr[g].rearrange("(q t p) d -> p q t d", t=QUAD, p=P)[:, bass.ds(q, 1), :, :]
                sp.dma_start(rows.rearrange("p q t d -> p (q t) d"), yq[ring]).then_inc(d_yq[ring], 16)

            sp.wait_ge(d_xs[0], 16 * 2 * GJ)
            for ring in range(2):
                load_quad(0, ring, ring, ring)
            for g in range(GROUPS):
                with sp.Fori(0, QUADS // 2 - 1) as i:
                    for ring in range(2):
                        load_quad(g, i * 2 + (2 + ring), ring, i * 2 + (QUADS * g + 2 + ring))
                        store_quad(g, i * 2 + ring, ring, i * 2 + (QUADS * g + ring))
                if g + 1 < GROUPS:
                    sp.wait_ge(d_xs[g + 1], 16 * 2 * GJ)
                    for ring in range(2):
                        load_quad(g + 1, ring, ring, QUADS * (g + 1) + ring)
                for ring in range(2):
                    store_quad(g, QUADS - 2 + ring, ring, QUADS * (g + 1) - 2 + ring)
                for ring in range(2):
                    sp.wait_ge(d_yq[ring], 16 * (g + 1) * QUADS // 2)
                sp.sem_inc(y_stored, 1)
            for b in range(NB):
                sp.wait_ge(fin_made, b + 1)
                sp.dma_start(out[b], xs[:, NT * b:NT * (b + 1), :]).then_inc(d_out, 16)
            sp.wait_ge(d_out, 16 * NB)

        @block.gpsimd
        def _(pool):
            nc.gpsimd.memset(mhalf[:, :], -0.5).then_inc(half_made, 1)
            nc.gpsimd.memset(qp[:, 2, 0:H * NB * SP_ // RP], 1.0).then_inc(ones_row, 1)
            nc.gpsimd.memset(v_sb[:, :, :, FD:2 * FD], 1.0).then_inc(ones_made, 1)
            nc.gpsimd.memset(den[:, 0, :], 0.0).then_inc(zero_made, 1)
            nc.gpsimd.memset(ones16[:, :], 1.0).then_inc(ones16_made, 1)

            def rsqrt(kind, n):
                l = ln_index(kind, n)
                pool.wait_ge(var_made, l + 1)
                nc.gpsimd.tensor_tensor(rstd[:, l, :], veps[:, l, :], mhalf[:, :], ALU.pow).then_inc(rstd_made, 1)

            def weights_low(e):
                for i in (2 * e, 2 * e + 1):
                    pool.wait_ge(whi_made, i + 1)
                    cols = slice(i % 2 * WH, (i % 2 + 1) * WH)
                    nc.gpsimd.tensor_tensor(w_lo[:, e, cols], w_st[:, i % W_RING, :], w_hi[:, e, cols],
                                            ALU.subtract).then_inc(wlo_made, 1)

            pool.wait_ge(half_made, 1)
            rsqrt(1, 0)

            def rest_q(n, a):
                i, m = MISC[("qB" if a else "qA", n)]
                pool.wait_ge(misc_free[i], m + 1)
                nc.gpsimd.tensor_tensor(f_q[:, a, :], f_q[:, a, :], qp[:, 0, a * T:(a + 1) * T],
                                        ALU.subtract).then_inc(qr_made, 1)

            def third_q(n, a):
                pool.wait_ge(qp1_made, 2 * n + a - 1)
                nc.gpsimd.tensor_tensor(qp[:, 2, a * T:(a + 1) * T], f_q[:, a, :], qp[:, 1, a * T:(a + 1) * T],
                                        ALU.subtract).then_inc(qp_made, 1)

            weights_low(0)
            weights_low(1)
            rsqrt(1, 1)
            rest_q(1, 0)
            rest_q(1, 1)
            third_q(1, 0)
            third_q(1, 1)
            rsqrt(1, 2)

            def normalise(n):
                for g in range(NG):
                    k = NG * n + g
                    pool.wait_ge(den_made, k + 1)
                    rows = osum[:, n % 2, g, :]
                    nc.gpsimd.tensor_tensor(rows, rows, den_tile(n, g), ALU.mult).then_inc(on_made, 1)

            for s in range(SLOTS):
                n, g = divmod(s, NG)
                if g == 3 and n >= 1:
                    normalise(n - 1)
                if g == 2 and n + 2 < NB:
                    rest_q(n + 2, 0)
                    rest_q(n + 2, 1)
                if g == 3 and n + 2 < NB:
                    third_q(n + 2, 0)
                    third_q(n + 2, 1)
                if g == 3 and n + 3 < NB:
                    rsqrt(1, n + 3)
                weights_low(s + 2)
                if g == 0 and n >= 2:
                    rsqrt(2, n - 2)

            def scatter(g, tiles):
                for j in tiles:
                    n, t = divmod(GJ * g + j, NT)
                    for k in range(2):
                        nc.gpsimd.indirect_dma_start(x_scr[g], bass.IndirectOffsetOnAxis(posu[:, g, k, j:j + 1], 0),
                                                     xhat_tile(2, n)[:, t, :], None).then_inc(d_xs[g], 16)

            pool.wait_ge(d_fill, 16 * GROUPS)
            pool.wait_ge(pos_made, 1)
            scatter(0, range(GJ // 2))
            rsqrt(2, 2)
            scatter(0, range(GJ // 2, GJ))
            normalise(3)
            rsqrt(2, 3)
            pool.wait_ge(pos_made, 2)
            scatter(1, range(GJ))

            i, m = MISC[("fc", 3)]
            pool.wait_ge(misc_full[i], m + 1)
            for g in range(GROUPS):
                pool.wait_ge(y_stored, g + 1)
                for b in range(GB):
                    for t in range(NT):
                        for k in range(2):
                            j = NT * b + t
                            nc.gpsimd.indirect_dma_start(yg[g][:, k, j, :], None, y_scr[g],
                                                         bass.IndirectOffsetOnAxis(posu[:, g, k, j:j + 1], 0))\
                                .then_inc(d_yg[GB * g + b], 16)

        @block.scalar
        def _(act):
            def full(key):
                i, m = MISC[key]
                act.wait_ge(misc_full[i], m + 1)
                return misc_bank[i], misc_free[i]

            def load_weights(i):
                if i >= W_RING:
                    act.wait_ge(wlo_made, i - W_RING + 1)
                act.dma_start(w_st[:, i % W_RING, :], wall[i // 2, :, i % 2 * WH:(i % 2 + 1) * WH])\
                    .then_inc(d_w[i % W_RING], 16)

            def weights_high(i):
                act.wait_ge(d_w[i % W_RING], 16 * (i // W_RING + 1))
                nc.scalar.activation(w_hi[:, i // 2, i % 2 * WH:(i % 2 + 1) * WH], w_st[:, i % W_RING, :],
                                     ACT.Copy).then_inc(whi_made, 1)
                if i >= 1 and i + 1 < 2 * E:
                    load_weights(i + 1)

            act.dma_start(ctx_sb, ctx[:, 0:P, :].rearrange("n k d -> k n d")).then_inc(d_ctx, 16)
            load_weights(0)
            load_weights(1)

            act.wait_ge(d_const, 16)
            nc.scalar.activation(tanhg[:, :], cst[:, C_GX:C_GX + 2], ACT.Tanh).then_inc(tanh_made, 1)

            def copy_qT(n):
                src, free = full(("qT", n))
                if n >= 1:
                    i, m = MISC[("qB", n - 1)]
                    act.wait_ge(misc_full[i], m + 1)
                nc.scalar.activation(qT[:, :], src[:, :], ACT.Copy).then_inc(free, 1)

            def features(dst, src):
                return nc.scalar.activation(dst, src, ACT.Exp, bias=sgnb[:, :], scale=cst[:, C_SGN:C_SGN + 1])

            def exp_q(n, half):
                if n >= 1:
                    act.wait_ge(qp_made, 2 * n + half - 1)
                    act.wait_ge(d_qout[half], 16 * n)
                src, free = full(("qA" if half == 0 else "qB", n))
                features(f_q[:, half, :], src[:, :])
                features(qp[:, 0, half * T:(half + 1) * T], src[:, :]).then_inc(free, 1)

            def exp_k(r, lo, i):
                w = ZK_COLS[i]
                src, free = full(("zk", i))
                features(f_k[r][:, lo:lo + w], src[:, 0:w])
                features(kp[r][:, 0, lo:lo + w], src[:, 0:w]).then_inc(free, 1)

            weights_high(0)
            weights_high(1)
            src, free = full(("cT", 0))
            nc.scalar.activation(ctxT[:, :, 0:P], src[:, :].rearrange("p (n k) -> p n k", n=NB),
                                 ACT.Copy).then_inc(free, 1)
            src, free = full(("cT", 1))
            nc.scalar.activation(ctxT[:, :, P:SP_], src[:, 0:P].rearrange("p (n k) -> p n k", n=NB),
                                 ACT.Copy).then_inc(free, 1)
            act.wait_ge(sgnb_made, 1)
            exp_k(0, 0, 0)
            copy_qT(0)
            exp_q(0, 0)
            exp_q(0, 1)
            weights_high(2)
            exp_k(1, 0, 1)
            exp_k(1, ZK_COLS[1], 2)
            weights_high(3)
            copy_qT(1)
            i, m = MISC[("v", 0)]
            act.wait_ge(misc_free[i], m + 1)
            act.wait_ge(ones_made, 1)
            z = v_tmp.rearrange("p (n h e) -> p n h e", n=NB, h=H)
            for k, sg in enumerate((1.0, -1.0)):
                for n in range(NB):
                    ins = nc.scalar.activation(v_sb[:, n, :, k * HD:(k + 1) * HD], z[:, n, :, :], ACT.Exp, scale=sg)
                    ins.then_inc(v_made, 1)
            i, m = MISC[("v", 1)]
            act.wait_ge(misc_free[i], m + 1)
            act.wait_ge(vz_made, 1)
            z = v_tmr[:, 0:NB * NG * HD].rearrange("p (n g e) -> p n g e", n=NB, g=NG)
            for j in range(GH):
                for k, sg in enumerate((1.0, -1.0)):
                    rows = slice(RP * j, RP * j + SR)
                    nc.scalar.activation(v_rm[rows, :, :, RP * j + k * HD:RP * j + (k + 1) * HD],
                                         z[rows, :, :, :], ACT.Exp, scale=sg).then_inc(v_made, 1)
            exp_q(1, 0)
            exp_q(1, 1)

            def move_max(s):
                n, g = divmod(s, NG)
                src, free = full(("nm", s))
                if s >= 1:
                    act.wait_ge(d_nm, 16 * s)
                nc.scalar.activation(nmT[:, :], src[0:PARTS * GH, :].bitcast(BF16)[:, 0:T], ACT.Copy)\
                    .then_inc(free, 1)
                act.wait_ge(free, MISC[("nm", s)][1] + 1)
                act.dma_start(qs[KROWS:SROWS, n % 2, GH * g:GH * (g + 1), :], nmT[:, :]).then_inc(d_nm, 16)

            move_max(0)
            for s in range(1, AHEAD - 1):
                move_max(s)

            def probs(s, u):
                k = UNITS * s + u
                act.wait_ge(s_done, k + 1)
                if k >= P_RING:
                    act.wait_ge(pv_done, (k - P_RING) // UNITS + 1)
                nc.scalar.activation(prob[:, k % P_RING, :], s_bank[k % S_RING][:, :], ACT.Exp,
                                     scale=SCALE).then_inc(p_made, 1)

            def copy_out(s):
                act.wait_ge(pv_done, s + 1)
                n, g = divmod(s, NG)
                if s == 0:
                    for i in range(2):
                        act.wait_ge(d_kout[i], 16 * PARTS)
                if n >= 2:
                    i, m = MISC[("fc", n - 2)]
                    act.wait_ge(misc_full[i], m + 1)
                nc.scalar.activation(osum[:, n % 2, g, :], ot_bank[:, :], ACT.Copy).then_inc(o_made, 1)

            def copy_x2T(n):
                src, free = full(("xT", n))
                if n >= 1:
                    i, m = MISC[("lg", n - 1)]
                    act.wait_ge(misc_full[i], m + 1)
                    act.wait_ge(xh_made, n)
                nc.scalar.activation(x2T[:, :], src[:, :], ACT.Copy).then_inc(free, 1)

            def exp_gates(n):
                act.wait_ge(dl_made, n + 1)
                nc.scalar.activation(gex[:, :], dl[:, :], ACT.Exp).then_inc(gex_made, 1)

            def copy_gates(n):
                src, free = full(("gT", n))
                if n >= 2:
                    act.wait_ge(y_add, 2 * (n - 2) + 1)
                nc.scalar.activation(gT[n % 2], src[0:E_ROUTED + 1, :], ACT.Copy).then_inc(free, 1)

            def copy_biases(g):
                src, free = full(("bs", g))
                nc.scalar.activation(bsel[:, :, TILES * g:TILES * (g + 1)],
                                     src[:, 0:2 * HC * TILES].rearrange("p (c i) -> p c i", i=TILES),
                                     ACT.Copy).then_inc(free, 1)

            for s in range(SLOTS):
                n, g = divmod(s, NG)
                probs(s, 0)
                probs(s, 1)
                if s + AHEAD <= SLOTS:
                    move_max(s + AHEAD - 1)
                probs(s, 2)
                weights_high(2 * s + 4)
                probs(s, 3)
                if s >= 1:
                    copy_out(s - 1)
                probs(s, 4)
                if g == 0 and n + 2 < NB:
                    copy_qT(n + 2)
                if g == 1 and n + 2 < NB:
                    exp_q(n + 2, 0)
                    exp_q(n + 2, 1)
                if g == 1 and n >= 2:
                    copy_x2T(n - 2)
                if g == 3 and n >= 2:
                    exp_gates(n - 2)
                weights_high(2 * s + 5)
            copy_out(SLOTS - 1)

            act.wait_ge(s_done, UNITS * SLOTS)

            def silu(c, bias):
                nc.scalar.activation(sil[c], h1_bank[c][:, :], ACT.Silu, bias=bias).then_inc(sil_made, 1)

            def high(ring, c):
                nc.scalar.activation(hsp[:, 0, ring, c, :], hf[c], ACT.Copy).then_inc(hi_made, 1)

            def shared(u, e):
                for c in range(HC):
                    k = HC * u + c
                    act.wait_ge(h1_done, k + 1)
                    ge(act, hf_made, k - 1)
                    at = C_B1 + HC * e + c
                    silu(c, cst[:, at:at + 1])
                    if k >= 1:
                        act.wait_ge(hf_made, k)
                        high((k - 1) // HC % 2, (k - 1) % HC)

            def quad_high(q, ring):
                act.wait_ge(xt_done, q + 1)
                ge(act, xql_made, q - 1)
                ge(act, h2_done, 2 * q + (2 * UA - 2))
                nc.scalar.activation(xqs[:, 0, ring, :], misc_bank[1][:, :], ACT.Copy).then_inc(xqh_made, 1)

            def store(q, ring):
                act.wait_ge(y_done, q + (UA + 1))
                if not isinstance(q, int) or q >= 2:
                    act.wait_ge(d_yq[ring], (q - ring) * 8)
                nc.scalar.activation(yq[ring], y_bank[ring][:, :], ACT.Copy).then_inc(y_out, 1)

            def quad(q, ring, first=False, last=False):
                ge(act, sil_made, 2 * q + (2 * UA - 2))
                if isinstance(q, int) and q % QUADS == 0:
                    i, m = MISC[("bs", q // QUADS)]
                    act.wait_ge(misc_free[i], m + 1)
                nc.scalar.activation(b1q[:, ring, :, :], bsel[:, 0:HC, bass.ds(q * QUAD, QUAD)], ACT.Copy)\
                    .then_inc(b1_made, 1)
                act.wait_ge(b1_made, q + 1)
                for c in range(HC):
                    act.wait_ge(h1_done, 2 * q + (2 * UA + c + 1))
                    act.wait_ge(hf_made, 2 * q + (2 * UA + c - 1))
                    for t in range(QUAD):
                        cols = slice(t * P, (t + 1) * P)
                        ins = nc.scalar.activation(sil[c][:, cols], h1_bank[c][:, cols], ACT.Silu,
                                                   bias=b1q[:, ring, c, t:t + 1])
                    ins.then_inc(sil_made, 1)
                    if not (first and c == 0):
                        act.wait_ge(hf_made, 2 * q + (2 * UA + c))
                        high(ring if c else 1 - ring, 1 - c)
                if not last:
                    quad_high(q + 1, 1 - ring)
                if not first:
                    store(q - 1, 1 - ring)

            def routing(u):
                if u == 0:
                    copy_gates(0)
                if u == 2:
                    copy_gates(1)
                if u == 3:
                    copy_biases(0)
                if u == UA + 1:
                    copy_x2T(2)
                if u == UA + 3:
                    exp_gates(2)
                    copy_x2T(3)
                if u == UA + 5:
                    exp_gates(3)
                if u == UA + 7:
                    copy_biases(1)
                    copy_gates(2)
                    copy_gates(3)

            for u, (e, b) in enumerate(SHARED_A):
                routing(u)
                shared(u, e)
            act.wait_ge(hf_made, 2 * UA)
            high(1, 1)
            quad_high(0, 0)
            for q in range(ALLQ):
                routing(UA + q)
                quad(q, q % 2, first=q == 0, last=q + 1 == ALLQ)
            for i, (e, b) in enumerate(SHARED_B):
                shared(UA + ALLQ + i, e)
                if i == 0:
                    store(ALLQ - 1, 1)
            act.wait_ge(hf_made, 2 * (UA + ALLQ + len(SHARED_B)))
            high(1, 1)

        @block.vector
        def _(dve):
            chain = [0]

            def link(ins):
                chain[0] += 1
                ins.then_inc(v_chain, 1)
                dve.wait_ge(v_chain, chain[0])

            def full(key):
                i, m = MISC[key]
                dve.wait_ge(misc_full[i], m + 1)
                return misc_bank[i], misc_free[i]

            def layer_norm(kind, n):
                moments(kind, n)
                scale_rows(kind, n)

            def moments(kind, n):
                l = ln_index(kind, n)
                if kind == 1:
                    dve.wait_ge(d_x[n], 16)
                for t in range(NT):
                    ins = nc.vector.bn_stats(stats[:, l, t, :], xs[:, NT * n + t, :])
                link(ins)
                for t in range(NT):
                    ins = nc.vector.bn_aggr(mv[:, l, t, :], stats[:, l, t, :])
                link(ins)
                nc.vector.tensor_scalar(veps[:, l, :], mv[:, l, :, 1], EPS, None, ALU.add).then_inc(var_made, 1)

            def scale_rows(kind, n):
                l = ln_index(kind, n)
                dve.wait_ge(rstd_made, l + 1)
                if (kind, n) == (2, 2):
                    dve.wait_ge(pv_done, SLOTS)
                if l >= X_RING:
                    kind_, n_ = LN[l - X_RING]
                    i, m = MISC[("qT" if kind_ == 1 else "xT", n_)]
                    dve.wait_ge(misc_full[i], m + 1)
                for t in range(NT):
                    ins = nc.vector.tensor_scalar(xhat_tile(kind, n)[:, t, :], xs[:, NT * n + t, :], mv[:, l, t, 0:1],
                                                  rstd[:, l, t:t + 1], ALU.subtract, ALU.mult)
                ins.then_inc(xhat_made, 1)

            def split_rest(src, parts):
                link(nc.vector.tensor_tensor(src, src, parts[0], ALU.subtract))
                link(nc.vector.tensor_copy(parts[1], src))
                return nc.vector.tensor_tensor(parts[2], src, parts[1], ALU.subtract)

            def first_queries(half):
                i, m = MISC[("qB" if half else "qA", 0)]
                dve.wait_ge(misc_free[i], m + 1)
                dve.wait_ge(d_ones, 16 * PARTS)
                split_rest(f_q[:, half, :], [qp[:, c, half * T:(half + 1) * T] for c in range(PARTS)])\
                    .then_inc(qp_made, 1)

            def second_part(n):
                for half in range(2):
                    dve.wait_ge(qr_made, 2 * n + half - 1)
                    nc.vector.tensor_copy(qp[:, 1, half * T:(half + 1) * T], f_q[:, half, :]).then_inc(qp1_made, 1)

            def split_keys(r):
                for i in ((0,), (1, 2))[r]:
                    b, m = MISC[("zk", i)]
                    dve.wait_ge(misc_free[b], m + 1)
                link(split_rest(f_k[r], [kp[r][:, c, :] for c in range(PARTS)]))
                n0, n1 = K_ROUNDS[r]
                pad = kp[r].rearrange("p c (m k) -> p c m k", k=SP_)[:, :, :, S:SP_]
                nc.vector.memset(pad, 0.0).then_inc(kp_made, 1)

            nc.vector.memset(ctx_rm, 0.0).then_inc(z_rem, 1)
            link(nc.vector.memset(v_rm[:, :, :, :], 0.0))
            for j in range(GH):
                ins = nc.vector.memset(v_rm[RP * j:RP * j + SR, :, :, RP * j + FD:RP * (j + 1)], 1.0)
            ins.then_inc(vz_made, 1)
            dve.wait_ge(d_const, 16)
            nc.vector.tensor_tensor(bd[:, :, :, :].rearrange("p h s e -> p h s e"),
                                    cst[:, C_MASK:C_MASK + H].rearrange("p (h s e) -> p h s e", s=1, e=1)
                                    .to_broadcast([P, H, 2, HD]),
                                    cst[:, C_FM:C_FM + HD].rearrange("p (h s e) -> p h s e", h=1, s=1)
                                    .to_broadcast([P, H, 2, HD]), ALU.mult).then_inc(bd_made, 1)
            nc.vector.tensor_tensor(sgnb[:, :], cst[:, C_FMB:C_FMB + 1], cst[:, C_SGN:C_SGN + 1],
                                    ALU.mult).then_inc(sgnb_made, 1)
            nc.vector.tensor_copy(ident16[:, :], ident).then_inc(ident16_made, 1)
            layer_norm(1, 0)
            split_keys(0)
            first_queries(0)
            first_queries(1)
            src, free = full(("v", 0))
            vb = cst[:, C_FMBV:C_FMBV + HD].rearrange("p (m e) -> p m e", m=1).to_broadcast([P, NB * H, HD])
            nc.vector.tensor_tensor(v_tmp.rearrange("p (m e) -> p m e", e=HD),
                                    src[:, :].rearrange("p (m e) -> p m e", e=HD), vb, ALU.add)\
                .then_inc(free, 1)
            src, free = full(("v", 1))
            vb = cst[:, C_FMBV:C_FMBV + HD].rearrange("p (m e) -> p m e", m=1).to_broadcast([P, NB * NG, HD])
            nc.vector.tensor_tensor(v_tmr[:, 0:NB * NG * HD].rearrange("p (m e) -> p m e", e=HD),
                                    src[:, 0:NB * NG * HD].rearrange("p (m e) -> p m e", e=HD), vb, ALU.add)\
                .then_inc(free, 1)

            layer_norm(1, 1)
            split_keys(1)

            def row_max(m):
                i = m % MAXU
                at, w = sum(MAX_BLOCKS[:i]), MAX_BLOCKS[i]
                dve.wait_ge(max_done, m + 1)
                nc.vector.reduce_max(mxf[:, at:at + w],
                                     mx_bank[m % 2][:, 0:w * S].rearrange("p (h k) -> p h k", h=w), AX_X)\
                    .then_inc(max_read, 1)

            def split_max(s):
                dve.wait_ge(max_read, MAXU * (s + 1))
                if s >= 1:
                    i, m = MISC[("nm", s - 1)]
                    dve.wait_ge(misc_full[i], m + 1)
                link(nc.vector.tensor_scalar(nm[:, :, 0, :], mx[:, :, :], -1.0, None, ALU.mult))
                link(nc.vector.scalar_tensor_tensor(out=nm_r[:, :, :], in0=mx[:, :, :], scalar=-1.0,
                                                    in1=nm[:, :, 0, :], op0=ALU.mult, op1=ALU.subtract))
                link(nc.vector.tensor_copy(nm[:, :, 1, :], nm_r[:, :, :]))
                nc.vector.tensor_tensor(nm[:, :, 2, :], nm_r[:, :, :], nm[:, :, 1, :],
                                        ALU.subtract).then_inc(nm_made, 1)

            def maxima(s, half):
                for m in range(MAXU * s + MAXU * half // 2, MAXU * s + MAXU * (half + 1) // 2):
                    row_max(m)
                if half == 1:
                    split_max(s)

            for s in range(AHEAD):
                maxima(s, 0)
                maxima(s, 1)
            second_part(1)
            dve.wait_ge(d_tri, 16)
            nc.vector.tensor_copy(tri16[:, :], den[:, 1, 0:P]).then_inc(tri_made, 1)
            moments(1, 2)

            def reciprocals(n):
                dve.wait_ge(d_dn[1], 16 * (n + 1))
                if n >= 1:
                    dve.wait_ge(d_dn[2], 16 * n)
                nc.vector.reciprocal(dn[:, 1, :], dn[:, 0, :]).then_inc(rec_made, 1)

            def spread(n, groups):
                dve.wait_ge(d_dn[3], 16 * (n + 1))
                if n == 0:
                    dve.wait_ge(d_fill, 16 * GROUPS)
                    dve.wait_ge(tri_made, 1)
                for g in groups:
                    k = NG * n + g
                    if n + 1 == NB:
                        dve.wait_ge(pv_done, SLOTS)
                    elif k >= 2:
                        dve.wait_ge(on_made, k - 1)
                    nc.vector.stream_shuffle(den_tile(n, g), osum[:, n % 2, g, :],
                                             [FD] * (2 * FD)).then_inc(den_made, 1)

            def add_attention(n):
                src, free = full(("fc", n))
                dve.wait_ge(tanh_made, 1)
                rows = xs[:, NT * n:NT * (n + 1), :].rearrange("p t d -> p (t d)")
                ins = nc.vector.scalar_tensor_tensor(out=rows, in0=src[:, :], scalar=tanhg[:, 0:1], in1=rows,
                                                     op0=ALU.mult, op1=ALU.add)
                ins.then_inc(free, 1)
                dve.wait_ge(free, MISC[("fc", n)][1] + 1)

            def split_x2(n):
                i, m = MISC[("xT", n)]
                dve.wait_ge(misc_free[i], m + 1)
                cols = slice(n * T, (n + 1) * T)
                link(nc.vector.tensor_copy(xh[:, cols], x2T[:, :]))
                nc.vector.tensor_tensor(xl[:, cols], x2T[:, :], xh[:, cols], ALU.subtract).then_inc(xh_made, 1)

            def route(n):
                src, free = full(("lg", n))
                if n == 0:
                    for a in range(2):
                        dve.wait_ge(d_qout[a], 16 * NB)
                    dve.wait_ge(qp_made, 2 * NB)
                    i, m = MISC[("qB", NB - 1)]
                    dve.wait_ge(misc_full[i], m + 1)
                nc.vector.tensor_copy(lg[:, :, :], src[:, 0:NT * E_ROUTED].rearrange("p (t e) -> p t e", t=NT))\
                    .then_inc(free, 1)
                dve.wait_ge(free, MISC[("lg", n)][1] + 1)
                for t in range(NT):
                    ins = nc.vector.max(top[:, t, :], lg[:, t, :])
                link(ins)
                if n >= 1:
                    dve.wait_ge(gex_made, n)
                nc.vector.tensor_tensor(dl[:, :], top[:, :, 1], top[:, :, 0], ALU.subtract).then_inc(dl_made, 1)
                for t in range(NT):
                    ins = nc.vector.max_index(idx[:, t, :], top[:, t, :], lg[:, t, :])
                link(ins)
                link(nc.vector.tensor_copy(idf[:, :, :], idx[:, :, :]))
                iota = cst[:, C_IOTA:C_IOTA + E_ROUTED].rearrange("p (t e) -> p t e", t=1)\
                    .to_broadcast([P, NT, E_ROUTED])
                for i in range(2):
                    ins = nc.vector.tensor_tensor(oh[:, i, NT * n:NT * (n + 1), :], iota,
                                                  idf[:, :, i:i + 1].to_broadcast([P, NT, E_ROUTED]), ALU.is_equal)
                link(ins)

            def gates(n):
                tiles = slice(NT * n, NT * (n + 1))
                dve.wait_ge(gex_made, n + 1)
                if n == 0:
                    link(nc.vector.memset(gts[:, :, E_ROUTED:E_ROUTED + 1], 1.0))
                link(nc.vector.tensor_scalar(gsum[:, 0, :], gex[:, :], 1.0, None, ALU.add))
                link(nc.vector.reciprocal(gk[:, tiles, 0], gsum[:, 0, :]))
                link(nc.vector.tensor_tensor(gk[:, tiles, 1], gex[:, :], gk[:, tiles, 0], ALU.mult))
                nc.vector.tensor_scalar(gkt[:, tiles, :], gk[:, tiles, :], tanhg[:, 1:2], None, ALU.mult)

                def share(i):
                    return gk[:, tiles, i:i + 1].to_broadcast([P, NT, E_ROUTED])

                nc.vector.tensor_tensor(gtmp, oh[:, 0, tiles, :], share(0), ALU.mult)
                link(nc.vector.tensor_tensor(gts[:, tiles, 0:E_ROUTED], oh[:, 1, tiles, :], share(1), ALU.mult))
                nc.vector.tensor_tensor(gts[:, tiles, 0:E_ROUTED], gts[:, tiles, 0:E_ROUTED], gtmp, ALU.add)\
                    .then_inc(gts_made, 1)
                dve.wait_ge(gts_made, n + 1)

            def members(g):
                if g == 0:
                    nc.vector.memset(member[:, GJ, :], 0.0)
                tiles = slice(GJ * g, GJ * (g + 1))
                nc.vector.tensor_tensor(member[:, 0:GJ, :], oh[:, 0, tiles, :], oh[:, 1, tiles, :], ALU.add)\
                    .then_inc(member_made, 1)

            def positions(g):
                iota = cst[:, C_IOTA:C_IOTA + 32]
                if g == 0:
                    link(nc.vector.tensor_tensor(
                        below, iota[:, 0:E_ROUTED].rearrange("p (e f) -> p e f", f=1).to_broadcast([P, E_ROUTED, E_ROUTED]),
                        iota[:, 0:E_ROUTED].rearrange("p (e f) -> p e f", e=1).to_broadcast([P, E_ROUTED, E_ROUTED]),
                        ALU.is_gt))
                src, free = full(("pf", g))
                nc.vector.tensor_copy(pref, src[:, 0:(GJ + 1) * E_ROUTED].rearrange("p (j e) -> p j e", j=GJ + 1))\
                    .then_inc(free, 1)
                dve.wait_ge(free, MISC[("pf", g)][1] + 1)
                link(nc.vector.tensor_scalar(btile[:, 0, :], pref[:, GJ, :], 1.0 / P, None, ALU.mult))
                c3 = cmp_[:, 0:CMAX * E_ROUTED].rearrange("p (e m) -> p e m", m=CMAX)
                link(nc.vector.tensor_tensor(
                    c3, btile[:, 0, :].rearrange("p (e m) -> p e m", m=1).to_broadcast([P, E_ROUTED, CMAX]),
                    iota[:, 0:CMAX].rearrange("p (e m) -> p e m", e=1).to_broadcast([P, E_ROUTED, CMAX]), ALU.is_gt))
                link(nc.vector.reduce_sum(btile[:, 1, :], c3, AX_X))
                c3 = cmp_[:, 0:E_ROUTED ** 2].rearrange("p (e f) -> p e f", e=E_ROUTED)
                link(nc.vector.tensor_tensor(
                    c3, below, btile[:, 1, :].rearrange("p (e f) -> p e f", e=1).to_broadcast([P, E_ROUTED, E_ROUTED]),
                    ALU.mult))
                link(nc.vector.reduce_sum(btile[:, 2, :], c3, AX_X))
                link(nc.vector.scalar_tensor_tensor(
                    out=slot0, in0=btile[:, 2, :].rearrange("p (j e) -> p j e", j=1).to_broadcast([P, GJ, E_ROUTED]),
                    scalar=float(P), in1=pref[:, 0:GJ, :], op0=ALU.mult, op1=ALU.add))
                tiles = slice(GJ * g, GJ * (g + 1))
                c3 = cmp_[:, 0:2 * GJ * E_ROUTED].rearrange("p (k j e) -> p k j e", k=2, e=E_ROUTED)
                for k in range(2):
                    ins = nc.vector.tensor_tensor(c3[:, k, :, :], slot0, oh[:, k, tiles, :], ALU.mult)
                link(ins)
                for k in range(2):
                    ins = nc.vector.reduce_sum(posf[:, k, :], c3[:, k, :, :], AX_X)
                link(ins)
                nc.vector.tensor_copy(posu[:, g, :, :], posf[:, :, :]).then_inc(pos_made, 1)
                dve.wait_ge(pos_made, g + 1)
                link(nc.vector.tensor_tensor(btile[:, 3, :], btile[:, 1, :], btile[:, 2, :], ALU.add))
                c3 = cmp_[:, 0:TILES * E_ROUTED].rearrange("p (i e) -> p i e", e=E_ROUTED)
                link(nc.vector.tensor_tensor(
                    c3, iota[:, 0:TILES].rearrange("p (i e) -> p i e", e=1).to_broadcast([P, TILES, E_ROUTED]),
                    btile[:, 3, :].rearrange("p (i e) -> p i e", i=1).to_broadcast([P, TILES, E_ROUTED]), ALU.is_ge))
                link(nc.vector.reduce_sum(exf[:, :], c3, AX_X))
                link(nc.vector.tensor_scalar(exf[:, :], exf[:, :], float(E_ROUTED - 1), None, ALU.min))
                nc.vector.tensor_copy(exu[0:1, TILES * g:TILES * (g + 1)], exf[0:1, :])
                if g >= 1:
                    i, m = MISC[("bs", g - 1)]
                    dve.wait_ge(misc_full[i], m + 1)
                nc.vector.tensor_scalar(exT[:, :], exf[0:E_ROUTED, :], cst[0:E_ROUTED, C_PART:C_PART + 1], None,
                                        ALU.is_equal).then_inc(ext_made, 1)
                dve.wait_ge(ext_made, g + 1)

            for s in range(SLOTS):
                n, g = divmod(s, NG)
                if s + AHEAD < SLOTS:
                    maxima(s + AHEAD, 0)
                if s == 0:
                    scale_rows(1, 2)
                if g == 1 and n >= 2:
                    scale_rows(2, n - 2)
                if g == 2 and n >= 2:
                    split_x2(n - 2)
                if g == 1 and n >= 1:
                    reciprocals(n - 1)
                if g == 3 and n >= 1:
                    spread(n - 1, (2, 3))
                if s + AHEAD < SLOTS:
                    maxima(s + AHEAD, 1)
                if g == 0 and n >= 2:
                    add_attention(n - 2)
                    moments(2, n - 2)
                if g == 2:
                    if n >= 1:
                        spread(n - 1, (0, 1))
                    if n + 2 < NB:
                        second_part(n + 2)
                    if n >= 2:
                        route(n - 2)
                    if n + 3 < NB:
                        moments(1, n + 3)
                    if n == 3:
                        members(0)
                if g == 3:
                    if n + 3 < NB:
                        scale_rows(1, n + 3)
                    if n >= 2:
                        gates(n - 2)
                    if n == 3:
                        positions(0)
            add_attention(2)
            moments(2, 2)

            def low(ring, c):
                nc.vector.tensor_tensor(hsp[:, 1, ring, c, :], hf[c], hsp[:, 0, ring, c, :],
                                        ALU.subtract).then_inc(lo_made, 1)

            def shared(u, e):
                for c in range(HC):
                    k = HC * u + c
                    dve.wait_ge(sil_made, k + 1)
                    dve.wait_ge(h2_done, k + 1)
                    ge(dve, lo_made, k - 1)
                    at = C_B11 + HC * e + c
                    nc.vector.scalar_tensor_tensor(out=hf[c], in0=h2_bank[c][:, :], scalar=cst[:, at:at + 1],
                                                   in1=sil[c], op0=ALU.add, op1=ALU.mult).then_inc(hf_made, 1)
                    if k >= 1:
                        dve.wait_ge(hi_made, k)
                        low((k - 1) // HC % 2, (k - 1) % HC)

            def add_shared(u, b, k):
                dve.wait_ge(y_done, u + 1)
                rows = xs[:, NT * b:NT * (b + 1), :].rearrange("p t d -> p (t d)")
                nc.vector.scalar_tensor_tensor(out=rows, in0=y_bank[u % 2][:, :], scalar=tanhg[:, 1:2], in1=rows,
                                               op0=ALU.mult, op1=ALU.add).then_inc(y_add, 1)
                dve.wait_ge(y_add, k + 1)

            def quad_low(q, ring):
                dve.wait_ge(xqh_made, q + 1)
                nc.vector.tensor_tensor(xqs[:, 1, ring, :], misc_bank[1][:, :], xqs[:, 0, ring, :], ALU.subtract)\
                    .then_inc(xql_made, 1)

            def quad(q, ring, first=False, last=False):
                for c in range(HC):
                    dve.wait_ge(sil_made, 2 * q + (2 * UA + c + 1))
                    dve.wait_ge(h2_done, 2 * q + (2 * UA + c + 1))
                    dve.wait_ge(lo_made, 2 * q + (2 * UA + c - 1))
                    for t in range(QUAD):
                        cols = slice(t * P, (t + 1) * P)
                        ins = nc.vector.scalar_tensor_tensor(out=hf[c][:, cols], in0=h2_bank[c][:, cols],
                                                             scalar=bsel[:, HC + c, bass.ds(q * QUAD + t, 1)],
                                                             in1=sil[c][:, cols], op0=ALU.add, op1=ALU.mult)
                    ins.then_inc(hf_made, 1)
                    if not (first and c == 0):
                        dve.wait_ge(hi_made, 2 * q + (2 * UA + c))
                        low(ring if c else 1 - ring, 1 - c)
                if not last:
                    quad_low(q + 1, 1 - ring)

            def combine(b):
                g, at = divmod(b, GB)
                dve.wait_ge(d_yg[b], 16 * 2 * NT)
                for k in range(2):
                    for t in range(NT):
                        j = NT * b + t
                        ins = nc.vector.scalar_tensor_tensor(out=xs[:, j, :], in0=yg[g][:, k, NT * at + t, :],
                                                             scalar=gkt[:, j, k:k + 1], in1=xs[:, j, :],
                                                             op0=ALU.mult, op1=ALU.add)
                    if k == 0:
                        link(ins)
                ins.then_inc(fin_made, 1)

            def routing(u):
                if u == 2:
                    reciprocals(3)
                if u == UA:
                    scale_rows(2, 2)
                    spread(3, range(NG))
                if u == UA + 1:
                    split_x2(2)
                    add_attention(3)
                    moments(2, 3)
                if u == UA + 2:
                    scale_rows(2, 3)
                    route(2)
                if u == UA + 4:
                    gates(2)
                    route(3)
                    members(1)
                if u == UA + 5:
                    positions(1)
                if u == UA + 6:
                    gates(3)
                    split_x2(3)
                if u in (UA + QUADS + 5, UA + QUADS + 6):
                    combine(u - (UA + QUADS + 5))

            for u, (e, b) in enumerate(SHARED_A):
                routing(u)
                shared(u, e)
                if u >= 1:
                    add_shared(u - 1, SHARED_A[u - 1][1], u - 1)
            dve.wait_ge(hi_made, 2 * UA)
            low(1, 1)
            add_shared(UA - 1, SHARED_A[UA - 1][1], UA - 1)
            for q in range(ALLQ):
                routing(UA + q)
                if q == 0:
                    quad_low(0, 0)
                quad(q, q % 2, first=q == 0, last=q + 1 == ALLQ)
            for i, (e, b) in enumerate(SHARED_B):
                u = UA + ALLQ + i
                shared(u, e)
                if i + 1 == len(SHARED_B):
                    dve.wait_ge(hi_made, 2 * (u + 1))
                    low(1, 1)
                if i >= 1:
                    add_shared(u - 1, SHARED_B[i - 1][1], UA + i - 1)
            combine(2)
            u = UA + ALLQ + len(SHARED_B)
            add_shared(u - 1, NB - 1, UA + len(SHARED_B) - 1)
            combine(3)

        @block.tensor
        def _(pe):
            def claim(key):
                i, m = MISC[key]
                if m >= 1:
                    pe.wait_ge(misc_free[i], m)
                return misc_bank[i], misc_full[i]

            def xhat_T(kind, n):
                l = ln_index(kind, n)
                dst, full = claim(("qT" if kind == 1 else "xT", n))
                pe.wait_ge(xhat_made, l + 1)
                for t in range(NT):
                    mm = nc.tensor.transpose(dst[:, t * P:(t + 1) * P], xhat_tile(kind, n)[:, t, :], ident)
                mm.then_inc(full, 1)
                return full

            def q_T(n):
                xhat_T(1, n)

            def q_features(n, half):
                dst, full = claim(("qA" if half == 0 else "qB", n))
                i, m = MISC[("qT", n)]
                pe.wait_ge(misc_free[i], m + 1)
                pe.wait_ge(bd_made, 1)
                nc.tensor.matmul(dst[:, :], bdz[:, half * P:(half + 1) * P], qT[:, :],
                                 start=True, stop=True).then_inc(full, 1)

            pe.wait_ge(d_const, 16)
            dst, full = claim(("cT", 0))
            pe.wait_ge(d_ctx, 16 * (1 + NB))
            for n in range(NB):
                mm = nc.tensor.transpose(dst[:, n * P:(n + 1) * P], ctx_sb[:, n, :], ident)
            mm.then_inc(full, 1)
            dst, full = claim(("cT", 1))
            nc.tensor.transpose(dst[:, 0:P], ctx_rm, ident).then_inc(full, 1)
            for k in range(2):
                i, m = MISC[("cT", k)]
                pe.wait_ge(misc_free[i], m + 1)
            pe.wait_ge(bd_made, 1)

            def keys_z(dst, at, half, n0, n1):
                return nc.tensor.matmul(dst[:, at:at + (n1 - n0) * SP_], bdz[:, half * P:(half + 1) * P],
                                        ctxT.rearrange("p n k -> p (n k)")[:, n0 * SP_:n1 * SP_],
                                        start=True, stop=True)

            dst, full = claim(("zk", 0))
            keys_z(dst, 0, 0, *K_ROUNDS[0])
            keys_z(dst, SP_, 1, *K_ROUNDS[0]).then_inc(full, 1)
            q_T(0)
            q_features(0, 0)
            q_features(0, 1)
            for half in range(2):
                dst, full = claim(("zk", 1 + half))
                keys_z(dst, 0, half, *K_ROUNDS[1]).then_inc(full, 1)
            dst, full = claim(("v", 0))
            for n in range(NB):
                mm = nc.tensor.matmul(dst[:, n * P:(n + 1) * P], ctxT[:, n, 0:P], bd[:, :, 0, :],
                                      start=True, stop=True)
            mm.then_inc(full, 1)
            dst, full = claim(("v", 1))
            for n in range(NB):
                for j in range(GH):
                    mm = nc.tensor.matmul(dst[RP * j:RP * (j + 1), n * NG * HD:(n + 1) * NG * HD], ctxT[:, n, P:SP_],
                                          bd[:, j:H:GH, 0, :], start=True, stop=True)
            mm.then_inc(full, 1)
            q_T(1)

            def max_unit(m):
                s, i = divmod(m, MAXU)
                n, g = divmod(s, NG)
                if i == 0 and g % 2 == 0:
                    pe.wait_ge(d_qin[n % 2][g // 2], 16 * len(Q_TERMS) * (n // 2 + 1))
                if i == 0 and s in (0, NG):
                    pe.wait_ge(d_kin[s // NG], 16 * len(K_TERMS))
                if m >= 2:
                    pe.wait_ge(max_read, m - 1)
                for j in range(MAX_BLOCKS[i]):
                    t, h = divmod(sum(MAX_BLOCKS[:i]) + j, GH)
                    h += GH * g
                    mm = nc.tensor.matmul(mx_bank[m % 2][:, j * S:(j + 1) * S],
                                          qs[0:KROWS, n % 2, h, t * P:(t + 1) * P],
                                          ks[0:KROWS, h, n, 0:S], start=True, stop=True)
                mm.then_inc(max_done, 1)

            def max_T(s):
                dst, full = claim(("nm", s))
                pe.wait_ge(nm_made, s + 1)
                pe.wait_ge(ident16_made, 1)
                for t in range(NT):
                    mm = nc.tensor.transpose(dst[0:PARTS * GH, :].bitcast(BF16)[:, t * P:(t + 1) * P],
                                             nm[:, t, :, :].rearrange("p c h -> p (c h)"), ident16[:, :])
                mm.then_inc(full, 1)

            q_features(1, 0)
            q_features(1, 1)
            for m in range(MAXU):
                max_unit(m)
            max_T(0)
            for s in range(1, AHEAD):
                for m in range(MAXU * s, MAXU * (s + 1)):
                    max_unit(m)
                if s + 1 < AHEAD:
                    max_T(s)
            pe.wait_ge(d_ones, 16 * PARTS)

            def scores(s, u):
                n, g = divmod(s, NG)
                k = UNITS * s + u
                if k >= S_RING:
                    pe.wait_ge(p_made, k - S_RING + 1)
                dst = s_bank[k % S_RING]
                if u < GH:
                    h = GH * g + u
                    mm = nc.tensor.matmul(dst[:, :], ks[0:SROWS, h, n, 0:P], qs[0:SROWS, n % 2, h, :],
                                          start=True, stop=True)
                else:
                    for j in range(GH):
                        h = GH * g + j
                        mm = nc.tensor.matmul(dst[RP * j:RP * (j + 1), :], ks[0:SROWS, h, n, P:SP_],
                                              qs[0:SROWS, n % 2, h, :], start=True, stop=True)
                mm.then_inc(s_done, 1)

            def weighted(s):
                n, g = divmod(s, NG)
                k = UNITS * s
                pe.wait_ge(p_made, k + UNITS)
                if s == 0:
                    pe.wait_ge(v_made, V_OPS)
                    pe.wait_ge(ones_made, 1)
                if s >= 1:
                    pe.wait_ge(o_made, s)
                nc.tensor.matmul(ot_bank[:, :], v_rm[:, n, g, :], prob[:, (k + GH) % P_RING, :],
                                 start=True, stop=False, skip_group_check=True)

            def weighted_rest(s):
                n, g = divmod(s, NG)
                k = UNITS * s
                for j in range(GH):
                    mm = nc.tensor.matmul(ot_bank[RP * j:RP * (j + 1), :], v_sb[:, n, GH * g + j, :],
                                          prob[:, (k + j) % P_RING, :], start=False, stop=True,
                                          skip_group_check=True)
                mm.then_inc(pv_done, 1)

            def project(n):
                dst, full = claim(("fc", n))
                pe.wait_ge(on_made, NG * (n + 1))
                pe.wait_ge(d_fc, 16)
                for t in range(NT):
                    for g in range(NG):
                        nc.tensor.matmul(dst[:, t * P:(t + 1) * P], osum[:, n % 2, g, t * P:(t + 1) * P],
                                         fc_sb[:, g, :], start=(g == 0), stop=False)
                    mm = nc.tensor.matmul(dst[:, t * P:(t + 1) * P], one_row, fc_sb[0:1, NG, :],
                                          start=False, stop=True)
                mm.then_inc(full, 1)

            def logits(n):
                dst, full = claim(("lg", n))
                i, m = MISC[("xT", n)]
                pe.wait_ge(misc_free[i], m + 1)
                for t in range(NT):
                    mm = nc.tensor.matmul(dst[:, t * E_ROUTED:(t + 1) * E_ROUTED], x2T[:, t * P:(t + 1) * P],
                                          cst[:, C_WG:C_WG + E_ROUTED], start=True, stop=True)
                mm.then_inc(full, 1)

            def gates_T(n):
                dst, full = claim(("gT", n))
                pe.wait_ge(gts_made, n + 1)
                for t in range(NT):
                    mm = nc.tensor.transpose(dst[0:E_ROUTED + 1, t * P:(t + 1) * P], gts[:, NT * n + t, :], ident)
                mm.then_inc(full, 1)

            def prefix(g):
                dst, full = claim(("pf", g))
                pe.wait_ge(member_made, g + 1)
                pe.wait_ge(tri_made, 1)
                pe.wait_ge(ones16_made, 1)
                rows = member.rearrange("p j e -> p (j e)")
                n = (GJ + 1) * E_ROUTED
                nc.tensor.matmul(dst[:, 0:n], tri16[:, :], rows, start=True, stop=False, skip_group_check=True)
                for d in range(1, GJ + 1):
                    mm = nc.tensor.matmul(dst[:, d * E_ROUTED:n], ones16[:, :], rows[:, 0:n - d * E_ROUTED],
                                          start=False, stop=d == GJ, skip_group_check=True)
                mm.then_inc(full, 1)

            def biases(g):
                dst, full = claim(("bs", g))
                pe.wait_ge(ext_made, g + 1)
                pe.wait_ge(d_brow, 16)
                for c in range(2 * HC):
                    mm = nc.tensor.matmul(dst[:, c * TILES:(c + 1) * TILES], bTs[:, c * P:(c + 1) * P], exT[:, :],
                                          start=True, stop=True)
                mm.then_inc(full, 1)

            m = AHEAD * MAXU
            for s in range(SLOTS):
                n, g = divmod(s, NG)
                pe.wait_ge(d_nm, 16 * (s + 1))

                def maximum():
                    nonlocal m
                    if s + AHEAD < SLOTS:
                        max_unit(m)
                        m += 1

                scores(s, 0)
                maximum()
                scores(s, 1)
                maximum()
                if s + AHEAD <= SLOTS:
                    max_T(s + AHEAD - 1)
                scores(s, 2)
                if s >= 1:
                    weighted(s - 1)
                maximum()
                scores(s, 3)
                maximum()
                if s >= 1:
                    weighted_rest(s - 1)
                maximum()
                if s + 1 == SLOTS:
                    prefix(0)
                if g == 0 and n >= 2:
                    project(n - 2)
                if g == 1 and n >= 2:
                    xhat_T(2, n - 2)
                if g == 2 and n >= 2:
                    logits(n - 2)
                scores(s, 4)
                if g == 0 and n + 2 < NB:
                    q_T(n + 2)
                if g == 1 and n + 2 < NB:
                    q_features(n + 2, 0)
                    q_features(n + 2, 1)
                maximum()
            weighted(SLOTS - 1)
            weighted_rest(SLOTS - 1)
            project(2)

            pe.wait_ge(wlo_made, 2 * E)
            pe.wait_ge(p_made, UNITS * SLOTS)
            pe.wait_ge(o_made, SLOTS)
            pe.wait_ge(d_b2, 16)

            def three(dst, w_col, e, x_hi, x_lo, start, stop):
                hi = w_hi[:, e, w_col:w_col + P]
                lo = w_lo[:, e, w_col:w_col + P]
                nc.tensor.matmul(dst, hi, x_hi, start=start, stop=False)
                nc.tensor.matmul(dst, hi, x_lo, start=False, stop=False)
                return nc.tensor.matmul(dst, lo, x_hi, start=False, stop=stop)

            def up_shared(u, e, b):
                pe.wait_ge(xh_made, b + 1)
                x_hi, x_lo = xh[:, b * T:(b + 1) * T], xl[:, b * T:(b + 1) * T]
                for c in range(HC):
                    ge(pe, hf_made, HC * u + c - 1)
                    three(h1_bank[c][:, :], c * P, e, x_hi, x_lo, True, True).then_inc(h1_done, 1)
                    three(h2_bank[c][:, :], HID + c * P, e, x_hi, x_lo, True, True).then_inc(h2_done, 1)

            def down_tile(dst, ring, t, e, start):
                cols = slice(t * P, (t + 1) * P)
                for c in range(HC):
                    at = 2 * HID + c * P
                    hi, lo = hsp[:, 0, ring, c, cols], hsp[:, 1, ring, c, cols]
                    nc.tensor.matmul(dst, hi, w_hi[:, e, at:at + P], start=start and c == 0, stop=False)
                    nc.tensor.matmul(dst, hi, w_lo[:, e, at:at + P], start=False, stop=False)
                    mm = nc.tensor.matmul(dst, lo, w_hi[:, e, at:at + P], start=False, stop=c == HC - 1)
                return mm

            def down_shared(u, e, b, bank_sem, bank_count):
                ge(pe, bank_sem, bank_count)
                pe.wait_ge(lo_made, HC * (u + 1))
                if e == 0:
                    i, m = MISC[("gT", b)]
                    pe.wait_ge(misc_free[i], m + 1)
                for t in range(NT):
                    dst = y_bank[u % 2][:, t * P:(t + 1) * P]
                    if e == 0:
                        nc.tensor.matmul(dst, gT[b % 2][:, t * P:(t + 1) * P], b2r[:, :], start=True, stop=False)
                    mm = down_tile(dst, u % 2, t, e, e == 1)
                mm.then_inc(y_done, 1)

            def quad_T(q, ring):
                pe.wait_ge(d_xq[ring], (q + (2 - ring)) * 8)
                if q == 0:
                    pe.wait_ge(misc_free[1], SECOND_USES)
                else:
                    pe.wait_ge(xql_made, q)
                for t in range(QUAD):
                    mm = nc.tensor.transpose(misc_bank[1][:, t * P:(t + 1) * P], xq[ring][:, t * P:(t + 1) * P],
                                             ident)
                mm.then_inc(xt_done, 1)

            expert = {}

            def load_experts(q):
                _, values = nc.values_load_multi_w_load_instructions(
                    exu[0:1, QUAD * q:QUAD * (q + 1)], engines=(mybir.EngineType.PE,), min_val=0,
                    max_val=E_ROUTED - 1,
                    skip_runtime_bounds_check_because="VectorE counts from zero and takes the least of this and the last")
                for t in range(QUAD):
                    expert[q, t] = values[t]

            def weights(w, q, t, at):
                return w[:, bass.ds(expert[q, t] + 2, 1), at:at + P].rearrange("p e w -> p (e w)")

            def up_quad(q):
                ring = q % 2
                pe.wait_ge(xql_made, q + 1)
                for c in range(HC):
                    pe.wait_ge(hf_made, 2 * q + (2 * UA + c - 1))
                    for bank, at, done in ((h1_bank[c], c * P, h1_done), (h2_bank[c], HID + c * P, h2_done)):
                        for t in range(QUAD):
                            cols = slice(t * P, (t + 1) * P)
                            hi, lo = weights(w_hi, q, t, at), weights(w_lo, q, t, at)
                            nc.tensor.matmul(bank[:, cols], hi, xqs[:, 0, ring, cols], start=True, stop=False)
                            nc.tensor.matmul(bank[:, cols], hi, xqs[:, 1, ring, cols], start=False, stop=False)
                            mm = nc.tensor.matmul(bank[:, cols], lo, xqs[:, 0, ring, cols], start=False, stop=True)
                        mm.then_inc(done, 1)

            def down_quad(q, ahead):
                ring = q % 2
                if q < 2:
                    pe.wait_ge(y_add, UA - 1 + ring)
                else:
                    pe.wait_ge(y_out, q - 1)
                pe.wait_ge(lo_made, 2 * q + (2 * UA + 2))
                for t in range(QUAD):
                    cols = slice(t * P, (t + 1) * P)
                    dst = y_bank[ring][:, cols]
                    for c in range(HC):
                        at = 2 * HID + c * P
                        w_h, w_l = weights(w_hi, q, t, at), weights(w_lo, q, t, at)
                        hi, lo = hsp[:, 0, ring, c, cols], hsp[:, 1, ring, c, cols]
                        nc.tensor.matmul(dst, hi, w_h, start=c == 0, stop=False)
                        nc.tensor.matmul(dst, hi, w_l, start=False, stop=False)
                        mm = nc.tensor.matmul(dst, lo, w_h, start=False, stop=c == HC - 1)
                    if t == 0 and ahead % QUADS:
                        load_experts(ahead)
                mm.then_inc(y_done, 1)

            def routing(u):
                if u == 0:
                    gates_T(0)
                if u == 2:
                    gates_T(1)
                if u == 3:
                    biases(0)
                if u == UA + 1:
                    xhat_T(2, 2)
                    project(3)
                if u == UA + 2:
                    logits(2)
                if u == UA + 3:
                    xhat_T(2, 3)
                if u == UA + 4:
                    logits(3)
                if u == UA + 5:
                    prefix(1)
                if u == UA + 7:
                    biases(1)
                    gates_T(2)
                    gates_T(3)

            for u, (e, b) in enumerate(SHARED_A):
                routing(u)
                up_shared(u, e, b)
                if u >= 1:
                    down_shared(u - 1, *SHARED_A[u - 1], y_add, u - 2)
            down_shared(UA - 1, *SHARED_A[UA - 1], y_add, UA - 2)
            routing(UA)
            quad_T(0, 0)
            load_experts(0)
            for q in range(ALLQ):
                if q >= 1:
                    routing(UA + q)
                if q % QUADS == 0 and q:
                    load_experts(q)
                up_quad(q)
                if q + 1 < ALLQ:
                    quad_T(q + 1, (q + 1) % 2)
                if q >= 1:
                    down_quad(q - 1, q + 1)
                elif q + 1 < ALLQ:
                    load_experts(q + 1)
            for i, (e, b) in enumerate(SHARED_B):
                u = UA + ALLQ + i
                up_shared(u, e, b)
                if i == 0:
                    down_quad(ALLQ - 1, ALLQ)
                elif i <= 2:
                    down_shared(u - 1, *SHARED_B[i - 1], y_out, ALLQ - 2 + i)
                else:
                    down_shared(u - 1, *SHARED_B[i - 1], y_add, UA + i - 2)
            down_shared(UA + ALLQ + 3, *SHARED_B[3], y_add, UA + 2)


def kernel(x, ctx_1024, g_xattn, g_ffn, L0_xattn_fm_w, L0_xattn_fm_b, L0_xattn_fc_w, L0_xattn_fc_b,
           L0_ffn_Wg, L0_ffn_W1, L0_ffn_b1, L0_ffn_W11, L0_ffn_b11, L0_ffn_W2, L0_ffn_b2,
           L0_ffn_Ws1, L0_ffn_bs1, L0_ffn_Ws11, L0_ffn_bs11, L0_ffn_Ws2, L0_ffn_bs2):
    import numpy as np
    import concourse.bacc as bacc
    from concourse.bass_utils import run_bass_kernel_spmd

    f = lambda a: np.asarray(a)
    xin = np.ascontiguousarray(f(x).reshape(NB, NT, P, D).transpose(0, 2, 1, 3))

    const = np.zeros((P, C_END), np.float32)
    const[:, C_FM:C_FM + HD] = np.tile(f(L0_xattn_fm_w).T, (H, 1))
    rows = np.arange(P)
    const[:, C_MASK:C_MASK + H] = rows[:, None] // HD == np.arange(H)[None, :]
    const[:, C_SGN] = np.where(rows % FD < HD, 1.0, -1.0)
    const[:, C_FMB] = np.tile(f(L0_xattn_fm_b), P // HD)
    const[:, C_FMBV:C_FMBV + HD] = f(L0_xattn_fm_b)[None, :]
    const[:, C_WG:C_WG + E_ROUTED] = f(L0_ffn_Wg)
    const[:, C_GX] = f(g_xattn)
    const[:, C_GF] = f(g_ffn)
    const[:, C_IOTA:C_IOTA + 32] = np.arange(32)[None, :]
    const[:, C_B1:C_B11] = f(L0_ffn_bs1).reshape(2 * HC, P).T
    const[:, C_B11:C_PART] = f(L0_ffn_bs11).reshape(2 * HC, P).T
    const[:, C_PART] = rows
    const[:, C_ID:C_END] = np.eye(P)

    tri = np.triu(np.ones((P, P), np.float32), 1)
    brows = np.zeros((E_ROUTED + 1, 2 * HID + D), np.float32)
    brows[0:E_ROUTED] = np.concatenate([f(L0_ffn_b1), f(L0_ffn_b11), f(L0_ffn_b2)], axis=1)
    brows[E_ROUTED, 2 * HID:] = f(L0_ffn_bs2)

    fcw = np.zeros((P, NG + 1, D), np.float32)
    w = f(L0_xattn_fc_w).T.reshape(NG, GH, FD, D)
    for j in range(GH):
        fcw[2 * FD * j:2 * FD * j + FD, 0:NG] = w[:, j].transpose(1, 0, 2)
    fcw[0, NG] = f(L0_xattn_fc_b)

    def ups(shared, routed):
        return np.concatenate([f(shared).reshape(D, 2, HID).transpose(1, 0, 2), f(routed)])

    downs = np.concatenate([f(L0_ffn_Ws2).reshape(2, HID, D), f(L0_ffn_W2)])
    downs = downs.reshape(E, HC, P, D).transpose(0, 2, 1, 3).reshape(E, P, HC * D)
    wall = np.concatenate([ups(L0_ffn_Ws1, L0_ffn_W1), ups(L0_ffn_Ws11, L0_ffn_W11), downs], axis=2)

    arrays = {"x": xin, "ctx": f(ctx_1024), "const": const, "tri": tri, "brows": brows, "fcw": fcw, "wall": wall}
    nc = bacc.Bacc("TRN2", target_bir_lowering=False, num_devices=1)
    args = [nc.dram_tensor(f"in_{k}", a.shape, F32, kind="ExternalInput").ap() for k, a in arrays.items()]
    out = nc.dram_tensor("out", (NB, P, NT, D), F32, kind="ExternalOutput").ap()
    build(nc, *args, out)
    r = run_bass_kernel_spmd(nc, [{f"in_{k}": np.ascontiguousarray(a) for k, a in arrays.items()}], core_ids=[0])
    y = r.results[0]["out"]
    return y.transpose(0, 2, 1, 3).reshape(NB, T, D)
```
